# Optimizing a Trainium2 kernel written in Bass

```python
import numpy as np
import jax
import jax.numpy as jnp

def _softmax(x, axis=-1):
    return jax.nn.softmax(x, axis=axis)

def _gelu(x):
    return jax.nn.gelu(x, approximate=True)

def _silu(x):
    return jax.nn.silu(x)

def _sigmoid(x):
    return jax.nn.sigmoid(x)

def _layernorm(x, axis=-1, eps=1e-05):
    m = jnp.mean(x, axis=axis, keepdims=True)
    v = jnp.var(x, axis=axis, keepdims=True)
    return (x - m) / jnp.sqrt(v + eps)

def _scatter_add(tgt, idx, src, axis=0):
    return tgt.at[idx].add(src)

def _segment_sum(src, seg, n):
    return jax.ops.segment_sum(src, seg, n)
kernel_name = 'mk_gnn_resnorm_d1_gnn_r8_6eca3b'

def setup_inputs(seed: int=0):
    np.random.seed(seed)
    _w = jnp.asarray

    def _rec_inputs():
        import jax
        import jax.numpy as jnp
        _gk = jax.random.key(seed)
        x = -0.0009044 + 1 * jax.random.normal(jax.random.fold_in(_gk, 1), (6250, 160), jnp.float32)
        src = jax.random.randint(jax.random.fold_in(_gk, 2), (100000,), 0, 6250, jnp.int32)
        dst = jnp.minimum((6250 * jax.random.uniform(jax.random.fold_in(_gk, 3), (100000,)) ** 2.0).astype(jnp.int32), 49999)
        _o = jnp.argsort(dst, stable=True)
        src = src[_o]
        dst = dst[_o]
        edge_attr_3 = 0.00262751 + 0.999568 * jax.random.normal(jax.random.fold_in(_gk, 12), (100000, 3), jnp.float32)
        edge_attr_64 = jax.random.uniform(jax.random.fold_in(_gk, 13), (100000, 64), jnp.float32, 0.0, 1)
        node_vec1 = jax.random.uniform(jax.random.fold_in(_gk, 14), (6250, 1), jnp.float32, 0.0, 1)
        return (x, src, dst, edge_attr_3, edge_attr_64, node_vec1)
    x, src, dst, edge_attr_3, edge_attr_64, node_vec1 = _rec_inputs()

    def _L0_gnn_setup():
        import jax, jax.numpy as jnp
        import numpy as np
        N, E = (1250, 20000)
        C0, C1 = (64, 32)
        H, A = (8, 8)
        H0, H1 = (8, 4)
        M0, M1 = (128, 64)
        NG, RH = (64, 64)
        WN = C0 + C0 + C1 + C1 + C1
        DS, DV = (C0 + C1, C0 + 2 * C1)
        EPS = 1e-05
        SQ3 = np.float32(np.sqrt(3.0))
        SQ2 = np.float32(np.sqrt(2.0))

        def _split(x):
            return (x[:, :C0], x[:, C0:].reshape(x.shape[0], C1, 3))

        def _merge(s, v):
            return jnp.concatenate([s, v.reshape(v.shape[0], -1)], axis=1)

        def _eq_ln(x, w0, b0, w1):
            s, v = _split(x)
            s = s - s.mean(axis=1, keepdims=True)
            s = s * jax.lax.rsqrt(jnp.square(s).mean(axis=1, keepdims=True) + EPS) * w0 + b0
            v = v * jax.lax.rsqrt(jnp.square(v).mean(axis=(1, 2), keepdims=True) + EPS) * w1[None, :, None]
            return (s, v)

        def _eq_lin(s, v, ws, bs, wv):
            return (s @ ws + bs, jnp.einsum('nud,uk->nkd', v, wv))

        def _ln(x, g, b):
            xc = x - x.mean(-1, keepdims=True)
            return xc * jax.lax.rsqrt(jnp.square(xc).mean(-1, keepdims=True) + EPS) * g + b

        def _smooth_leaky(x, alpha=0.2):
            return 0.5 * (1 + alpha) * x + 0.5 * (1 - alpha) * x * (2.0 * jax.nn.sigmoid(x) - 1.0)

        def _forward(node_input, node_attr, edge_vec, edge_scalars, edge_src, edge_dst, ln1_w0, ln1_b0, ln1_w1, ln2_w0, ln2_b0, ln2_w1, msrc_ws, msrc_wv, mdst_ws, mdst_bs, mdst_wv, rw1, rb1, rg1, rbe1, rw2, rb2, rg2, rbe2, rw3, roff, lin_ws, lin_bs, lin_wv, alpha_dot, proj_ws, proj_bs, proj_wv, f1_ws, f1_bs, f1_wv, f2_ws, f2_bs, f2_wv):
            n = node_input.shape[0]
            s, v = _eq_ln(node_input, ln1_w0, ln1_b0, ln1_w1)
            src_s = s @ msrc_ws
            src_v = jnp.einsum('nud,uk->nkd', v, msrc_wv)
            dst_s = s @ mdst_ws + mdst_bs
            dst_v = jnp.einsum('nud,uk->nkd', v, mdst_wv)
            ms = src_s[edge_src] + dst_s[edge_dst]
            mv = src_v[edge_src] + dst_v[edge_dst]
            h = jax.nn.silu(_ln(edge_scalars @ rw1 + rb1, rg1, rbe1))
            h = jax.nn.silu(_ln(h @ rw2 + rb2, rg2, rbe2))
            w = h @ rw3 + roff
            rhat = edge_vec * jax.lax.rsqrt(jnp.sum(jnp.square(edge_vec), -1, keepdims=True) + 1e-12)
            Y1 = SQ3 * rhat
            w1, w2, w3, w4, w5 = jnp.split(w, [C0, 2 * C0, 2 * C0 + C1, 2 * C0 + 2 * C1], axis=1)
            o0a = w1 * ms
            o0b = w4 * (jnp.einsum('eud,ed->eu', mv, Y1) / SQ3)
            o1a = (w2 * ms)[:, :, None] * Y1[:, None, :]
            o1b = w3[:, :, None] * mv
            o1c = w5[:, :, None] * (jnp.cross(mv, Y1[:, None, :]) / SQ2)
            ds = jnp.concatenate([o0a, o0b], axis=1)
            dv = jnp.concatenate([o1a, o1b, o1c], axis=1)
            ls, lv = _eq_lin(ds, dv, lin_ws, lin_bs, lin_wv)
            e = ls.shape[0]
            alpha = ls[:, :H * A].reshape(e, H, A)
            vs = ls[:, H * A:].reshape(e, H, H0)
            vv = lv.reshape(e, H, H1, 3)
            a = jnp.einsum('ehk,hk->eh', _smooth_leaky(alpha), alpha_dot)
            amax = jax.lax.stop_gradient(jax.ops.segment_max(a, edge_dst, num_segments=n))
            a = jnp.exp(a - amax[edge_dst])
            a = a / (jax.ops.segment_sum(a, edge_dst, num_segments=n)[edge_dst] + 1e-12)
            ns = jax.ops.segment_sum(vs * a[..., None], edge_dst, num_segments=n).reshape(n, H * H0)
            nv = jax.ops.segment_sum(vv * a[..., None, None], edge_dst, num_segments=n).reshape(n, H * H1, 3)
            ps, pv = _eq_lin(ns, nv, proj_ws, proj_bs, proj_wv)
            x = node_input + _merge(ps, pv)
            s2, v2 = _eq_ln(x, ln2_w0, ln2_b0, ln2_w1)
            a0 = node_attr[:, :1]
            fs, fv = _eq_lin(s2, v2, f1_ws, f1_bs, f1_wv)
            fs = fs * a0
            fv = fv * a0[:, :, None]
            sc = jax.nn.silu(fs[:, :M0])
            fv = fv * jax.nn.sigmoid(fs[:, M0:])[:, :, None]
            os_, ov = _eq_lin(sc, fv, f2_ws, f2_bs, f2_wv)
            os_ = os_ * a0
            ov = ov * a0[:, :, None]
            return x + _merge(os_, ov)
        key = jax.random.key(seed)
        ks = iter(jax.random.split(key, 24))

        def nrm(shape, fan):
            return jax.random.normal(next(ks), shape, jnp.float32) / np.float32(np.sqrt(fan))
        inp = {}
        inp['node_input'] = jax.random.normal(next(ks), (N, C0 + 3 * C1), jnp.float32)
        inp['node_attr'] = jnp.ones((N, 1), jnp.float32)
        inp['edge_vec'] = jax.random.normal(next(ks), (E, 3), jnp.float32)
        inp['edge_scalars'] = jax.random.uniform(next(ks), (E, NG), dtype=jnp.float32)
        inp['edge_src'] = jax.random.randint(next(ks), (E,), 0, N)
        inp['edge_dst'] = jax.random.randint(next(ks), (E,), 0, N)
        inp['ln1_w0'] = jnp.ones((C0,), jnp.float32)
        inp['ln1_b0'] = jnp.zeros((C0,), jnp.float32)
        inp['ln1_w1'] = jnp.ones((C1,), jnp.float32)
        inp['ln2_w0'] = jnp.ones((C0,), jnp.float32)
        inp['ln2_b0'] = jnp.zeros((C0,), jnp.float32)
        inp['ln2_w1'] = jnp.ones((C1,), jnp.float32)
        inp['msrc_ws'] = nrm((C0, C0), C0)
        inp['msrc_wv'] = nrm((C1, C1), C1)
        inp['mdst_ws'] = nrm((C0, C0), C0)
        inp['mdst_bs'] = jnp.zeros((C0,), jnp.float32)
        inp['mdst_wv'] = nrm((C1, C1), C1)
        inp['rw1'] = nrm((NG, RH), NG)
        inp['rb1'] = jnp.zeros((RH,), jnp.float32)
        inp['rg1'] = jnp.ones((RH,), jnp.float32)
        inp['rbe1'] = jnp.zeros((RH,), jnp.float32)
        inp['rw2'] = nrm((RH, RH), RH)
        inp['rb2'] = jnp.zeros((RH,), jnp.float32)
        inp['rg2'] = jnp.ones((RH,), jnp.float32)
        inp['rbe2'] = jnp.zeros((RH,), jnp.float32)
        inp['rw3'] = nrm((RH, WN), RH)
        inp['roff'] = 0.1 * jax.random.normal(next(ks), (WN,), jnp.float32)
        inp['lin_ws'] = nrm((DS, H * A + H * H0), DS)
        inp['lin_bs'] = jnp.zeros((H * A + H * H0,), jnp.float32)
        inp['lin_wv'] = nrm((DV, H * H1), DV)
        inp['alpha_dot'] = nrm((H, A), A)
        inp['proj_ws'] = nrm((H * H0, C0), H * H0)
        inp['proj_bs'] = jnp.zeros((C0,), jnp.float32)
        inp['proj_wv'] = nrm((H * H1, C1), H * H1)
        inp['f1_ws'] = nrm((C0, M0 + M1), C0)
        inp['f1_bs'] = jnp.zeros((M0 + M1,), jnp.float32)
        inp['f1_wv'] = nrm((C1, M1), C1)
        inp['f2_ws'] = nrm((M0, C0), M0)
        inp['f2_bs'] = jnp.zeros((C0,), jnp.float32)
        inp['f2_wv'] = nrm((M1, C1), M1)
        return inp
    _L0_gnn_all = _L0_gnn_setup()
    _L0_gnn_in = {k: v for k, v in _L0_gnn_all.items() if k in ('ln1_w0', 'ln1_b0', 'ln1_w1', 'ln2_w0', 'ln2_b0', 'ln2_w1', 'msrc_ws', 'msrc_wv', 'mdst_ws', 'mdst_bs', 'mdst_wv', 'rw1', 'rb1', 'rg1', 'rbe1', 'rw2', 'rb2', 'rg2', 'rbe2', 'rw3', 'roff', 'lin_ws', 'lin_bs', 'lin_wv', 'alpha_dot', 'proj_ws', 'proj_bs', 'proj_wv', 'f1_ws', 'f1_bs', 'f1_wv', 'f2_ws', 'f2_bs', 'f2_wv')}
    del _L0_gnn_all
    return {'x': x, 'src': src, 'dst': dst, 'edge_attr_3': edge_attr_3, 'edge_attr_64': edge_attr_64, 'node_vec1': node_vec1, 'L0_gnn_ln1_w0': _L0_gnn_in['ln1_w0'], 'L0_gnn_ln1_b0': _L0_gnn_in['ln1_b0'], 'L0_gnn_ln1_w1': _L0_gnn_in['ln1_w1'], 'L0_gnn_ln2_w0': _L0_gnn_in['ln2_w0'], 'L0_gnn_ln2_b0': _L0_gnn_in['ln2_b0'], 'L0_gnn_ln2_w1': _L0_gnn_in['ln2_w1'], 'L0_gnn_msrc_ws': _L0_gnn_in['msrc_ws'], 'L0_gnn_msrc_wv': _L0_gnn_in['msrc_wv'], 'L0_gnn_mdst_ws': _L0_gnn_in['mdst_ws'], 'L0_gnn_mdst_bs': _L0_gnn_in['mdst_bs'], 'L0_gnn_mdst_wv': _L0_gnn_in['mdst_wv'], 'L0_gnn_rw1': _L0_gnn_in['rw1'], 'L0_gnn_rb1': _L0_gnn_in['rb1'], 'L0_gnn_rg1': _L0_gnn_in['rg1'], 'L0_gnn_rbe1': _L0_gnn_in['rbe1'], 'L0_gnn_rw2': _L0_gnn_in['rw2'], 'L0_gnn_rb2': _L0_gnn_in['rb2'], 'L0_gnn_rg2': _L0_gnn_in['rg2'], 'L0_gnn_rbe2': _L0_gnn_in['rbe2'], 'L0_gnn_rw3': _L0_gnn_in['rw3'], 'L0_gnn_roff': _L0_gnn_in['roff'], 'L0_gnn_lin_ws': _L0_gnn_in['lin_ws'], 'L0_gnn_lin_bs': _L0_gnn_in['lin_bs'], 'L0_gnn_lin_wv': _L0_gnn_in['lin_wv'], 'L0_gnn_alpha_dot': _L0_gnn_in['alpha_dot'], 'L0_gnn_proj_ws': _L0_gnn_in['proj_ws'], 'L0_gnn_proj_bs': _L0_gnn_in['proj_bs'], 'L0_gnn_proj_wv': _L0_gnn_in['proj_wv'], 'L0_gnn_f1_ws': _L0_gnn_in['f1_ws'], 'L0_gnn_f1_bs': _L0_gnn_in['f1_bs'], 'L0_gnn_f1_wv': _L0_gnn_in['f1_wv'], 'L0_gnn_f2_ws': _L0_gnn_in['f2_ws'], 'L0_gnn_f2_bs': _L0_gnn_in['f2_bs'], 'L0_gnn_f2_wv': _L0_gnn_in['f2_wv']}

def reference(x, src, dst, edge_attr_3, edge_attr_64, node_vec1, L0_gnn_ln1_w0, L0_gnn_ln1_b0, L0_gnn_ln1_w1, L0_gnn_ln2_w0, L0_gnn_ln2_b0, L0_gnn_ln2_w1, L0_gnn_msrc_ws, L0_gnn_msrc_wv, L0_gnn_mdst_ws, L0_gnn_mdst_bs, L0_gnn_mdst_wv, L0_gnn_rw1, L0_gnn_rb1, L0_gnn_rg1, L0_gnn_rbe1, L0_gnn_rw2, L0_gnn_rb2, L0_gnn_rg2, L0_gnn_rbe2, L0_gnn_rw3, L0_gnn_roff, L0_gnn_lin_ws, L0_gnn_lin_bs, L0_gnn_lin_wv, L0_gnn_alpha_dot, L0_gnn_proj_ws, L0_gnn_proj_bs, L0_gnn_proj_wv, L0_gnn_f1_ws, L0_gnn_f1_bs, L0_gnn_f1_wv, L0_gnn_f2_ws, L0_gnn_f2_bs, L0_gnn_f2_wv):
    import jax
    import jax.numpy as jnp

    def _L0_gnn_ref(node_input, node_attr, edge_vec, edge_scalars, edge_src, edge_dst, ln1_w0, ln1_b0, ln1_w1, ln2_w0, ln2_b0, ln2_w1, msrc_ws, msrc_wv, mdst_ws, mdst_bs, mdst_wv, rw1, rb1, rg1, rbe1, rw2, rb2, rg2, rbe2, rw3, roff, lin_ws, lin_bs, lin_wv, alpha_dot, proj_ws, proj_bs, proj_wv, f1_ws, f1_bs, f1_wv, f2_ws, f2_bs, f2_wv):
        import jax, jax.numpy as jnp
        import numpy as np
        N, E = (1250, 20000)
        C0, C1 = (64, 32)
        H, A = (8, 8)
        H0, H1 = (8, 4)
        M0, M1 = (128, 64)
        NG, RH = (64, 64)
        WN = C0 + C0 + C1 + C1 + C1
        DS, DV = (C0 + C1, C0 + 2 * C1)
        EPS = 1e-05
        SQ3 = np.float32(np.sqrt(3.0))
        SQ2 = np.float32(np.sqrt(2.0))

        def _split(x):
            return (x[:, :C0], x[:, C0:].reshape(x.shape[0], C1, 3))

        def _merge(s, v):
            return jnp.concatenate([s, v.reshape(v.shape[0], -1)], axis=1)

        def _eq_ln(x, w0, b0, w1):
            s, v = _split(x)
            s = s - s.mean(axis=1, keepdims=True)
            s = s * jax.lax.rsqrt(jnp.square(s).mean(axis=1, keepdims=True) + EPS) * w0 + b0
            v = v * jax.lax.rsqrt(jnp.square(v).mean(axis=(1, 2), keepdims=True) + EPS) * w1[None, :, None]
            return (s, v)

        def _eq_lin(s, v, ws, bs, wv):
            return (s @ ws + bs, jnp.einsum('nud,uk->nkd', v, wv))

        def _ln(x, g, b):
            xc = x - x.mean(-1, keepdims=True)
            return xc * jax.lax.rsqrt(jnp.square(xc).mean(-1, keepdims=True) + EPS) * g + b

        def _smooth_leaky(x, alpha=0.2):
            return 0.5 * (1 + alpha) * x + 0.5 * (1 - alpha) * x * (2.0 * jax.nn.sigmoid(x) - 1.0)

        def _forward(node_input, node_attr, edge_vec, edge_scalars, edge_src, edge_dst, ln1_w0, ln1_b0, ln1_w1, ln2_w0, ln2_b0, ln2_w1, msrc_ws, msrc_wv, mdst_ws, mdst_bs, mdst_wv, rw1, rb1, rg1, rbe1, rw2, rb2, rg2, rbe2, rw3, roff, lin_ws, lin_bs, lin_wv, alpha_dot, proj_ws, proj_bs, proj_wv, f1_ws, f1_bs, f1_wv, f2_ws, f2_bs, f2_wv):
            n = node_input.shape[0]
            s, v = _eq_ln(node_input, ln1_w0, ln1_b0, ln1_w1)
            src_s = s @ msrc_ws
            src_v = jnp.einsum('nud,uk->nkd', v, msrc_wv)
            dst_s = s @ mdst_ws + mdst_bs
            dst_v = jnp.einsum('nud,uk->nkd', v, mdst_wv)
            ms = src_s[edge_src] + dst_s[edge_dst]
            mv = src_v[edge_src] + dst_v[edge_dst]
            h = jax.nn.silu(_ln(edge_scalars @ rw1 + rb1, rg1, rbe1))
            h = jax.nn.silu(_ln(h @ rw2 + rb2, rg2, rbe2))
            w = h @ rw3 + roff
            rhat = edge_vec * jax.lax.rsqrt(jnp.sum(jnp.square(edge_vec), -1, keepdims=True) + 1e-12)
            Y1 = SQ3 * rhat
            w1, w2, w3, w4, w5 = jnp.split(w, [C0, 2 * C0, 2 * C0 + C1, 2 * C0 + 2 * C1], axis=1)
            o0a = w1 * ms
            o0b = w4 * (jnp.einsum('eud,ed->eu', mv, Y1) / SQ3)
            o1a = (w2 * ms)[:, :, None] * Y1[:, None, :]
            o1b = w3[:, :, None] * mv
            o1c = w5[:, :, None] * (jnp.cross(mv, Y1[:, None, :]) / SQ2)
            ds = jnp.concatenate([o0a, o0b], axis=1)
            dv = jnp.concatenate([o1a, o1b, o1c], axis=1)
            ls, lv = _eq_lin(ds, dv, lin_ws, lin_bs, lin_wv)
            e = ls.shape[0]
            alpha = ls[:, :H * A].reshape(e, H, A)
            vs = ls[:, H * A:].reshape(e, H, H0)
            vv = lv.reshape(e, H, H1, 3)
            a = jnp.einsum('ehk,hk->eh', _smooth_leaky(alpha), alpha_dot)
            amax = jax.lax.stop_gradient(jax.ops.segment_max(a, edge_dst, num_segments=n))
            a = jnp.exp(a - amax[edge_dst])
            a = a / (jax.ops.segment_sum(a, edge_dst, num_segments=n)[edge_dst] + 1e-12)
            ns = jax.ops.segment_sum(vs * a[..., None], edge_dst, num_segments=n).reshape(n, H * H0)
            nv = jax.ops.segment_sum(vv * a[..., None, None], edge_dst, num_segments=n).reshape(n, H * H1, 3)
            ps, pv = _eq_lin(ns, nv, proj_ws, proj_bs, proj_wv)
            x = node_input + _merge(ps, pv)
            s2, v2 = _eq_ln(x, ln2_w0, ln2_b0, ln2_w1)
            a0 = node_attr[:, :1]
            fs, fv = _eq_lin(s2, v2, f1_ws, f1_bs, f1_wv)
            fs = fs * a0
            fv = fv * a0[:, :, None]
            sc = jax.nn.silu(fs[:, :M0])
            fv = fv * jax.nn.sigmoid(fs[:, M0:])[:, :, None]
            os_, ov = _eq_lin(sc, fv, f2_ws, f2_bs, f2_wv)
            os_ = os_ * a0
            ov = ov * a0[:, :, None]
            return x + _merge(os_, ov)
        return _forward(node_input, node_attr, edge_vec, edge_scalars, edge_src, edge_dst, ln1_w0, ln1_b0, ln1_w1, ln2_w0, ln2_b0, ln2_w1, msrc_ws, msrc_wv, mdst_ws, mdst_bs, mdst_wv, rw1, rb1, rg1, rbe1, rw2, rb2, rg2, rbe2, rw3, roff, lin_ws, lin_bs, lin_wv, alpha_dot, proj_ws, proj_bs, proj_wv, f1_ws, f1_bs, f1_wv, f2_ws, f2_bs, f2_wv)
    x = _layernorm(x + _L0_gnn_ref(x, node_vec1, edge_attr_3, edge_attr_64, src, dst, L0_gnn_ln1_w0, L0_gnn_ln1_b0, L0_gnn_ln1_w1, L0_gnn_ln2_w0, L0_gnn_ln2_b0, L0_gnn_ln2_w1, L0_gnn_msrc_ws, L0_gnn_msrc_wv, L0_gnn_mdst_ws, L0_gnn_mdst_bs, L0_gnn_mdst_wv, L0_gnn_rw1, L0_gnn_rb1, L0_gnn_rg1, L0_gnn_rbe1, L0_gnn_rw2, L0_gnn_rb2, L0_gnn_rg2, L0_gnn_rbe2, L0_gnn_rw3, L0_gnn_roff, L0_gnn_lin_ws, L0_gnn_lin_bs, L0_gnn_lin_wv, L0_gnn_alpha_dot, L0_gnn_proj_ws, L0_gnn_proj_bs, L0_gnn_proj_wv, L0_gnn_f1_ws, L0_gnn_f1_bs, L0_gnn_f1_wv, L0_gnn_f2_ws, L0_gnn_f2_bs, L0_gnn_f2_wv), axis=-1)
    return x

_drawn_inputs = setup_inputs


def setup_inputs(seed=0):
    import zlib

    import numpy as np

    out = dict(_drawn_inputs(seed))
    spreads = {'L0_gnn_ln1_w0': (1.0, 0.2),
     'L0_gnn_ln1_b0': (0.0, 0.39),
     'L0_gnn_ln1_w1': (1.0, 0.6),
     'L0_gnn_ln2_w0': (1.0, 0.6),
     'L0_gnn_ln2_b0': (0.0, 0.8),
     'L0_gnn_ln2_w1': (1.0, 0.6),
     'L0_gnn_mdst_bs': (0.0, 0.541),
     'L0_gnn_rb1': (0.0, 0.1),
     'L0_gnn_rg1': (1.0, 0.2),
     'L0_gnn_rbe1': (0.0, 0.288),
     'L0_gnn_rb2': (0.0, 0.1),
     'L0_gnn_rg2': (1.0, 0.2),
     'L0_gnn_rbe2': (0.0, 0.301),
     'L0_gnn_lin_bs': (0.0, 0.281),
     'L0_gnn_proj_bs': (0.0, 0.1),
     'L0_gnn_f1_bs': (0.0, 0.8),
     'L0_gnn_f2_bs': (0.0, 0.517)}
    factors = {}
    for name, (base, spread) in spreads.items():
        noise = np.random.default_rng([zlib.crc32(name.encode()), seed]).standard_normal(out[name].shape)
        drawn = base * np.exp(spread * noise) if base else spread * noise
        out[name] = jnp.asarray(drawn.astype(out[name].dtype))
    for name, factor in factors.items():
        out[name] = (out[name] * factor).astype(out[name].dtype)
    return out
```

```python
import concourse.bass as bass
from concourse import mybir
from contextlib import ExitStack

F32 = mybir.dt.float32
BF16 = mybir.dt.bfloat16
I32 = mybir.dt.int32
ALU = mybir.AluOpType
ACT = mybir.ActivationFunctionType
AX = mybir.AxisListType

N, E = 6250, 100000
C0, C1 = 64, 32
CV = 3 * C1
C = C0 + CV
H = 8
M0, M1 = 128, 64
P = 125
G = 8
TILES = E // P
GROUPS = TILES // G
NT = 5
NODE_TILES = N // P
NODE_GROUPS = NODE_TILES // NT
ROW = 180
SUMS = H + C
R_MAX, R_DST = SUMS, SUMS + H
BIG = 1e30
EPS = 1e-5
SQ3 = 3.0 ** 0.5
SQ2 = 2.0 ** 0.5

B_NODE, B_MLP1, B_MLP2, B_W, B_LIN, B_PROJ, B_F1, B_F2, B_END = 0, 320, 832, 1344, 1792, 2208, 2368, 2560, 2720
W_TILE = 224
PROD = 352
LIN = 416
MSG = LIN - 64
PAY = SUMS + 3 * CV

RDIR = 7
LAG_T, LAG_LIN, LAG_ATT, LAG_PAY, LAG_SUM = 2, 3, 4, 16, 17
W_ORDER = ((0, 0, 64), (64, 160, 192), (96, 64, 128), (160, 128, 160), (192, 192, 224))
PIECES = 16 * 2 * NT
LOADS, WEIGHT_STEPS, SEARCH_STEPS, NORM_STEPS, LAST_STEPS = 109, 31, 12, 9, 25
CARRY_ROWS = 2 + 8
PEEL, LOOP_END, STEPS = 6, GROUPS - 2, GROUPS + 4


def spread(ap, axis, n):
    ap = ap.unsqueeze(axis)
    shape = list(ap.shape)
    shape[axis] = n
    return ap.broadcast_to(shape)


def build(nc, inp, out):
    ctx = ExitStack()
    with ctx:
        def sb(name, shape, dt=F32):
            return ctx.enter_context(nc.sbuf_tensor(name, shape, dt))

        def sem(name):
            return ctx.enter_context(nc.semaphore(name))

        src_table = nc.dram_tensor("src_table", (N, C), F32).ap()
        dst_table = nc.dram_tensor("dst_table", (N, C), F32).ap()
        runs = nc.dram_tensor("runs", (E, ROW), F32).ap()
        carry = nc.dram_tensor("carry", (TILES + 1, ROW), F32).ap()

        ident = sb("ident", [128, 128])
        ones3 = sb("ones3", [3, 128], BF16)
        bias3 = sb("bias3", [3, B_END], BF16)
        ln1 = sb("ln1", [CV, 3])
        ln2 = sb("ln2", [CV, 3])
        mlp_affine = sb("mlp_affine", [128, 8])
        w_node_s = sb("w_node_s", [C0, 128])
        w_node_v = sb("w_node_v", [CV, 192])
        w_mlp = sb("w_mlp", [128, 2, 128])
        w3 = sb("w3", [128, 2 * W_TILE])
        w_lin = sb("w_lin", [CV, 192])
        w_a = sb("w_a", [C0, C1])
        w_b = sb("w_b", [CV, CV])
        w_c = sb("w_c", [CV, CV])
        w_proj_s = sb("w_proj_s", [C0, C0])
        w_proj_v = sb("w_proj_v", [CV, CV])
        w_f1_s = sb("w_f1_s", [C0, 192])
        w_f1_v = sb("w_f1_v", [CV, 192])
        w_f2_s = sb("w_f2_s", [M0, C0])
        w_f2_v = sb("w_f2_v", [CV, 2, CV])
        minus_half = sb("minus_half", [P, 16])

        idx_all = sb("idx_all", [P, GROUPS, 2 * G], I32)
        dst_all = sb("dst_all", [P, GROUPS, G])
        rhat_all = sb("rhat_all", [P, GROUPS, G, RDIR])
        node_all = sb("node_all", [P, NODE_TILES])
        place_all = sb("place_all", [P, 2, NODE_TILES], I32)

        AREA = 34000
        area = sb("area", [128, AREA])
        top = [0]

        def part(parts, *dims, dt=F32, reset=False):
            if reset:
                top[0] = 0
            n = 1
            for d in dims:
                n *= d
            words = n if dt != BF16 else (n + 1) // 2
            ap = area[0:parts, top[0]:top[0] + words]
            top[0] += words
            assert top[0] <= AREA, top[0]
            if dt != F32:
                ap = ap.bitcast(dt)
            names = "abcd"[:len(dims)]
            if len(dims) > 1:
                ap = ap.rearrange(f"p ({' '.join(names)}) -> p {' '.join(names)}",
                                  **{m: d for m, d in zip(names[1:], dims[1:])})
            return ap

        K = TILES // 100
        nat_i = part(100, 2, K, P, dt=I32, reset=True)
        nat_f = part(100, 2, K, P)
        nat_v = part(100, K, P, 3)
        first_dst = part(P, TILES)
        vec_all = part(P, GROUPS, G, 3)
        vec_sq = part(P, TILES, 3)
        vec_n2 = part(P, TILES)
        vec_inv = part(P, TILES)
        vec_half = part(P, TILES)
        node_i = part(P, NODE_TILES, dt=I32)
        search_junk = vec_sq.rearrange("p t c -> p (t c)")[:, 0:TILES]
        search_node = part(P, NT)
        search_cnt = part(P, NT)
        search_tile = part(P, NT)
        search_tile_i = part(P, NT, dt=I32)
        search_dst = part(P, NT, P, dt=I32)
        search_le = part(P, NT, P)
        search_in = part(P, NT)
        search_row = part(P, NT)
        bias_row = part(1, B_END)
        bias_rest = part(1, B_END)
        bias_parts = part(1, 3, B_END, dt=BF16)
        bias_mean = part(1, 2, G)
        mlp_mean = part(128, 2)
        w3_raw = part(128, 2 * W_TILE)
        lin_raw = part(CV, 128)
        adot = part(CV, 64)
        linv_a = part(C0, C1)
        linv_b = part(CV, CV)
        linv_c = part(CV, CV)
        lin_b_raw = part(1, 128)
        x_in = [part(P, NT, C, reset=(q == 0)) for q in (0, 1)]
        x_sq = part(P, NT, C)
        x_norm = [part(P, NT, C) for q in (0, 1)]
        x_sum = part(P, NT)
        x_mean = part(P, NT)
        x_cen = part(P, NT, C)
        x_ss = part(P, 2, NT)
        x_var = part(P, 2, NT)
        x_rstd = part(P, 2, NT)
        table = [part(P, NT, 2 * C) for q in (0, 1)]
        tile_s = part(128, 2, P)
        tile_v = part(CV, 2, 2, P)
        a0 = [part(P, NT) for q in (0, 1)]
        node_no = [part(P, NT) for q in (0, 1)]
        place = [part(P, 2, NT, dt=I32) for q in (0, 1)]
        pieces = [part(P, 2, NT, ROW) for q in (0, 1)]
        found = part(P, 2, NT)
        absent = part(P, 2, NT)
        piece_max = part(P, 2, NT, H)
        both_max = part(P, NT, H)
        piece_d = part(P, 2, NT, H)
        piece_e = part(P, 2, NT, H)
        piece_f = part(P, 2, NT, H)
        agg_a = part(P, NT, SUMS)
        agg_b = part(P, NT, SUMS)
        agg = part(P, NT, SUMS)
        den = part(P, NT, H)
        rden = part(P, NT, H)
        x1 = part(P, NT, C)
        ff_g = part(P, 2, 384)
        ff_t = part(P, 2, 192)
        ff_s = part(P, NT, M0)
        ff_v = part(P, NT, 192)
        y_sum = part(P, NT, C)
        y_out = [part(P, NT, C) for q in (0, 1)]
        es_in = [part(P, G, 64, reset=(q == 0)) for q in (0, 1)]
        got_s = [part(P, G, C) for q in (0, 1)]
        got_d = [part(P, G, C) for q in (0, 1)]
        dst_row = [part(P, G, P, dt=I32) for q in (0, 1)]
        dst_th = [part(G * H, P, dt=I32) for q in (0, 1)]
        idx = [part(P, 2 * G, dt=I32) for q in (0, 1)]
        dst_col = [part(P, G) for q in (0, 1)]
        rhat = [part(P, G, RDIR) for q in (0, 1)]
        es_t = part(128, 4, P)
        mlp_sq = part(P, G, 64)
        mlp_ss = part(P, G)
        mlp_var = part(P, G)
        mlp_rstd = part(P, G)
        mlp_n = part(P, G, 64)
        mlp_tanh = part(128, 4, P)
        mlp_y = part(128, 4, P)
        h1_t = part(128, 4, P)
        h2_t = [part(128, 4, P) for q in (0, 1)]
        feat = part(P, 2, C + C1)
        dot_in = part(P, 2, CV)
        prod = [part(P, 2, PROD) for q in (0, 1)]
        prod_t = [part(CV, 4, P) for q in (0, 1)]
        att_tanh = [part(P, 64) for q in (0, 1)]
        att_u = [part(P, 64) for q in (0, 1)]
        msg = [part(P, G, MSG) for q in (0, 1)]
        logit = [part(P, G, H) for q in (0, 1)]
        run_ne = part(G * H, P)
        run_mask = part(G * H, P + 1)
        run_fwd = part(G * H, P)
        run_max = part(G * H, P)
        logit_d = part(P, G, H)
        prob = [part(P, G, H) for q in (0, 1)]
        prob_r = [part(P, G, RDIR, H) for q in (0, 1)]
        eq = [part(P, P) for q in (0, 1)]
        pay = [part(P, PAY) for q in (0, 1)]
        run_rows = [part(P, G, ROW) for q in (0, 1)]
        HALF = 88
        last = part(100, K, ROW, reset=True)
        last_max = part(100, K, HALF)
        chan = part(HALF, 2, TILES)
        chan_m = part(HALF, TILES)
        chan_d = part(HALF, TILES)
        same = part(HALF, TILES)
        restart = part(HALF, TILES)
        scan_m = part(HALF, TILES)
        step_m = part(HALF, TILES)
        keep = part(HALF, TILES)
        take = part(HALF, TILES)
        chan_x = part(HALF, 2, TILES)
        scan_x = part(HALF, 2, TILES)
        carry_rows = part(100, K, ROW)
        sentinel = part(1, ROW)

        ps = [ctx.enter_context(nc.psum_tensor(f"ps{i}", [128, 512], F32)) for i in range(8)]
        PM = ps[0]
        PR, PW, PT, PL, PO = ps[1], ps[2], (ps[3], ps[4]), (ps[5], ps[6]), ps[7]
        run_t = PR[0:G * H, 0:P]
        run_b = PR[0:P, 128:128 + G * H]

        x_v = inp["x"].rearrange("(g t p) c -> g p t c", t=NT, p=P)
        a0_v = inp["node_vec1"].rearrange("(g t p) c -> g p t c", t=NT, p=P)
        out_v = out.rearrange("(g t p) c -> g p t c", t=NT, p=P)
        src_v = src_table.rearrange("(g t p) c -> g p t c", t=NT, p=P)
        dst_v = dst_table.rearrange("(g t p) c -> g p t c", t=NT, p=P)
        es_v = inp["edge_attr_64"].rearrange("(g t p) c -> g p t c", t=G, p=P)
        dst_row_v = inp["dst"].rearrange("(g x e) -> g x e", x=1, e=G * P)
        dst_th_v = inp["dst"].rearrange("(g t x e) -> g t x e", t=G, x=1, e=P)
        dst_tiles = inp["dst"].rearrange("(t e) -> t e", e=P)
        runs_v = runs.rearrange("(g t p) c -> g p t c", t=G, p=P)
        last_v = runs.rearrange("(a k p) c -> p a k c", k=K, p=P)

        def W(name):
            return inp["L0_gnn_" + name]

        S = {}
        for name in (
            "zeroed", "weights_loaded", "weight_step", "bias_moved", "consts_made", "nat_loaded", "nat_cast",
            "cols_turned", "cols_kept", "vec_step", "vec_root", "search_step", "search_ready", "search_loaded",
            "x_loaded_0", "x_loaded_1", "norm_step", "x_var_ready", "x_rstd_ready", "x_norm_ready", "node_turned",
            "affine_ready", "node_projected", "table_ready", "stored_0", "stored_1",
            "es_loaded_0", "es_loaded_1", "meta_loaded_0", "meta_loaded_1", "gathered_0", "gathered_1",
            "idx_ready", "rhat_ready", "es_turned", "es_copied", "mlp_out", "mlp_squared", "mlp_ss_ready",
            "mlp_var_ready", "mlp_rstd_ready", "mlp_n_ready", "mlp_turned", "mlp_act_ready", "mlp_h_ready",
            "edge_consts", "sum_ready", "dots_in", "dots_ready", "w_ready", "prods_ready", "prods_turned",
            "prods_copied", "lin_ready", "att_tanh_ready", "msg_ready", "att_u_ready", "logits_ready",
            "cols_ready", "run_ne_ready", "mask_ready", "logits_turned", "fwd_ready", "max_ready", "max_turned",
            "max_kept", "logit_d_ready", "prob_ready", "prob_r_ready", "eq_ready", "pay_ready", "sums_ready",
            "rows_ready", "rows_stored_0", "rows_stored_1",
            "last_loaded", "last_spread", "last_turned", "last_copied", "carry_step", "carry_exp_in", "carry_exp", "carry_done",
            "carry_turned", "carry_rows_ready", "carry_stored",
            "place_ready", "pieces_loaded_0", "pieces_loaded_1", "nodes_loaded_0", "nodes_loaded_1", "last_step", "merge_in", "merge_exp", "agg_ready",
            "tile_turned", "tile_copied", "projected", "x1_ready", "f1_ready", "ff_scaled", "ff_tanh",
            "ff_ready", "f2_ready", "x2_ready", "x2_norm_ready", "y_var_ready", "y_rstd_ready", "y_ready",
            "out_stored_0", "out_stored_1", "waits_passed",
            "prologue_over", "node_pass_over", "edge_pass_over", "carry_over",
        ):
            S[name] = sem(name)

        def done(h, q, lag, n, k, back=0):
            return h * (2 * n) + ((q - lag) * n + k + 1 - back)

        def turn(h, q, lag, n=16):
            return h * n + ((q - lag) // 2 + 1) * n

        def wait(eng, name, count):
            if isinstance(count, int) and count <= 0:
                return
            eng.wait_ge(S[name], count)

        def alone(eng, name, count):
            wait(eng, name, count)
            if not isinstance(count, int):
                eng.sem_inc(S["waits_passed"])

        def steps(eng, body):
            for s in range(PEEL):
                body(s // 2, s % 2, lambda lag, s=s: 0 <= s - lag < GROUPS)
            with eng.Fori(PEEL // 2, LOOP_END // 2) as h:
                for q in (0, 1):
                    body(h, q, lambda lag: True)
            for s in range(LOOP_END, STEPS):
                body(s // 2, s % 2, lambda lag, s=s: 0 <= s - lag < GROUPS)

        def node_groups(eng, body):
            for q in (0, 1):
                body(0, q, True)
            with eng.Fori(1, NODE_GROUPS // 2 - 1) as h:
                for q in (0, 1):
                    body(h, q, True)
            for q in (0, 1):
                body(NODE_GROUPS // 2 - 1, q, q == 0)

        def behind(j, lag):
            return 1 - (j - lag) // G, (j - lag) % G

        def barrier(eng, name):
            eng.drain().then_inc(S[name], 1)
            eng.wait_ge(S[name], 5)

        def one(g):
            return bass.ds(g, 1)

        loads = [0]
        ZERO_TILES = (w_mlp[:, :, :], w3_raw, w_node_v[:, :], linv_b, linv_c, w_proj_v[:, :], w_f1_v[:, :], w_f2_v[:, :, :], bias_row)
        ZEROED = len(ZERO_TILES) + 1

        block = ctx.enter_context(nc.Block())

        @block.sync
        def _(sp):
            def load(dst, src):
                sp.dma_start(dst, src, allow_slow_non_contiguous=True).then_inc(S["weights_loaded"], 16)
                loads[0] += 1

            def row(name):
                return W(name).unsqueeze(0)

            sp.dma_start(nat_i[:, 0], inp["src"].rearrange("(a k e) -> a k e", k=K, e=P)).then_inc(S["nat_loaded"], 16)
            sp.dma_start(nat_i[:, 1], inp["dst"].rearrange("(a k e) -> a k e", k=K, e=P)).then_inc(S["nat_loaded"], 16)
            sp.dma_start(nat_v, inp["edge_attr_3"].rearrange("(a k e) c -> a k e c", k=K, e=P)).then_inc(
                S["nat_loaded"], 16)
            sp.wait_ge(S["zeroed"], ZEROED)
            for w, b, v, dst in (("ln1_w0", "ln1_b0", "ln1_w1", ln1), ("ln2_w0", "ln2_b0", "ln2_w1", ln2)):
                load(dst[0:C0, 0:1], W(w).unsqueeze(1))
                load(dst[0:C0, 1:2], W(b).unsqueeze(1))
                for d in range(3):
                    load(dst[C1 * d:C1 * (d + 1), 2:3], W(v).unsqueeze(1))
            load(w_node_s[:, 0:64], W("msrc_ws"))
            load(w_node_s[:, 64:128], W("mdst_ws"))
            for d in range(3):
                rows = slice(C1 * d, C1 * (d + 1))
                load(w_node_v[rows, C1 * d:C1 * (d + 1)], W("msrc_wv"))
                load(w_node_v[rows, CV + C1 * d:CV + C1 * (d + 1)], W("mdst_wv"))
                load(linv_b[rows, C1 * d:C1 * (d + 1)], W("lin_wv")[64:96, :])
                load(linv_c[rows, C1 * d:C1 * (d + 1)], W("lin_wv")[96:128, :])
                load(w_f1_v[rows, M1 * d:M1 * (d + 1)], W("f1_wv"))
                for k in range(4):
                    load(w_proj_v[C1 * d + 8 * k:C1 * d + 8 * k + 8, C1 * d:C1 * (d + 1)],
                         W("proj_wv").rearrange("(h k) n -> k h n", k=4)[k])
            for k in range(8):
                load(w_proj_s[8 * k:8 * k + 8, :], W("proj_ws").rearrange("(h k) n -> k h n", k=8)[k])
            for half in (0, 1):
                rows = slice(64 * half, 64 * half + 64)
                load(w_mlp[rows, 0, rows], W("rw1"))
                load(w_mlp[rows, 1, rows], W("rw2"))
                for c, v in enumerate(("rg1", "rbe1", "rg2", "rbe2")):
                    load(mlp_affine[rows, c:c + 1], W(v).unsqueeze(1))
                for at, lo, hi in W_ORDER:
                    load(w3_raw[rows, W_TILE * half + at:W_TILE * half + at + hi - lo], W("rw3")[:, lo:hi])
            load(lin_raw, W("lin_ws"))
            load(adot, W("alpha_dot").rearrange("(x h) k -> x (h k)", x=1).broadcast_to([CV, 64]))
            load(linv_a, W("lin_wv")[0:64, :])
            load(lin_b_raw, row("lin_bs"))
            load(bias_row[:, B_NODE + C:B_NODE + C + 64], row("mdst_bs"))
            for t in range(G):
                load(bias_row[:, B_MLP1 + 64 * t:B_MLP1 + 64 * t + 64], row("rb1"))
                load(bias_row[:, B_MLP2 + 64 * t:B_MLP2 + 64 * t + 64], row("rb2"))
            for t in range(2):
                for at, lo, hi in W_ORDER:
                    load(bias_row[:, B_W + W_TILE * t + at:B_W + W_TILE * t + at + hi - lo], row("roff")[:, lo:hi])
            load(bias_row[:, B_PROJ:B_PROJ + 64], row("proj_bs"))
            load(bias_row[:, B_F1:B_F1 + 192], row("f1_bs"))
            load(bias_row[:, B_F2:B_F2 + 64], row("f2_bs"))
            load(w_f1_s[:, :], W("f1_ws"))
            load(w_f2_s[:, :], W("f2_ws"))
            load(w_f2_v[0:64, 0, 0:32], W("f2_wv"))
            load(w_f2_v[64:96, 0, 32:64], W("f2_wv")[0:32, :])
            load(w_f2_v[0:32, 1, 32:64], W("f2_wv")[32:64, :])
            load(w_f2_v[32:96, 1, 64:96], W("f2_wv"))
            assert loads[0] == LOADS, loads[0]
            sp.wait_ge(S["weight_step"], WEIGHT_STEPS)
            for k in range(3):
                sp.dma_start(bias3[k:k + 1, :], bias_parts[0:1, k, :]).then_inc(S["bias_moved"], 16)
            sp.wait_ge(S["bias_moved"], 48)
            barrier(sp, "prologue_over")

            sp.dma_start(x_in[0], x_v[0]).then_inc(S["x_loaded_0"], 16)

            def node_step(h, q, more):
                if more:
                    alone(sp, "x_norm_ready", done(h, q, 1, 1, 0))
                    sp.dma_start(x_in[1 - q], x_v[h * 2 + (q + 1)]).then_inc(S[f"x_loaded_{1 - q}"], 16)
                alone(sp, "table_ready", done(h, q, 0, NT, NT - 1))
                sp.dma_start(src_v[h * 2 + q], table[q][:, :, 0:C]).then_inc(S[f"stored_{q}"], 16)
                sp.dma_start(dst_v[h * 2 + q], table[q][:, :, C:2 * C]).then_inc(S[f"stored_{q}"], 16)

            node_groups(sp, node_step)
            for q in (0, 1):
                sp.wait_ge(S[f"stored_{q}"], 32 * (NODE_GROUPS // 2))
            barrier(sp, "node_pass_over")

            sp.dma_start(es_in[0], es_v[0]).then_inc(S["es_loaded_0"], 16)

            def step(h, q, live):
                if live(-1):
                    alone(sp, "es_turned", done(h, q, 1, 1, 0))
                    sp.dma_start(es_in[1 - q], es_v[h * 2 + (q + 1)]).then_inc(S[f"es_loaded_{1 - q}"], 16)
                if live(4):
                    alone(sp, "rows_ready", done(h, q, 4, G // 2, G // 2 - 1))
                    alone(sp, "max_kept", done(h, q, 4, 2, 1))
                    sp.dma_start(runs_v[h * 2 + (q - 4)], run_rows[q]).then_inc(S[f"rows_stored_{q}"], 16)
                if live(1):
                    alone(sp, "run_ne_ready", done(h, q, 3, 1, 0))
                    alone(sp, "eq_ready", done(h, q, 3, G, G - 1))
                    sp.dma_start(dst_row[1 - q], dst_row_v[h * 2 + (q - 1)].broadcast_to([P, G * P])
                                 .rearrange("p (t e) -> p t e", t=G)).then_inc(S[f"meta_loaded_{1 - q}"], 16)
                    sp.dma_start(dst_th[1 - q], dst_th_v[h * 2 + (q - 1)].broadcast_to([G, H, P])).then_inc(
                        S[f"meta_loaded_{1 - q}"], 16)

            steps(sp, step)
            for q in (0, 1):
                sp.wait_ge(S[f"rows_stored_{q}"], 16 * (GROUPS // 2))
            barrier(sp, "edge_pass_over")

            sp.dma_start(last, last_v[P - 1]).then_inc(S["last_loaded"], 16)
            sp.wait_ge(S["carry_rows_ready"], CARRY_ROWS)
            sp.dma_start(carry[1:TILES + 1, :].rearrange("(a k) c -> a k c", k=K), carry_rows).then_inc(
                S["carry_stored"], 16)
            sp.dma_start(carry[0:1, :], sentinel).then_inc(S["carry_stored"], 16)
            sp.wait_ge(S["carry_stored"], 32)
            barrier(sp, "carry_over")

            def load_nodes(h, q, ahead):
                g = h * 2 + (q + ahead)
                r = (q + ahead) % 2
                sp.dma_start(x_in[r], x_v[g]).then_inc(S[f"nodes_loaded_{r}"], 16)
                sp.dma_start(a0[r].unsqueeze(2), a0_v[g], allow_slow_non_contiguous=True).then_inc(
                    S[f"nodes_loaded_{r}"], 16)

            load_nodes(0, 0, 0)

            def last_pass(h, q, more):
                if more:
                    alone(sp, "y_ready", done(h, q, 1, 1, 0))
                    load_nodes(h, q, 1)
                alone(sp, "y_ready", done(h, q, 0, 1, 0))
                sp.dma_start(out_v[h * 2 + q], y_out[q]).then_inc(S[f"out_stored_{q}"], 16)

            node_groups(sp, last_pass)
            for q in (0, 1):
                sp.wait_ge(S[f"out_stored_{q}"], 16 * (NODE_GROUPS // 2))

        @block.gpsimd
        def _(pool):
            nc.gpsimd.memset(ident[:, :], 0.0).then_inc(S["consts_made"], 1)
            nc.gpsimd.memset(minus_half[:, :], -0.5).then_inc(S["consts_made"], 1)
            nc.gpsimd.memset(vec_half, -0.5).then_inc(S["consts_made"], 1)
            nc.gpsimd.iota(node_i, pattern=[[P, NODE_TILES]], base=0, channel_multiplier=1).then_inc(
                S["consts_made"], 1)
            pool.wait_ge(S["consts_made"], 4)
            nc.gpsimd.affine_select(out=ident[:, :], in_=ident[:, :], compare_op=ALU.not_equal, fill=1.0, base=0,
                                    pattern=[[-1, 128]], channel_multiplier=1).then_inc(S["consts_made"], 1)
            pool.wait_ge(S["vec_step"], 3)
            nc.gpsimd.tensor_tensor(vec_inv, vec_n2, vec_half, ALU.pow).then_inc(S["vec_root"], 1)
            with pool.Fori(0, NODE_GROUPS) as i:
                alone(pool, "search_ready", i + 1)
                for t in range(NT):
                    nc.gpsimd.indirect_dma_start(
                        out=search_dst[:, t], out_offset=None, in_=dst_tiles,
                        in_offset=bass.IndirectOffsetOnAxis(ap=search_tile_i[:, t:t + 1], axis=0),
                    ).then_inc(S["search_loaded"], 16)
            pool.wait_ge(S["search_loaded"], 16 * NODE_TILES)
            barrier(pool, "prologue_over")

            def rstd(name, count, n, ready):
                alone(pool, name, count)
                nc.gpsimd.tensor_tensor(
                    x_rstd.rearrange("p a b -> p (a b)")[:, 0:n], x_var.rearrange("p a b -> p (a b)")[:, 0:n],
                    minus_half[:, 0:n], ALU.pow).then_inc(S[ready], 1)

            node_groups(pool, lambda h, q, more: rstd("x_var_ready", done(h, q, 0, 1, 0), 2 * NT, "x_rstd_ready"))
            barrier(pool, "node_pass_over")

            def step(h, q, live):
                if not live(0):
                    return
                alone(pool, "idx_ready", done(h, q, 0, 1, 0))
                alone(pool, "sum_ready", done(h, q, 2, G // 2, G // 2 - 1))
                for j in range(G):
                    for at, table_, got in ((0, src_table, got_s), (G, dst_table, got_d)):
                        nc.gpsimd.indirect_dma_start(
                            out=got[q][:, j], out_offset=None, in_=table_,
                            in_offset=bass.IndirectOffsetOnAxis(ap=idx[q][:, at + j:at + j + 1], axis=0),
                        ).then_inc(S[f"gathered_{q}"], 16)
                    if j in (1, 4):
                        alone(pool, "mlp_var_ready", done(h, q, 0, 2, j // 4))
                        nc.gpsimd.tensor_tensor(mlp_rstd, mlp_var, minus_half[:, 0:G], ALU.pow).then_inc(
                            S["mlp_rstd_ready"], 1)

            steps(pool, step)
            for q in (0, 1):
                pool.wait_ge(S[f"gathered_{q}"], 16 * 2 * G * (GROUPS // 2))
            barrier(pool, "edge_pass_over")
            barrier(pool, "carry_over")

            def fetch(h, q, ahead):
                r = (q + ahead) % 2
                alone(pool, "place_ready", done(h, q + ahead, 0, 3, 2))
                for t in range(NT):
                    for k, rows in enumerate((runs, carry)):
                        nc.gpsimd.indirect_dma_start(
                            out=pieces[r][:, k, t], out_offset=None, in_=rows,
                            in_offset=bass.IndirectOffsetOnAxis(ap=place[r][:, k, t:t + 1], axis=0),
                        ).then_inc(S[f"pieces_loaded_{r}"], 16)

            fetch(0, 0, 0)

            def last_pass(h, q, more):
                if more:
                    fetch(h, q, 1)
                rstd("y_var_ready", done(h, q, 0, 2, 0), 2 * NT, "y_rstd_ready")
                rstd("y_var_ready", done(h, q, 0, 2, 1), NT, "y_rstd_ready")

            node_groups(pool, last_pass)
            for q in (0, 1):
                pool.wait_ge(S[f"pieces_loaded_{q}"], PIECES * (NODE_GROUPS // 2))

        @block.scalar
        def _(act):
            barrier(act, "prologue_over")

            def affine(u, w, count):
                wait(act, "node_turned" if w is ln1 else "tile_turned", count)
                nc.scalar.activation(tile_s[0:C0, u], PT[u][0:C0, 0:P], ACT.Identity, bias=w[0:C0, 1:2],
                                     scale=w[0:C0, 0:1]).then_inc(S["affine_ready" if w is ln1 else "tile_copied"], 1)
                nc.scalar.activation(tile_v[0:CV, u, 0], PT[u][0:CV, P:2 * P], ACT.Copy,
                                     scale=w[0:CV, 2:3]).then_inc(S["affine_ready" if w is ln1 else "tile_copied"], 1)

            def node_step(h, q, more):
                for t in range(NT):
                    u = (q * NT + t) % 2
                    wait(act, "node_projected", done(h, q, 0, NT, t, back=2))
                    affine(u, ln1, done(h, q, 0, NT, t))
                    if t == 0:
                        wait(act, f"stored_{q}", turn(h, q, 2, 32))
                    wait(act, "node_projected", done(h, q, 0, NT, t))
                    nc.scalar.copy(table[q][:, t], PL[u][0:P, 0:2 * C]).then_inc(S["table_ready"], 1)

            node_groups(act, node_step)
            barrier(act, "node_pass_over")

            def step(h, q, live):
                for j in range(G):
                    if live(0) and j == 0:
                        wait(act, "mlp_out", done(h, q, 1, 2, 0))
                        wait(act, "es_turned", done(h, q, 0, 1, 0))
                        nc.scalar.copy(es_t, PM[:, 0:4 * P].rearrange("p (a e) -> p a e", a=4)).then_inc(
                            S["es_copied"], 1)
                    if live(0) and j in (1, 4):
                        wait(act, "mlp_ss_ready", done(h, q, 0, 2, j // 4, back=1))
                        wait(act, "mlp_out", done(h, q, 0, 2, j // 4))
                        nc.scalar.activation(mlp_sq, PM[0:P, :].rearrange("p (t c) -> p t c", t=G),
                                             ACT.Square).then_inc(S["mlp_squared"], 1)
                    if live(0) and j in (3, 6):
                        k = j // 6
                        wait(act, "mlp_h_ready", done(h, q, 0, 2, k, back=1))
                        wait(act, "mlp_turned", done(h, q, 0, 2, k))
                        turned = PM[:, 0:4 * P].rearrange("p (a e) -> p a e", a=4)
                        nc.scalar.activation(mlp_tanh, turned, ACT.Tanh, bias=mlp_affine[:, 5 + 2 * k:6 + 2 * k],
                                             scale=mlp_affine[:, 4 + 2 * k:5 + 2 * k]).then_inc(S["mlp_act_ready"], 1)
                        nc.scalar.activation(mlp_y, turned, ACT.Identity, bias=mlp_affine[:, 1 + 2 * k:2 + 2 * k],
                                             scale=mlp_affine[:, 2 * k:1 + 2 * k]).then_inc(S["mlp_act_ready"], 1)
                    lag, k = behind(j, LAG_SUM)
                    if live(lag) and k % 2 == 1:
                        r = (q - lag) % 2
                        if k == 1:
                            wait(act, f"rows_stored_{r}", turn(h, q, lag + 2))
                        wait(act, "sums_ready", done(h, q, lag, G, k))
                        nc.scalar.copy(run_rows[r][:, k - 1:k + 1, 0:SUMS],
                                       PO[0:P, 0:2 * SUMS].rearrange("p (t c) -> p t c", t=2)).then_inc(
                            S["rows_ready"], 1)
                    lag, k = behind(j, LAG_T)
                    if live(lag):
                        wait(act, "lin_ready", done(h, q, lag, G, k, back=2))
                        wait(act, "prods_turned", done(h, q, lag, G, k))
                        nc.scalar.copy(prod_t[k % 2], PT[k % 2][0:CV, 0:4 * P].rearrange("p (a e) -> p a e", a=4)
                                       ).then_inc(S["prods_copied"], 1)
                    lag, k = behind(j, LAG_LIN)
                    if live(lag):
                        wait(act, "att_u_ready", done(h, q, lag, G, k, back=2))
                        wait(act, "lin_ready", done(h, q, lag, G, k))
                        nc.scalar.activation(att_tanh[k % 2], PL[k % 2][0:P, 0:64], ACT.Tanh, scale=0.5).then_inc(
                            S["att_tanh_ready"], 1)
                        wait(act, "pay_ready", done(h, q, lag + 2, 5 * G, 5 * k + 4))
                        nc.scalar.copy(msg[(q - lag) % 2][:, k], PL[k % 2][0:P, 64:LIN]).then_inc(S["msg_ready"], 1)
                    if live(2) and j == 6:
                        wait(act, "pay_ready", done(h, q, 4, 5 * G, 5 * G - 1))
                        wait(act, "logit_d_ready", done(h, q, 2, 1, 0))
                        nc.scalar.activation(prob[q], logit_d, ACT.Exp).then_inc(S["prob_ready"], 1)

            steps(act, step)
            barrier(act, "edge_pass_over")

            act.wait_ge(S["carry_exp_in"], 2)
            nc.scalar.activation(keep, step_m, ACT.Exp).then_inc(S["carry_exp"], 1)
            nc.scalar.activation(take, chan_d, ACT.Exp).then_inc(S["carry_exp"], 1)
            barrier(act, "carry_over")

            def last_pass(h, q, more):
                wait(act, "merge_in", done(h, q, 0, 1, 0))
                nc.scalar.activation(piece_e, piece_d, ACT.Exp).then_inc(S["merge_exp"], 1)
                for t in range(NT):
                    u = (q * NT + t) % 2
                    wait(act, "tile_turned", done(h, q, 0, 3 * NT, t))
                    wait(act, "projected", done(h, q, 0, NT, t, back=2) if t >= 2 else 0)
                    nc.scalar.copy(tile_s[0:C0, u], PT[u][0:C0, 0:P]).then_inc(S["tile_copied"], 1)
                    nc.scalar.copy(tile_v[0:CV, u, 0], PT[u][0:CV, P:2 * P]).then_inc(S["tile_copied"], 1)
                for t in range(NT):
                    u = (q * NT + t) % 2
                    wait(act, "f1_ready", done(h, q, 0, NT, t, back=2) if t >= 2 else 0)
                    affine(u, ln2, done(h, q, 0, 3 * NT, NT + t))
                    wait(act, "ff_scaled", done(h, q, 0, NT, t))
                    wait(act, "ff_ready", done(h, q, 0, 2 * NT, 2 * t + 1, back=4))
                    nc.scalar.activation(ff_t[:, u], ff_g[:, u, 0:192], ACT.Tanh, scale=0.5).then_inc(S["ff_tanh"], 1)
                for t in range(NT):
                    u = (q * NT + t) % 2
                    wait(act, "tile_turned", done(h, q, 0, 3 * NT, 2 * NT + t))
                    wait(act, "f2_ready", done(h, q, 0, NT, t, back=2) if t >= 2 else 0)
                    nc.scalar.copy(tile_s[:, u], PT[u][:, 0:P]).then_inc(S["tile_copied"], 1)
                    nc.scalar.copy(tile_v[0:CV, u], PT[u][0:CV, P:3 * P].rearrange("p (a e) -> p a e", a=2)).then_inc(
                        S["tile_copied"], 1)

            node_groups(act, last_pass)

        @block.tensor
        def _(pe):
            def mm(o, lhs_t, rhs, start=False, stop=False):
                return nc.tensor.matmul(o, lhs_t, rhs, start=start, stop=stop)

            def turn_tile(o, i, n):
                return nc.tensor.transpose(o, i, ident[0:n, 0:n])

            def bias(o, at, n, stop=False):
                return mm(o, ones3[:, 0:P], bias3[:, at:at + n], start=True, stop=stop)

            pe.wait_ge(S["consts_made"], 5)
            pe.wait_ge(S["nat_cast"], 2)
            for c in range(6):
                for b in range(4):
                    k = (c % 2) * 4 + b
                    nat = nat_f[:, c // 2, k] if c < 4 else spread(nat_f[:, 1, k, 0:1], 2, P)[:, 0, :]
                    turned = turn_tile(ps[c][0:P, 100 * b:100 * b + 100], nat, 100)
                turned.then_inc(S["cols_turned"], 1)
            pe.wait_ge(S["nat_loaded"], 48)
            for c in range(6):
                bank = ps[(6 + c) % 8]
                if c >= 2:
                    pe.wait_ge(S["cols_kept"], (1, 2, 5, 6)[c - 2])
                for b in range(4):
                    turned = turn_tile(bank[0:P, 100 * b:100 * b + 100], nat_v[:, (c % 2) * 4 + b, :, c // 2], 100)
                turned.then_inc(S["cols_turned"], 1)
            pe.wait_ge(S["bias_moved"], 48)
            pe.wait_ge(S["weight_step"], WEIGHT_STEPS)
            barrier(pe, "prologue_over")

            def node_step(h, q, more):
                for t in range(NT + 1):
                    if t < NT:
                        u = (q * NT + t) % 2
                        if t == 0:
                            wait(pe, "x_norm_ready", done(h, q, 0, 1, 0))
                        turn_tile(PT[u][0:CV, P:2 * P], x_norm[q][:, t, C0:C], P)
                        turn_tile(PT[u][0:C0, 0:P], x_norm[q][:, t, 0:C0], P).then_inc(S["node_turned"], 1)
                    if t > 0:
                        u = (q * NT + t - 1) % 2
                        wait(pe, "affine_ready", done(h, q, 0, 2 * NT, 2 * t - 1))
                        wait(pe, "table_ready", done(h, q, 0, NT, t - 1, back=2))
                        o = PL[u][0:P, :]
                        bias(o[:, 0:2 * C], B_NODE, 2 * C)
                        mm(o[:, 0:C0], tile_s[0:C0, u], w_node_s[:, 0:64])
                        mm(o[:, C:C + C0], tile_s[0:C0, u], w_node_s[:, 64:128])
                        mm(o[:, C0:C], tile_v[0:CV, u, 0], w_node_v[:, 0:CV])
                        mm(o[:, C + C0:2 * C], tile_v[0:CV, u, 0], w_node_v[:, CV:2 * CV], stop=True).then_inc(
                            S["node_projected"], 1)

            node_groups(pe, node_step)
            barrier(pe, "node_pass_over")

            def mlp(h, q, k, j):
                src = es_t if k == 0 else h1_t
                if k == 0:
                    wait(pe, "es_copied", done(h, q, 0, 1, 0))
                else:
                    wait(pe, "mlp_h_ready", done(h, q, 0, 2, 0))
                wait(pe, "mlp_n_ready", done(h, q, 0, 2, k, back=1))
                bias(PM[0:P, :], (B_MLP1, B_MLP2)[k], 64 * G)
                for a in range(G // 2):
                    last_mm = mm(PM[0:P, 128 * a:128 * a + 128], src[:, a], w_mlp[:, k], stop=a == G // 2 - 1)
                last_mm.then_inc(S["mlp_out"], 1)

            def step(h, q, live):
                for j in range(G):
                    if live(0) and j == 0:
                        wait(pe, "mlp_act_ready", done(h, q, 1, 4, 3))
                        wait(pe, f"es_loaded_{q}", turn(h, q, 0))
                        for a in range(4):
                            turned = turn_tile(PM[:, P * a:P * a + P],
                                               es_in[q][:, 2 * a:2 * a + 2].rearrange("p t c -> p (t c)"), P)
                        turned.then_inc(S["es_turned"], 1)
                    if live(0) and j == 1:
                        mlp(h, q, 0, j)
                    if live(0) and j == 4:
                        mlp(h, q, 1, j)
                    if live(0) and j in (3, 6):
                        k = j // 6
                        wait(pe, "mlp_n_ready", done(h, q, 0, 2, k))
                        if k == 0:
                            wait(pe, "es_copied", done(h, q, 0, 1, 0))
                        else:
                            wait(pe, "mlp_act_ready", done(h, q, 0, 4, 1))
                        for a in range(4):
                            turned = turn_tile(PM[:, P * a:P * a + P],
                                               mlp_n[:, 2 * a:2 * a + 2].rearrange("p t c -> p (t c)"), P)
                        turned.then_inc(S["mlp_turned"], 1)
                    if live(1) and j % 2 == 0:
                        r = 1 - q
                        wait(pe, "prods_ready", done(h, q, 1, 2 * G, 2 * j - 1))
                        wait(pe, "mlp_h_ready", done(h, q, 1, 2, 1))
                        bias(PW[0:P, 0:2 * W_TILE], B_W, 2 * W_TILE)
                        last_mm = mm(PW[0:P, 0:2 * W_TILE], h2_t[r][:, j // 2], w3[:, :], stop=True)
                        last_mm.then_inc(S["w_ready"], 1)
                    lag, k = behind(j, LAG_SUM)
                    if live(lag):
                        u = k % 2
                        wait(pe, "eq_ready", done(h, q, lag, G, k))
                        wait(pe, "pay_ready", done(h, q, lag, 5 * G, 5 * k + 4))
                        if u == 0:
                            wait(pe, "rows_ready", done(h, q, lag, G // 2, k // 2 - 1))
                        o = PO[0:P, SUMS * u:SUMS * (u + 1)]
                        v = o[:, SUMS - CV:SUMS]
                        a, plus, minus = (pay[u][:, SUMS + CV * n:SUMS + CV * (n + 1)] for n in range(3))
                        mm(o, eq[u], pay[u][:, 0:SUMS], start=True)
                        mm(v, eq[u], a)
                        mm(v[:, 0:2 * C1], eq[u], plus[:, C1:CV])
                        mm(v[:, 2 * C1:CV], eq[u], plus[:, 0:C1])
                        mm(v[:, C1:CV], eq[u], minus[:, 0:2 * C1])
                        mm(v[:, 0:C1], eq[u], minus[:, 2 * C1:CV], stop=True).then_inc(S["sums_ready"], 1)
                    lag, k = behind(j, LAG_T)
                    if live(lag):
                        wait(pe, "prods_ready", done(h, q, lag, 2 * G, 4 * (k // 2) + 3))
                        wait(pe, "prods_copied", done(h, q, lag, G, k, back=2))
                        for a, lo in enumerate((0, 96, 160, 256)):
                            turned = turn_tile(PT[k % 2][0:CV, P * a:P * a + P],
                                               prod[(k // 2) % 2][:, k % 2, lo:lo + CV], P)
                        turned.then_inc(S["prods_turned"], 1)
                    lag, k = behind(j, LAG_LIN)
                    if live(lag):
                        u = k % 2
                        wait(pe, "prods_copied", done(h, q, lag, G, k))
                        wait(pe, "msg_ready", done(h, q, lag, G, k, back=2))
                        o = PL[u][0:P, :]
                        bias(o[:, 0:LIN], B_LIN, LIN)
                        mm(o[:, 0:192], prod_t[u][:, 0], w_lin[:, :])
                        mm(o[:, 192:288], prod_t[u][:, 2], w_b[:, :])
                        mm(o[:, 288:320], prod_t[u][0:C0, 1], w_a[:, :])
                        mm(o[:, 320:416], prod_t[u][:, 3], w_c[:, :], stop=True).then_inc(S["lin_ready"], 1)
                    if live(2) and j == 4:
                        wait(pe, "logits_ready", done(h, q, 2, G, G - 1))
                        wait(pe, "logit_d_ready", done(h, q, 3, 1, 0))
                        alone(pe, "max_kept", done(h, q, 3, 2, 1))
                        turn_tile(run_t, logit[q].rearrange("p t h -> p (t h)"), P).then_inc(S["logits_turned"], 1)
                    if live(2) and j == 5:
                        alone(pe, "max_ready", done(h, q, 2, 1, 0))
                        turn_tile(run_b, run_max, G * H).then_inc(S["max_turned"], 1)

            steps(pe, step)
            barrier(pe, "edge_pass_over")

            pe.wait_ge(S["last_loaded"], 16)
            pe.wait_ge(S["last_spread"], 1)
            for b in range(K // 4):
                for k in range(4):
                    cols = slice(100 * k, 100 * k + 100)
                    rows = last[:, 4 * b + k]
                    turn_tile(ps[b][0:HALF, cols], rows[:, 0:HALF], 100)
                    turn_tile(ps[2 + b][0:SUMS - HALF, cols], rows[:, HALF:SUMS], 100)
                    turn_tile(ps[4 + b][0:HALF, cols], last_max[:, 4 * b + k], 100)
                    turned = turn_tile(ps[6 + b][0:HALF, cols], spread(rows[:, R_DST:R_DST + 1], 2, HALF)[:, 0, :], 100)
                turned.then_inc(S["last_turned"], 1)
            pe.wait_ge(S["carry_done"], 1)
            for k in range(K):
                o = ps[k]
                col = scan_x.rearrange("p x (a k) -> p x k a", k=K)[:, :, k]
                turn_tile(o[0:100, 0:HALF], col[:, 0], HALF)
                turn_tile(o[0:100, HALF:SUMS], col[0:SUMS - HALF, 1], SUMS - HALF)
                turn_tile(o[0:100, R_MAX:R_MAX + H], scan_m[0:H].rearrange("p (a k) -> p k a", k=K)[:, k], H).then_inc(S["carry_turned"], 1)
            barrier(pe, "carry_over")

            def last_pass(h, q, more):
                def rounds(turn_in, product):
                    for t in range(NT + 1):
                        if t < NT:
                            turn_in(t, (q * NT + t) % 2)
                        if t > 0:
                            product(t - 1, (q * NT + t - 1) % 2)

                def turn_agg(t, u):
                    if t == 0:
                        wait(pe, "agg_ready", done(h, q, 0, 1, 0))
                    wait(pe, "tile_copied", done(h, q, 0, 6 * NT, 2 * t - 1, back=2))
                    turn_tile(PT[u][0:CV, P:2 * P], agg[:, t, H + C0:SUMS], P)
                    turn_tile(PT[u][0:C0, 0:P], agg[:, t, H:H + C0], P).then_inc(S["tile_turned"], 1)

                def project(t, u):
                    wait(pe, "tile_copied", done(h, q, 0, 6 * NT, 2 * t + 1))
                    wait(pe, "x1_ready", done(h, q, 0, 2 * NT, 2 * t - 3) if t >= 2 else 0)
                    o = PL[u][0:P, :]
                    bias(o[:, 0:C], B_PROJ, C)
                    mm(o[:, 0:C0], tile_s[0:C0, u], w_proj_s[:, :])
                    mm(o[:, C0:C], tile_v[0:CV, u, 0], w_proj_v[:, :], stop=True).then_inc(S["projected"], 1)

                def turn_norm(t, u):
                    if t == 0:
                        wait(pe, "x1_ready", done(h, q, 0, 2 * NT, 2 * NT - 1))
                        wait(pe, "x2_norm_ready", done(h, q, 0, 1, 0))
                    wait(pe, "tile_copied", done(h, q, 0, 6 * NT, 2 * NT + 2 * t - 1, back=2))
                    turn_tile(PT[u][0:CV, P:2 * P], x_norm[0][:, t, C0:C], P)
                    turn_tile(PT[u][0:C0, 0:P], x_norm[0][:, t, 0:C0], P).then_inc(S["tile_turned"], 1)

                def f1(t, u):
                    wait(pe, "tile_copied", done(h, q, 0, 6 * NT, 2 * NT + 2 * t + 1))
                    wait(pe, "ff_scaled", done(h, q, 0, NT, t, back=2))
                    o = PL[u][0:P, :]
                    bias(o[:, 0:192], B_F1, 192)
                    mm(o[:, 0:192], tile_s[0:C0, u], w_f1_s[:, :], stop=True)
                    mm(o[:, 192:384], tile_v[0:CV, u, 0], w_f1_v[:, :], start=True, stop=True).then_inc(
                        S["f1_ready"], 1)

                def turn_ff(t, u):
                    wait(pe, "ff_ready", done(h, q, 0, 2 * NT, 2 * t + 1))
                    wait(pe, "tile_copied", done(h, q, 0, 6 * NT, 4 * NT + 2 * t - 1, back=2))
                    turn_tile(PT[u][:, 0:P], ff_s[:, t], P)
                    turn_tile(PT[u][0:CV, P:2 * P], ff_v[:, t, 0:CV], P)
                    turn_tile(PT[u][0:CV, 2 * P:3 * P], ff_v[:, t, CV:2 * CV], P).then_inc(S["tile_turned"], 1)

                def f2(t, u):
                    wait(pe, "tile_copied", done(h, q, 0, 6 * NT, 4 * NT + 2 * t + 1))
                    wait(pe, "x2_ready", done(h, q, 0, 2 * NT, 2 * t - 3) if t >= 2 else 0)
                    o = (PW, PO)[u][0:P, 0:C]
                    bias(o, B_F2, C)
                    mm(o[:, 0:C0], tile_s[:, u], w_f2_s[:, :])
                    mm(o[:, C0:C], tile_v[0:CV, u, 0], w_f2_v[:, 0])
                    mm(o[:, C0:C], tile_v[0:CV, u, 1], w_f2_v[:, 1], stop=True).then_inc(S["f2_ready"], 1)

                rounds(turn_agg, project)
                for t in range(NT + 2):
                    if t < NT:
                        turn_norm(t, (q * NT + t) % 2)
                    if 0 < t <= NT:
                        f1(t - 1, (q * NT + t - 1) % 2)
                rounds(turn_ff, f2)

            node_groups(pe, last_pass)

        @block.vector
        def _(dve):
            v = nc.vector

            def chain(name):
                count = [0]

                def link(ins):
                    count[0] += 1
                    ins.then_inc(S[name], 1)
                    dve.wait_ge(S[name], count[0])
                return link

            for tile_ in ZERO_TILES:
                v.memset(tile_, 0.0).then_inc(S["zeroed"], 1)
            v.memset(ones3[:, :], 1.0).then_inc(S["zeroed"], 1)
            dve.wait_ge(S["nat_loaded"], 48)
            v.tensor_copy(nat_f[:, 1], nat_i[:, 1]).then_inc(S["nat_cast"], 1)
            v.tensor_copy(nat_f[:, 0], nat_i[:, 0]).then_inc(S["nat_cast"], 1)

            def cols(bank):
                return bank[0:P, 0:400].rearrange("p (k a) -> p a k", k=4)

            for c in range(4):
                dve.wait_ge(S["cols_turned"], c + 1)
                at = c * 4
                last_ins = v.tensor_copy(idx_all[:, :, at:at + 4], cols(ps[c]))
                last_ins.then_inc(S["cols_kept"], 1)
            for c in (2, 3):
                v.tensor_copy(dst_all[:, :, 4 * (c - 2):4 * (c - 2) + 4], cols(ps[c])).then_inc(S["cols_kept"], 1)
            for c in (4, 5):
                dve.wait_ge(S["cols_turned"], c + 1)
                v.tensor_copy(first_dst[:, 400 * (c - 4):400 * (c - 4) + 400], ps[c][0:P, 0:400]).then_inc(
                    S["cols_kept"], 1)
            for c in range(6):
                dve.wait_ge(S["cols_turned"], 6 + c + 1)
                k = (c % 2) * 4
                v.tensor_copy(vec_all[:, :, k:k + 4, c // 2], cols(ps[(6 + c) % 8])).then_inc(S["cols_kept"], 1)

            dve.wait_ge(S["cols_kept"], 14)
            flat = vec_all.rearrange("p g t c -> p (g t) c")
            v.tensor_tensor(vec_sq, flat, flat, ALU.mult).then_inc(S["vec_step"], 1)
            dve.wait_ge(S["vec_step"], 1)
            v.tensor_reduce(vec_n2, vec_sq, AX.X, ALU.add).then_inc(S["vec_step"], 1)
            dve.wait_ge(S["vec_step"], 2)
            v.tensor_scalar(vec_n2, vec_n2, 1e-12, None, ALU.add).then_inc(S["vec_step"], 1)
            dve.wait_ge(S["consts_made"], 5)
            v.tensor_copy(node_all[:, :], node_i).then_inc(S["vec_step"], 1)
            dve.wait_ge(S["vec_root"], 1)
            rh = rhat_all[:, :, :, :].rearrange("p g t c -> p (g t) c")
            v.tensor_tensor(rh[:, :, 0:3], flat, spread(vec_inv, 2, 3), ALU.mult).then_inc(S["vec_step"], 1)
            dve.wait_ge(S["vec_step"], 5)
            v.tensor_copy(rh[:, :, 3:4], rh[:, :, 0:1]).then_inc(S["vec_step"], 1)
            v.tensor_scalar(rh[:, :, 4:5], rh[:, :, 2:3], -1.0, None, ALU.mult).then_inc(S["vec_step"], 1)
            v.tensor_scalar(rh[:, :, 5:7], rh[:, :, 0:2], -1.0, None, ALU.mult).then_inc(S["vec_step"], 1)
            dve.wait_ge(S["vec_step"], 8)

            with dve.Fori(0, NODE_GROUPS) as i:
                links = [0]

                def search(ins):
                    links[0] += 1
                    ins.then_inc(S["search_step"], 1)
                    dve.wait_ge(S["search_step"], i * SEARCH_STEPS + links[0])

                search(v.tensor_copy(search_node, node_all[:, bass.ds(i * NT, NT)]))
                for t in range(NT):
                    search(v.tensor_scalar(search_junk, first_dst, search_node[:, t:t + 1], None, ALU.is_le, ALU.add,
                                           accum_out=search_cnt[:, t:t + 1]))
                search(v.tensor_scalar(search_tile, search_cnt, -1.0, 0.0, ALU.add, ALU.max))
                search(v.tensor_copy(place_all[:, 1, bass.ds(i * NT, NT)], search_tile))
                v.tensor_copy(search_tile_i, search_tile).then_inc(S["search_ready"], 1)
                dve.wait_ge(S["search_loaded"], i * (16 * NT) + 16 * NT)
                search(v.tensor_tensor(search_le, search_dst, spread(search_node, 2, P), ALU.is_le))
                search(v.tensor_reduce(search_in, search_le, AX.X, ALU.add))
                search(v.scalar_tensor_tensor(search_row, search_tile, float(P), search_in, ALU.mult, ALU.add))
                search(v.tensor_scalar(place_all[:, 0, bass.ds(i * NT, NT)], search_row, -1.0, 0.0, ALU.add, ALU.max))
                assert links[0] == SEARCH_STEPS, links[0]

            dve.wait_ge(S["weights_loaded"], 16 * LOADS)
            link = chain("weight_step")
            link(v.tensor_reduce(mlp_mean, w_mlp[:, :, :], AX.X, ALU.add))
            link(v.tensor_scalar(mlp_mean, mlp_mean, 1.0 / 64, None, ALU.mult))
            for rows in (slice(0, 64), slice(64, 128)):
                link(v.tensor_tensor(w_mlp[rows, :, rows], w_mlp[rows, :, rows], spread(mlp_mean[rows], 2, 64),
                                     ALU.subtract))
            link(v.tensor_scalar(w_mlp[:, 1], w_mlp[:, 1], 0.5, None, ALU.mult))
            link(v.tensor_scalar(w3[:, :], w3_raw, 0.5, None, ALU.mult))
            link(v.tensor_scalar(w_f2_s[:, :], w_f2_s[:, :], 0.5, None, ALU.mult))
            link(v.tensor_scalar(w_f2_v[:, :, :], w_f2_v[:, :, :], 0.5, None, ALU.mult))
            link(v.tensor_scalar(mlp_affine[:, 4:8], mlp_affine[:, 0:4], 0.5, None, ALU.mult))
            mlp_bias = bias_row[:, B_MLP1:B_W].rearrange("p (l t c) -> p l t c", l=2, t=G)
            link(v.tensor_reduce(bias_mean, mlp_bias, AX.X, ALU.add))
            link(v.tensor_scalar(bias_mean, bias_mean, 1.0 / 64, None, ALU.mult))
            for l in (0, 1):
                link(v.tensor_tensor(mlp_bias[:, l], mlp_bias[:, l], spread(bias_mean[:, l], 2, 64), ALU.subtract))
            lin_bias = bias_row[:, B_LIN:B_LIN + LIN]
            for o, raw, dot in ((w_lin[:, :], lin_raw, adot), (lin_bias, lin_b_raw, adot[0:1, :])):
                link(v.tensor_copy(o[:, 0:64], raw[:, 0:64]))
                link(v.scalar_tensor_tensor(o[:, 64:128], raw[:, 0:64], 0.4, dot, ALU.mult, ALU.mult))
                link(v.tensor_copy(o[:, 128:192].rearrange("p (k h) -> p k h", k=8),
                                   raw[:, 64:128].rearrange("p (h k) -> p k h", h=H)))
            link(v.tensor_scalar(w_a[:, :].rearrange("p (k h) -> p k h", k=4),
                                 linv_a.rearrange("p (h k) -> p k h", h=H), SQ3, None, ALU.mult))
            for o, raw, factor in ((w_b, linv_b, 1.0), (w_c, linv_c, SQ3 / SQ2)):
                for d in range(3):
                    link(v.tensor_scalar(o[:, C1 * d:C1 * (d + 1)].rearrange("p (k h) -> p k h", k=4),
                                         raw[:, C1 * d:C1 * (d + 1)].rearrange("p (h k) -> p k h", h=H),
                                         factor, None, ALU.mult))
            link(v.tensor_copy(bias_parts[:, 0], bias_row))
            link(v.tensor_tensor(bias_rest, bias_row, bias_parts[:, 0], ALU.subtract))
            link(v.tensor_copy(bias_parts[:, 1], bias_rest))
            link(v.tensor_tensor(bias_row, bias_rest, bias_parts[:, 1], ALU.subtract))
            link(v.tensor_copy(bias_parts[:, 2], bias_row))
            barrier(dve, "prologue_over")

            def by_component(ap):
                return ap.rearrange("p t (u d) -> p t d u", d=3)

            def normed(link, x, o, var_ready, count, rstd_ready, last_link):
                link(v.tensor_reduce(x_sum, x[:, :, 0:C0], AX.X, ALU.add))
                link(v.tensor_scalar(x_mean, x_sum, 1.0 / C0, None, ALU.mult))
                link(v.tensor_tensor(x_cen[:, :, 0:C0], x[:, :, 0:C0], spread(x_mean, 2, C0), ALU.subtract))
                link(v.tensor_tensor(x_sq[:, :, 0:C0], x_cen[:, :, 0:C0], x_cen[:, :, 0:C0], ALU.mult))
                link(v.tensor_tensor(x_sq[:, :, C0:C], x[:, :, C0:C], x[:, :, C0:C], ALU.mult))
                link(v.tensor_reduce(x_ss[:, 0], x_sq[:, :, 0:C0], AX.X, ALU.add))
                link(v.tensor_reduce(x_ss[:, 1], x_sq[:, :, C0:C], AX.X, ALU.add))
                link(v.tensor_scalar(x_var[:, 0], x_ss[:, 0], 1.0 / C0, EPS, ALU.mult, ALU.add))
                v.tensor_scalar(x_var[:, 1], x_ss[:, 1], 1.0 / CV, EPS, ALU.mult, ALU.add).then_inc(S[var_ready], 1)
                wait(dve, rstd_ready, count)
                link(v.tensor_tensor(o[:, :, 0:C0], x_cen[:, :, 0:C0], spread(x_rstd[:, 0], 2, C0), ALU.mult))
                last_link(v.tensor_tensor(o[:, :, C0:C].rearrange("p t (d u) -> p t d u", d=3),
                                          by_component(x[:, :, C0:C]),
                                          spread(spread(x_rstd[:, 1], 2, 3), 3, C1), ALU.mult))

            def node_step(h, q, more):
                links = [0]

                def link(ins):
                    links[0] += 1
                    ins.then_inc(S["norm_step"], 1)
                    dve.wait_ge(S["norm_step"], h * (2 * NORM_STEPS) + (q * NORM_STEPS + links[0]))

                wait(dve, f"x_loaded_{q}", turn(h, q, 0))
                wait(dve, "node_turned", done(h, q, 2, NT, NT - 1))
                normed(link, x_in[q], x_norm[q], "x_var_ready", done(h, q, 0, 1, 0), "x_rstd_ready",
                       lambda ins: ins.then_inc(S["x_norm_ready"], 1))
                assert links[0] == NORM_STEPS, links[0]

            node_groups(dve, node_step)
            barrier(dve, "node_pass_over")

            v.memset(run_mask, -BIG).then_inc(S["edge_consts"], 1)
            for q in (0, 1):
                v.memset(run_rows[q], 0.0).then_inc(S["edge_consts"], 1)

            dve.wait_ge(S["edge_consts"], 3)
            v.tensor_copy(idx[0], idx_all[:, 0, :]).then_inc(S["idx_ready"], 1)

            def step(h, q, live):
                for j in range(G):
                    p = j // 2
                    if j == 0 and live(-1):
                        r = 1 - q
                        wait(dve, f"gathered_{r}", turn(h, q, 1, 16 * 2 * G))
                        v.tensor_copy(idx[r], idx_all[:, one(h * 2 + (q + 1))].rearrange("p x t -> p (x t)")).then_inc(
                            S["idx_ready"], 1)
                    if j == 0 and live(1):
                        r = 1 - q
                        wait(dve, "prob_r_ready", done(h, q, 3, 1, 0))
                        wait(dve, "dots_in", done(h, q, 3, G // 2, G // 2 - 1))
                        v.tensor_copy(rhat[r], rhat_all[:, one(h * 2 + (q - 1))].rearrange(
                            "p x t c -> p (x t) c")).then_inc(S["rhat_ready"], 1)
                    ea = live(1)
                    r = 1 - q
                    pair = slice(2 * p, 2 * p + 2)
                    mv = feat[:, :, C0:C]
                    if ea and j % 2 == 0:
                        if p == 0:
                            wait(dve, f"gathered_{r}", turn(h, q, 1, 16 * 2 * G))
                        wait(dve, "prods_ready", done(h, q, 1, 2 * G, 4 * p - 1))
                        wait(dve, "dots_in", done(h, q, 1, G // 2, p - 1))
                        v.tensor_tensor(feat[:, :, 0:C], got_s[r][:, pair], got_d[r][:, pair], ALU.add).then_inc(
                            S["sum_ready"], 1)
                    plag, pk = behind(j, LAG_PAY)
                    pr, pu = (q - plag) % 2, pk % 2
                    if live(plag):
                        if pk == 0:
                            wait(dve, f"meta_loaded_{pr}", turn(h, q, plag, 32))
                            wait(dve, "cols_ready", done(h, q, plag, 1, 0))
                        wait(dve, "sums_ready", done(h, q, plag, G, pk, back=2))
                        v.tensor_scalar(eq[pu], dst_row[pr][:, pk], dst_col[pr][:, pk:pk + 1], None,
                                        ALU.is_equal).then_inc(S["eq_ready"], 1)
                    if ea and j % 2 == 0:
                        if p == 0:
                            wait(dve, "rhat_ready", done(h, q, 1, 1, 0))
                        wait(dve, "sum_ready", done(h, q, 1, G // 2, p))
                        wait(dve, "dots_ready", done(h, q, 1, G // 2, p - 1))
                        v.tensor_tensor(dot_in.rearrange("p t (d u) -> p t d u", d=3),
                                        mv.rearrange("p t (d u) -> p t d u", d=3),
                                        spread(rhat[r][:, pair, 0:3], 3, C1), ALU.mult).then_inc(S["dots_in"], 1)
                    if live(plag):
                        m = msg[pr][:, pk, 64:MSG]
                        if pk == 0:
                            wait(dve, "prob_r_ready", done(h, q, plag, 1, 0))
                            wait(dve, "prob_ready", done(h, q, plag, 1, 0))
                        wait(dve, "msg_ready", done(h, q, plag, G, pk))
                        v.tensor_tensor(pay[pu][:, H:SUMS].rearrange("p (k h) -> p k h", h=H),
                                        m[:, 0:C].rearrange("p (k h) -> p k h", h=H),
                                        spread(prob[pr][:, pk], 1, C // H), ALU.mult).then_inc(S["pay_ready"], 1)
                        v.tensor_copy(pay[pu][:, 0:H], prob[pr][:, pk]).then_inc(S["pay_ready"], 1)
                    if ea and j % 2 == 0:
                        wait(dve, "dots_in", done(h, q, 1, G // 2, p))
                        v.tensor_reduce(feat[:, :, C:C + C1], dot_in.rearrange("p t (d u) -> p t u d", d=3), AX.X,
                                        ALU.add).then_inc(S["dots_ready"], 1)
                    if ea and j % 2 == 1:
                        w = PW[0:P, 0:2 * W_TILE].rearrange("p (t c) -> p t c", t=2)
                        o = prod[p % 2]
                        wait(dve, "dots_ready", done(h, q, 1, G // 2, p))
                        wait(dve, "prods_turned", done(h, q, 1, G, 2 * p + 1, back=4))
                        wait(dve, "w_ready", done(h, q, 1, G // 2, p))
                        v.tensor_tensor(o[:, :, 0:192].rearrange("p t (a c) -> p t a c", a=2)[:, :, :, 0:C0],
                                        w[:, :, 0:192].rearrange("p t (a c) -> p t a c", a=2)[:, :, :, 0:C0],
                                        spread(feat[:, :, 0:C0], 2, 2), ALU.mult).then_inc(S["prods_ready"], 1)
                        v.tensor_tensor(o[:, :, 64:96], w[:, :, 64:96], feat[:, :, C:C + C1], ALU.mult).then_inc(
                            S["prods_ready"], 1)
                        for at, lo in ((160, 160), (256, 192)):
                            v.tensor_tensor(o[:, :, at:at + CV].rearrange("p t (d u) -> p t d u", d=3),
                                            spread(w[:, :, lo:lo + C1], 2, 3),
                                            mv.rearrange("p t (d u) -> p t d u", d=3), ALU.mult).then_inc(
                                S["prods_ready"], 1)
                    lag, k = behind(j, LAG_ATT)
                    if live(lag):
                        wait(dve, "logits_ready", done(h, q, lag, G, k, back=2))
                        wait(dve, "att_tanh_ready", done(h, q, lag, G, k))
                        wait(dve, "msg_ready", done(h, q, lag, G, k))
                        v.scalar_tensor_tensor(att_u[k % 2], att_tanh[k % 2], 1.5, msg[(q - lag) % 2][:, k, 0:64],
                                               ALU.add, ALU.mult).then_inc(S["att_u_ready"], 1)
                    if live(plag):
                        a = m[:, C:C + C1].rearrange("p (k h) -> p k h", h=H)
                        c_ = m[:, C + C1:C + C1 + CV].rearrange("p (d k h) -> p d k h", d=3, h=H)
                        for n, (src_, lo) in enumerate(((spread(a, 1, 3), 0), (c_, 1), (c_, 4))):
                            v.tensor_tensor(
                                pay[pu][:, SUMS + CV * n:SUMS + CV * (n + 1)].rearrange("p (d k h) -> p d k h", d=3, h=H),
                                src_, spread(prob_r[pr][:, pk, lo:lo + 3], 2, 4), ALU.mult).then_inc(S["pay_ready"], 1)
                    if live(lag):
                        wait(dve, "att_u_ready", done(h, q, lag, G, k))
                        if k == 0:
                            wait(dve, "logit_d_ready", done(h, q, lag + 2, 1, 0))
                            wait(dve, "logits_turned", done(h, q, lag + 2, 1, 0))
                        v.tensor_reduce(logit[(q - lag) % 2][:, k], att_u[k % 2].rearrange("p (h k) -> p h k", h=H),
                                        AX.X, ALU.add).then_inc(S["logits_ready"], 1)
                    if live(0) and j in (1, 4):
                        k = j // 4
                        wait(dve, "mlp_var_ready", done(h, q, 0, 2, k, back=1))
                        wait(dve, "mlp_squared", done(h, q, 0, 2, k))
                        v.tensor_reduce(mlp_ss, mlp_sq, AX.X, ALU.add).then_inc(S["mlp_ss_ready"], 1)
                        wait(dve, "mlp_rstd_ready", done(h, q, 0, 2, k, back=1))
                        wait(dve, "mlp_ss_ready", done(h, q, 0, 2, k))
                        v.tensor_scalar(mlp_var, mlp_ss, 1.0 / 64, EPS, ALU.mult, ALU.add).then_inc(
                            S["mlp_var_ready"], 1)
                    if live(0) and j in (2, 5):
                        k = j // 5
                        wait(dve, "mlp_turned", done(h, q, 0, 2, k, back=1))
                        wait(dve, "mlp_rstd_ready", done(h, q, 0, 2, k))
                        v.tensor_tensor(mlp_n, PM[0:P, :].rearrange("p (t c) -> p t c", t=G), spread(mlp_rstd, 2, 64),
                                        ALU.mult).then_inc(S["mlp_n_ready"], 1)
                    if live(0) and j in (3, 6):
                        k = j // 6
                        wait(dve, "mlp_act_ready", done(h, q, 0, 4, 2 * k + 1))
                        if k == 0:
                            wait(dve, "mlp_out", done(h, q, 1, 2, 1))
                        else:
                            wait(dve, "w_ready", done(h, q, 2, G // 2, G // 2 - 1))
                        v.scalar_tensor_tensor((h1_t, h2_t[q])[k], mlp_tanh, 1.0, mlp_y, ALU.add, ALU.mult).then_inc(
                            S["mlp_h_ready"], 1)
                    if live(2) and j == 3:
                        wait(dve, "eq_ready", done(h, q, 4, G, G - 1))
                        v.tensor_copy(dst_col[q], dst_all[:, one(h * 2 + (q - 2))].rearrange("p x t -> p (x t)")
                                      ).then_inc(S["cols_ready"], 1)
                        wait(dve, "mask_ready", done(h, q, 3, 1, 0))
                        wait(dve, f"meta_loaded_{q}", turn(h, q, 2, 32))
                        v.tensor_tensor(run_ne[:, 0:P - 1], dst_th[q][:, 1:P], dst_th[q][:, 0:P - 1],
                                        ALU.not_equal).then_inc(S["run_ne_ready"], 1)
                        wait(dve, "run_ne_ready", done(h, q, 2, 1, 0))
                        wait(dve, "max_ready", done(h, q, 3, 1, 0))
                        v.tensor_scalar(run_mask[:, 1:P], run_ne[:, 0:P - 1], -BIG, None, ALU.mult).then_inc(
                            S["mask_ready"], 1)
                    if live(2) and j == 4:
                        wait(dve, "mask_ready", done(h, q, 2, 1, 0))
                        wait(dve, "max_ready", done(h, q, 3, 1, 0))
                        wait(dve, "logits_turned", done(h, q, 2, 1, 0))
                        v.tensor_tensor_scan(run_fwd, run_mask[:, 0:P], run_t, 0.0, ALU.add, ALU.max).then_inc(
                            S["fwd_ready"], 1)
                    if live(2) and j == 5:
                        wait(dve, "max_turned", done(h, q, 3, 1, 0))
                        wait(dve, "fwd_ready", done(h, q, 2, 1, 0))
                        v.tensor_tensor_scan(run_max[:, ::-1], run_mask[:, 1:P + 1][:, ::-1], run_fwd[:, ::-1], 0.0,
                                             ALU.add, ALU.max).then_inc(S["max_ready"], 1)
                    if live(2) and j == 6:
                        wait(dve, "prob_ready", done(h, q, 3, 1, 0))
                        wait(dve, "max_turned", done(h, q, 2, 1, 0))
                        back = run_b.rearrange("p (t h) -> p t h", t=G)
                        v.tensor_tensor(logit_d, logit[q], back, ALU.subtract).then_inc(S["logit_d_ready"], 1)
                        wait(dve, f"rows_stored_{q}", turn(h, q, 4))
                        v.tensor_copy(run_rows[q][:, :, R_MAX:R_MAX + H], back).then_inc(S["max_kept"], 1)
                        wait(dve, "cols_ready", done(h, q, 2, 1, 0))
                        v.tensor_copy(run_rows[q][:, :, R_DST:R_DST + 1], dst_col[q].unsqueeze(2)).then_inc(
                            S["max_kept"], 1)
                    if live(2) and j == 7:
                        wait(dve, "pay_ready", done(h, q, 4, 5 * G, 5 * G - 1))
                        wait(dve, "prob_ready", done(h, q, 2, 1, 0))
                        v.tensor_tensor(prob_r[q], spread(prob[q], 2, RDIR), spread(rhat[q], 3, H), ALU.mult).then_inc(
                            S["prob_r_ready"], 1)

            steps(dve, step)
            barrier(dve, "edge_pass_over")

            link = chain("carry_step")

            def by_tile(ap):
                return ap.rearrange("p (a k) -> p a k", k=K)

            dve.wait_ge(S["last_loaded"], 16)
            v.tensor_copy(last_max.rearrange("p t (k h) -> p t k h", h=H),
                          spread(last[:, :, R_MAX:R_MAX + H], 2, HALF // H)).then_inc(S["last_spread"], 1)
            for b in range(2):
                dve.wait_ge(S["last_turned"], b + 1)
                for o, bank, n in ((chan[:, 0], ps[b], HALF), (chan[:, 1], ps[2 + b], SUMS - HALF),
                                   (chan_m, ps[4 + b], HALF), (chan_d, ps[6 + b], HALF)):
                    link(v.tensor_copy(by_tile(o[0:n])[:, :, 4 * b:4 * b + 4],
                                       bank[0:n, 0:400].rearrange("p (k a) -> p a k", k=4)))
            link(v.memset(same[:, 0:1], 0.0))
            link(v.memset(step_m[:, 0:1], 0.0))
            link(v.tensor_tensor(same[:, 1:], chan_d[:, 1:], chan_d[:, 0:TILES - 1], ALU.is_equal))
            link(v.tensor_scalar(restart, same, BIG, -BIG, ALU.mult, ALU.add))
            link(v.tensor_tensor_scan(scan_m, restart, chan_m, 0.0, ALU.add, ALU.max))
            link(v.tensor_tensor(step_m[:, 1:], scan_m[:, 0:TILES - 1], scan_m[:, 1:], ALU.subtract))
            link(v.tensor_scalar(step_m, step_m, 0.0, None, ALU.min))
            v.tensor_copy(chan_x[:, 0], chan[:, 0]).then_inc(S["carry_exp_in"], 1)
            v.tensor_tensor(chan_d, chan_m, scan_m, ALU.subtract).then_inc(S["carry_exp_in"], 1)
            dve.wait_ge(S["carry_exp"], 2)
            link(v.tensor_tensor(keep, keep, same, ALU.mult))
            link(v.tensor_tensor(chan_x[:, 0], chan[:, 0], take, ALU.mult))
            n = SUMS - HALF
            link(v.tensor_tensor(chan_x[0:n, 1], chan[0:n, 1], take[0:n], ALU.mult))
            link(v.tensor_tensor_scan(scan_x[:, 0], keep, chan_x[:, 0], 0.0, ALU.mult, ALU.add))
            link(v.memset(sentinel, 0.0))
            link(v.memset(sentinel[:, R_DST:R_DST + 1], -1.0))
            v.tensor_tensor_scan(scan_x[0:n, 1], keep[0:n], chan_x[0:n, 1], 0.0, ALU.mult, ALU.add).then_inc(
                S["carry_done"], 1)
            v.memset(carry_rows, 0.0).then_inc(S["carry_rows_ready"], 1)
            dve.wait_ge(S["carry_rows_ready"], 1)
            v.tensor_copy(carry_rows[:, :, R_DST:R_DST + 1], last[:, :, R_DST:R_DST + 1]).then_inc(
                S["carry_rows_ready"], 1)
            for k in range(K):
                dve.wait_ge(S["carry_turned"], k + 1)
                v.tensor_copy(carry_rows[:, k, 0:R_DST], ps[k][0:100, 0:R_DST]).then_inc(S["carry_rows_ready"], 1)
            barrier(dve, "carry_over")

            def places(h, q, ahead):
                r = (q + ahead) % 2
                g = h * (2 * NT) + (q + ahead) * NT
                for k in (0, 1):
                    v.tensor_copy(place[r][:, k], place_all[:, k, bass.ds(g, NT)]).then_inc(S["place_ready"], 1)
                v.tensor_copy(node_no[r], node_all[:, bass.ds(g, NT)]).then_inc(S["place_ready"], 1)

            places(0, 0, 0)

            def last_pass(h, q, more):
                links = [0]

                def link(ins):
                    links[0] += 1
                    ins.then_inc(S["last_step"], 1)
                    dve.wait_ge(S["last_step"], h * (2 * LAST_STEPS) + (q * LAST_STEPS + links[0]))

                if more:
                    places(h, q, 1)
                wait(dve, "place_ready", done(h, q, 0, 3, 2))
                wait(dve, f"pieces_loaded_{q}", turn(h, q, 0, PIECES))
                wait(dve, f"nodes_loaded_{q}", turn(h, q, 0, 32))
                two = pieces[q]
                link(v.tensor_tensor(found, two[:, :, :, R_DST], spread(node_no[q], 1, 2), ALU.is_equal))
                link(v.tensor_scalar(absent, found, BIG, -BIG, ALU.mult, ALU.add))
                link(v.tensor_tensor(piece_max, two[:, :, :, R_MAX:R_MAX + H], spread(absent, 3, H), ALU.add))
                link(v.tensor_tensor(both_max, piece_max[:, 0], piece_max[:, 1], ALU.max))
                v.tensor_tensor(piece_d, piece_max, spread(both_max, 1, 2), ALU.subtract).then_inc(S["merge_in"], 1)
                wait(dve, "merge_exp", done(h, q, 0, 1, 0))
                link(v.tensor_tensor(piece_f, piece_e, spread(found, 3, H), ALU.mult))
                for k, o in enumerate((agg_a, agg_b)):
                    link(v.tensor_tensor(o.rearrange("p t (k h) -> p t k h", h=H),
                                         two[:, k, :, 0:SUMS].rearrange("p t (k h) -> p t k h", h=H),
                                         spread(piece_f[:, k], 2, SUMS // H), ALU.mult))
                link(v.tensor_tensor(agg_a, agg_a, agg_b, ALU.add))
                link(v.tensor_scalar(den, agg_a[:, :, 0:H], 1e-12, None, ALU.add))
                link(v.reciprocal(rden, den))
                v.tensor_tensor(agg[:, :, H:SUMS].rearrange("p t (k h) -> p t k h", h=H),
                                agg_a[:, :, H:SUMS].rearrange("p t (k h) -> p t k h", h=H),
                                spread(rden, 2, C // H), ALU.mult).then_inc(S["agg_ready"], 1)
                x = x_in[q]
                for t in range(NT):
                    u = (q * NT + t) % 2
                    wait(dve, "projected", done(h, q, 0, NT, t))
                    v.tensor_tensor(x1[:, t, 0:C0], x[:, t, 0:C0], PL[u][0:P, 0:C0], ALU.add).then_inc(
                        S["x1_ready"], 1)
                    v.tensor_tensor(x1[:, t, C0:C].rearrange("p (u d) -> p d u", d=3),
                                    x[:, t, C0:C].rearrange("p (u d) -> p d u", d=3),
                                    PL[u][0:P, C0:C].rearrange("p (d u) -> p d u", d=3), ALU.add).then_inc(
                        S["x1_ready"], 1)
                wait(dve, "x1_ready", done(h, q, 0, 2 * NT, 2 * NT - 1))
                normed(link, x1, x_norm[0], "y_var_ready", done(h, q, 0, 2, 0), "y_rstd_ready",
                       lambda ins: ins.then_inc(S["x2_norm_ready"], 1))
                link(v.tensor_tensor(y_sum, x, x1, ALU.add))
                for t in range(NT):
                    u = (q * NT + t) % 2
                    wait(dve, "f1_ready", done(h, q, 0, NT, t))
                    v.tensor_scalar(ff_g[:, u], PL[u][0:P, 0:384], a0[q][:, t:t + 1], None, ALU.mult).then_inc(
                        S["ff_scaled"], 1)
                    wait(dve, "ff_scaled", done(h, q, 0, NT, t))
                    wait(dve, "ff_tanh", done(h, q, 0, NT, t))
                    v.scalar_tensor_tensor(ff_s[:, t], ff_t[:, u, 0:M0], 1.0, ff_g[:, u, 0:M0], ALU.add,
                                           ALU.mult).then_inc(S["ff_ready"], 1)
                    v.scalar_tensor_tensor(ff_v[:, t].rearrange("p (d m) -> p d m", d=3),
                                           spread(ff_t[:, u, M0:192], 1, 3), 1.0,
                                           ff_g[:, u, 192:384].rearrange("p (d m) -> p d m", d=3), ALU.add,
                                           ALU.mult).then_inc(S["ff_ready"], 1)
                for t in range(NT):
                    u = (q * NT + t) % 2
                    o = (PW, PO)[u][0:P, 0:C]
                    wait(dve, "f2_ready", done(h, q, 0, NT, t))
                    v.scalar_tensor_tensor(y_sum[:, t, 0:C0], o[:, 0:C0], a0[q][:, t:t + 1], y_sum[:, t, 0:C0],
                                           ALU.mult, ALU.add).then_inc(S["x2_ready"], 1)
                    yv = y_sum[:, t, C0:C].rearrange("p (u d) -> p d u", d=3)
                    v.scalar_tensor_tensor(yv, o[:, C0:C].rearrange("p (d u) -> p d u", d=3), a0[q][:, t:t + 1], yv,
                                           ALU.mult, ALU.add).then_inc(S["x2_ready"], 1)
                wait(dve, "x2_ready", done(h, q, 0, 2 * NT, 2 * NT - 1))
                link(v.tensor_reduce(x_sum, y_sum, AX.X, ALU.add))
                link(v.tensor_scalar(x_mean, x_sum, 1.0 / C, None, ALU.mult))
                link(v.tensor_tensor(x_cen, y_sum, spread(x_mean, 2, C), ALU.subtract))
                link(v.tensor_tensor(x_sq, x_cen, x_cen, ALU.mult))
                link(v.tensor_reduce(x_ss[:, 0], x_sq, AX.X, ALU.add))
                v.tensor_scalar(x_var[:, 0], x_ss[:, 0], 1.0 / C, EPS, ALU.mult, ALU.add).then_inc(
                    S["y_var_ready"], 1)
                wait(dve, f"out_stored_{q}", turn(h, q, 2))
                wait(dve, "y_rstd_ready", done(h, q, 0, 2, 1))
                v.tensor_tensor(y_out[q], x_cen, spread(x_rstd[:, 0], 2, C), ALU.mult).then_inc(S["y_ready"], 1)
                assert links[0] == LAST_STEPS, links[0]

            node_groups(dve, last_pass)


def kernel(**inputs):
    import numpy as _np
    import concourse.bacc as _bacc
    from concourse import mybir as _mybir
    from concourse.bass_utils import run_bass_kernel_spmd as _run

    nc = _bacc.Bacc("TRN2", target_bir_lowering=False, num_devices=1)
    arrays, handles = {}, {}
    for name in inputs:
        a = _np.ascontiguousarray(inputs[name])
        arrays[f"in_{name}"] = a
        handles[name] = nc.dram_tensor(f"in_{name}", a.shape, _mybir.dt.from_np(a.dtype), kind="ExternalInput").ap()
    out = nc.dram_tensor("out", (N, C), F32, kind="ExternalOutput").ap()
    build(nc, handles, out)
    r = _run(nc, [arrays], core_ids=[0])
    return r.results[0]["out"]
```

```python
import concourse.bass as bass
from concourse import mybir
from contextlib import ExitStack

F32 = mybir.dt.float32
BF16 = mybir.dt.bfloat16
I32 = mybir.dt.int32
ALU = mybir.AluOpType
ACT = mybir.ActivationFunctionType
AX = mybir.AxisListType

N, E = 6250, 100000
C0, C1 = 64, 32
CV = 3 * C1
C = C0 + CV
H = 8
M0, M1 = 128, 64
P = 125
G = 8
TILES = E // P
GROUPS = TILES // G
NT = 5
NODE_TILES = N // P
NODE_GROUPS = NODE_TILES // NT
ROW = 180
SUMS = H + C
R_MAX, R_DST = SUMS, SUMS + H
BIG = 1e30
EPS = 1e-5
SQ3 = 3.0 ** 0.5
SQ2 = 2.0 ** 0.5

B_NODE, B_MLP1, B_MLP2, B_W, B_PROJ, B_F1, B_F2, B_END = 0, 320, 832, 1344, 1792, 1952, 2144, 2304
W_TILE = 224
PROD = 4 * 128
ONE, REST = C0 + C1, 128
LIN = 328
LIN_S = 200
MSG = LIN - 64
PAY = SUMS + CV

RDIR = 7
LAG_T, LAG_LIN, LAG_ATT, LAG_PAY, LAG_SUM = 2, 3, 4, 16, 17
W_ORDER = ((0, 0, 64), (64, 160, 192), (96, 64, 128), (160, 128, 160), (192, 192, 224))
PIECES = 16 * 2 * NT
LOADS, WEIGHT_STEPS, COUNT_STEPS, PLACE_STEPS, NORM_STEPS, LAST_STEPS = 112, 32, 8, 4, 9, 25
REST_BLOCKS = ((0, 0, C0, CV, SQ3),) + tuple(
    (C0 + C1 * b, lo, lo + C1, C1 * d, factor)
    for b, (lo, d, factor) in enumerate(
        [(C0, d, 1.0) for d in range(3)]
        + [(C0 + C1, (d + 2) % 3, SQ3 / SQ2) for d in range(3)]
        + [(C0 + C1, (d + 1) % 3, SQ3 / SQ2) for d in range(3)]))
CARRY_ROWS = 2 + 8
PEEL, LOOP_END, STEPS = 6, GROUPS - 2, GROUPS + 4


def spread(ap, axis, n):
    ap = ap.unsqueeze(axis)
    shape = list(ap.shape)
    shape[axis] = n
    return ap.broadcast_to(shape)


def build(nc, inp, out):
    ctx = ExitStack()
    with ctx:
        def sb(name, shape, dt=F32):
            return ctx.enter_context(nc.sbuf_tensor(name, shape, dt))

        def sem(name):
            return ctx.enter_context(nc.semaphore(name))

        src_table = nc.dram_tensor("src_table", (N, C), F32).ap()
        dst_table = nc.dram_tensor("dst_table", (N, C), F32).ap()
        runs = nc.dram_tensor("runs", (E, ROW), F32).ap()
        carry = nc.dram_tensor("carry", (TILES + 1, ROW), F32).ap()

        ident = sb("ident", [128, 128])
        ones3 = sb("ones3", [3, 128], BF16)
        bias3 = sb("bias3", [3, B_END], BF16)
        ln1 = sb("ln1", [CV, 3])
        ln2 = sb("ln2", [CV, 3])
        mlp_affine = sb("mlp_affine", [128, 8])
        w_node_s = sb("w_node_s", [C0, 128])
        w_node_v = sb("w_node_v", [CV, 192])
        w_mlp = sb("w_mlp", [128, 2, 128])
        w3 = sb("w3", [128, 2 * W_TILE])
        w_lin = sb("w_lin", [128, LIN_S])
        w_rest = sb("w_rest", [128, 3, 128])
        w_proj_s = sb("w_proj_s", [C0, C0])
        w_proj_v = sb("w_proj_v", [CV, CV])
        w_f1_s = sb("w_f1_s", [C0, 192])
        w_f1_v = sb("w_f1_v", [CV, 192])
        w_f2_s = sb("w_f2_s", [M0, C0])
        w_f2_v = sb("w_f2_v", [CV, 2, CV])
        minus_half = sb("minus_half", [P, 16])

        idx_all = sb("idx_all", [P, GROUPS, 2 * G], I32)
        dst_all = sb("dst_all", [P, GROUPS, G])
        rhat_all = sb("rhat_all", [P, GROUPS, G, RDIR])
        node_all = sb("node_all", [P, NODE_TILES])
        place_all = sb("place_all", [P, 2, NODE_TILES], I32)

        AREA = 34000
        area = sb("area", [128, AREA])
        top = [0]

        def part(parts, *dims, dt=F32, reset=False):
            if reset:
                top[0] = 0
            n = 1
            for d in dims:
                n *= d
            words = n if dt != BF16 else (n + 1) // 2
            ap = area[0:parts, top[0]:top[0] + words]
            top[0] += words
            assert top[0] <= AREA, top[0]
            if dt != F32:
                ap = ap.bitcast(dt)
            names = "abcd"[:len(dims)]
            if len(dims) > 1:
                ap = ap.rearrange(f"p ({' '.join(names)}) -> p {' '.join(names)}",
                                  **{m: d for m, d in zip(names[1:], dims[1:])})
            return ap

        K = TILES // 100
        nat_i = part(100, 2, K, P, dt=I32, reset=True)
        nat_f = part(100, 2, K, P)
        nat_v = part(100, K, P, 3)
        first_dst = part(P, TILES)
        vec_all = part(P, GROUPS, G, 3)
        vec_sq = part(P, TILES, 3)
        vec_n2 = part(P, TILES)
        vec_inv = part(P, TILES)
        vec_root = part(P, TILES)
        node_i = part(P, NODE_TILES, dt=I32)
        search_junk = vec_sq.rearrange("p t c -> p (t c)")[:, 0:TILES]
        search_node = [part(P, NT) for q in (0, 1)]
        search_cnt = part(P, NT)
        search_tile = [part(P, NT) for q in (0, 1)]
        search_tile_i = [part(P, NT, dt=I32) for q in (0, 1)]
        search_dst = [part(P, NT, P, dt=I32) for q in (0, 1)]
        search_le = part(P, NT, P)
        search_in = part(P, NT)
        search_row = part(P, NT)
        bias_row = part(1, B_END)
        bias_rest = part(1, B_END)
        bias_parts = part(1, 3, B_END, dt=BF16)
        bias_mean = part(1, 2, G)
        mlp_mean = part(128, 2)
        w3_raw = part(128, 2 * W_TILE)
        lin_raw = part(CV + 1, 128)
        adot = part(CV + 1, 64)
        raw_rest = part(128, 3, C1)
        x_in = [part(P, NT, C, reset=(q == 0)) for q in (0, 1)]
        x_sq = part(P, NT, C)
        x_norm = [part(P, NT, C) for q in (0, 1)]
        x_sum = part(P, NT)
        x_mean = part(P, NT)
        x_cen = part(P, NT, C)
        x_ss = part(P, 2, NT)
        x_var = part(P, 2, NT)
        x_rstd = part(P, 2, NT)
        table = [part(P, NT, 2 * C) for q in (0, 1)]
        tile_s = part(128, 2, P)
        tile_v = part(CV, 2, 2, P)
        a0 = [part(P, NT) for q in (0, 1)]
        node_no = [part(P, NT) for q in (0, 1)]
        place = [part(P, 2, NT, dt=I32) for q in (0, 1)]
        pieces = [part(P, 2, NT, ROW) for q in (0, 1)]
        found = part(P, 2, NT)
        absent = part(P, 2, NT)
        piece_max = part(P, 2, NT, H)
        both_max = part(P, NT, H)
        piece_d = part(P, 2, NT, H)
        piece_e = part(P, 2, NT, H)
        piece_f = part(P, 2, NT, H)
        agg_a = part(P, NT, SUMS)
        agg_b = part(P, NT, SUMS)
        agg = part(P, NT, SUMS)
        den = part(P, NT, H)
        rden = part(P, NT, H)
        x1 = part(P, NT, C)
        ff_g = part(P, 2, 384)
        ff_t = part(P, 2, 192)
        ff_s = part(P, NT, M0)
        ff_v = part(P, NT, 192)
        y_sum = part(P, NT, C)
        y_out = [part(P, NT, C) for q in (0, 1)]
        es_in = [part(P, G, 64, reset=(q == 0)) for q in (0, 1)]
        got_s = [part(P, G, C) for q in (0, 1)]
        got_d = [part(P, G, C) for q in (0, 1)]
        dst_row = [part(P, G, P, dt=I32) for q in (0, 1)]
        dst_th = [part(G * H, P, dt=I32) for q in (0, 1)]
        idx = [part(P, 2 * G, dt=I32) for q in (0, 1)]
        dst_col = [part(P, G) for q in (0, 1)]
        rhat = [part(P, G, RDIR) for q in (0, 1)]
        es_t = part(128, 4, P)
        mlp_sq = part(P, G, 64)
        mlp_ss = part(P, G)
        mlp_var = part(P, G)
        mlp_rstd = part(P, G)
        mlp_n = part(P, G, 64)
        mlp_tanh = part(128, 4, P)
        mlp_y = part(128, 4, P)
        h1_t = part(128, 4, P)
        h2_t = [part(128, 4, P) for q in (0, 1)]
        feat = part(P, 2, C + C1)
        dot_in = part(P, 2, CV)
        prod_u = part(P, 2, CV)
        prod = [part(P, 2, PROD) for q in (0, 1)]
        prod_t = [part(128, 4, P) for q in (0, 1)]
        att_tanh = [part(P, 2, 64) for q in (0, 1)]
        att_u = part(P, 2, 64)
        msg = [part(P, G, MSG) for q in (0, 1)]
        logit = [part(P, G, H) for q in (0, 1)]
        run_ne = part(G * H, P)
        run_mask = part(G * H, P + 1)
        run_fwd = part(G * H, P)
        run_max = part(G * H, P)
        logit_d = part(P, G, H)
        prob = [part(P, G, H) for q in (0, 1)]
        prob_r = [part(P, G, 3, H) for q in (0, 1)]
        eq = [part(P, 2, P) for q in (0, 1)]
        pay = [part(P, 2, PAY) for q in (0, 1)]
        run_rows = [part(P, G, ROW) for q in (0, 1)]
        HALF = 88
        last = part(100, K, ROW, reset=True)
        last_max = part(100, K, HALF)
        chan = part(HALF, 2, TILES)
        chan_m = part(HALF, TILES)
        chan_d = part(HALF, TILES)
        same = part(HALF, TILES)
        restart = part(HALF, TILES)
        scan_m = part(HALF, TILES)
        step_m = part(HALF, TILES)
        keep = part(HALF, TILES)
        take = part(HALF, TILES)
        chan_x = part(HALF, 2, TILES)
        scan_x = part(HALF, 2, TILES)
        carry_rows = part(100, K, ROW)
        sentinel = part(1, ROW)

        ps = [ctx.enter_context(nc.psum_tensor(f"ps{i}", [128, 512], F32)) for i in range(8)]
        PM = ps[0]
        PR, PW, PT, PL, PO = ps[1], ps[2], (ps[3], ps[4]), (ps[5], ps[6]), ps[7]
        run_t = PR[0:G * H, 0:P]
        run_b = PR[0:P, 128:128 + G * H]

        x_v = inp["x"].rearrange("(g t p) c -> g p t c", t=NT, p=P)
        a0_v = inp["node_vec1"].rearrange("(g t p) c -> g p t c", t=NT, p=P)
        out_v = out.rearrange("(g t p) c -> g p t c", t=NT, p=P)
        src_v = src_table.rearrange("(g t p) c -> g p t c", t=NT, p=P)
        dst_v = dst_table.rearrange("(g t p) c -> g p t c", t=NT, p=P)
        es_v = inp["edge_attr_64"].rearrange("(g t p) c -> g p t c", t=G, p=P)
        dst_row_v = inp["dst"].rearrange("(g x e) -> g x e", x=1, e=G * P)
        dst_th_v = inp["dst"].rearrange("(g t x e) -> g t x e", t=G, x=1, e=P)
        dst_tiles = inp["dst"].rearrange("(t e) -> t e", e=P)
        runs_v = runs.rearrange("(g t p) c -> g p t c", t=G, p=P)
        last_v = runs.rearrange("(a k p) c -> p a k c", k=K, p=P)

        def W(name):
            return inp["L0_gnn_" + name]

        S = {}
        for name in (
            "zeroed", "weights_loaded", "weight_step", "bias_moved", "consts_made", "nat_loaded", "nat_cast",
            "cols_turned", "cols_kept", "vec_step", "vec_root", "vec_unit", "count_step", "place_step", "search_ready",
            "search_loaded_0", "search_loaded_1",
            "x_loaded_0", "x_loaded_1", "norm_step", "x_var_ready", "x_rstd_ready", "x_norm_ready", "node_turned",
            "affine_ready", "node_projected", "table_ready", "stored_0", "stored_1",
            "es_loaded_0", "es_loaded_1", "meta_loaded_0", "meta_loaded_1", "gathered_0", "gathered_1",
            "idx_ready", "rhat_ready", "es_turned", "es_copied", "mlp_out", "mlp_squared", "mlp_ss_ready",
            "mlp_var_ready", "mlp_rstd_ready", "mlp_n_ready", "mlp_turned", "mlp_act_ready", "mlp_h_ready",
            "edge_consts", "sum_ready", "dots_in", "dots_ready", "w_ready", "cross_in", "prods_ready", "prods_turned",
            "prods_copied", "lin_ready", "att_tanh_ready", "msg_ready", "att_u_ready", "logits_ready",
            "cols_ready", "run_ne_ready", "mask_ready", "logits_turned", "fwd_ready", "max_ready", "max_turned",
            "max_kept", "logit_d_ready", "prob_ready", "prob_r_ready", "eq_ready", "pay_ready", "sums_ready",
            "rows_ready", "rows_stored_0", "rows_stored_1",
            "last_loaded", "last_spread", "last_turned", "last_copied", "carry_step", "carry_exp_in", "carry_exp", "carry_done",
            "carry_turned", "carry_rows_ready", "carry_stored",
            "place_ready", "pieces_loaded_0", "pieces_loaded_1", "nodes_loaded_0", "nodes_loaded_1", "last_step", "merge_in", "merge_exp", "agg_ready",
            "tile_turned", "tile_copied", "projected", "x1_ready", "f1_ready", "ff_scaled", "ff_tanh",
            "ff_ready", "f2_ready", "x2_ready", "x2_norm_ready", "y_var_ready", "y_rstd_ready", "y_ready",
            "out_stored_0", "out_stored_1", "waits_passed",
            "prologue_over", "node_pass_over", "edge_pass_over", "carry_over",
        ):
            S[name] = sem(name)

        def done(h, q, lag, n, k, back=0):
            return h * (2 * n) + ((q - lag) * n + k + 1 - back)

        def turn(h, q, lag, n=16):
            return h * n + ((q - lag) // 2 + 1) * n

        def wait(eng, name, count):
            if isinstance(count, int) and count <= 0:
                return
            eng.wait_ge(S[name], count)

        def alone(eng, name, count):
            wait(eng, name, count)
            if not isinstance(count, int):
                eng.sem_inc(S["waits_passed"])

        def steps(eng, body):
            for s in range(PEEL):
                body(s // 2, s % 2, lambda lag, s=s: 0 <= s - lag < GROUPS)
            with eng.Fori(PEEL // 2, LOOP_END // 2) as h:
                for q in (0, 1):
                    body(h, q, lambda lag: True)
            for s in range(LOOP_END, STEPS):
                body(s // 2, s % 2, lambda lag, s=s: 0 <= s - lag < GROUPS)

        def node_groups(eng, body):
            for q in (0, 1):
                body(0, q, True)
            with eng.Fori(1, NODE_GROUPS // 2 - 1) as h:
                for q in (0, 1):
                    body(h, q, True)
            for q in (0, 1):
                body(NODE_GROUPS // 2 - 1, q, q == 0)

        def behind(j, lag):
            return 1 - (j - lag) // G, (j - lag) % G

        def barrier(eng, name):
            eng.drain().then_inc(S[name], 1)
            eng.wait_ge(S[name], 5)

        def one(g):
            return bass.ds(g, 1)

        loads = [0]
        ZERO_TILES = (w_mlp[:, :, :], w3_raw, w_node_v[:, :], w_lin[:, :], w_rest[:, :, :], w_proj_v[:, :], w_f1_v[:, :], w_f2_v[:, :, :], bias_row)
        ZEROED = len(ZERO_TILES) + 1

        block = ctx.enter_context(nc.Block())

        @block.sync
        def _(sp):
            def load(dst, src):
                sp.dma_start(dst, src, allow_slow_non_contiguous=True).then_inc(S["weights_loaded"], 16)
                loads[0] += 1

            def row(name):
                return W(name).unsqueeze(0)

            sp.dma_start(nat_i[:, 0], inp["src"].rearrange("(a k e) -> a k e", k=K, e=P)).then_inc(S["nat_loaded"], 16)
            sp.dma_start(nat_i[:, 1], inp["dst"].rearrange("(a k e) -> a k e", k=K, e=P)).then_inc(S["nat_loaded"], 16)
            sp.dma_start(nat_v, inp["edge_attr_3"].rearrange("(a k e) c -> a k e c", k=K, e=P)).then_inc(
                S["nat_loaded"], 16)
            sp.wait_ge(S["zeroed"], ZEROED)
            for w, b, v, dst in (("ln1_w0", "ln1_b0", "ln1_w1", ln1), ("ln2_w0", "ln2_b0", "ln2_w1", ln2)):
                load(dst[0:C0, 0:1], W(w).unsqueeze(1))
                load(dst[0:C0, 1:2], W(b).unsqueeze(1))
                for d in range(3):
                    load(dst[C1 * d:C1 * (d + 1), 2:3], W(v).unsqueeze(1))
            load(w_node_s[:, 0:64], W("msrc_ws"))
            load(w_node_s[:, 64:128], W("mdst_ws"))
            for d in range(3):
                rows = slice(C1 * d, C1 * (d + 1))
                load(w_node_v[rows, C1 * d:C1 * (d + 1)], W("msrc_wv"))
                load(w_node_v[rows, CV + C1 * d:CV + C1 * (d + 1)], W("mdst_wv"))
                load(w_f1_v[rows, M1 * d:M1 * (d + 1)], W("f1_wv"))
                for k in range(4):
                    load(w_proj_v[C1 * d + 8 * k:C1 * d + 8 * k + 8, C1 * d:C1 * (d + 1)],
                         W("proj_wv").rearrange("(h k) n -> k h n", k=4)[k])
            for k in range(8):
                load(w_proj_s[8 * k:8 * k + 8, :], W("proj_ws").rearrange("(h k) n -> k h n", k=8)[k])
            for half in (0, 1):
                rows = slice(64 * half, 64 * half + 64)
                load(w_mlp[rows, 0, rows], W("rw1"))
                load(w_mlp[rows, 1, rows], W("rw2"))
                for c, v in enumerate(("rg1", "rbe1", "rg2", "rbe2")):
                    load(mlp_affine[rows, c:c + 1], W(v).unsqueeze(1))
                for at, lo, hi in W_ORDER:
                    load(w3_raw[rows, W_TILE * half + at:W_TILE * half + at + hi - lo], W("rw3")[:, lo:hi])
            load(lin_raw[0:CV], W("lin_ws"))
            load(adot, W("alpha_dot").rearrange("(x h) k -> x (h k)", x=1).broadcast_to([CV + 1, 64]))
            for at, lo, hi, _, _ in REST_BLOCKS:
                load(raw_rest[at % 128:at % 128 + hi - lo, at // 128], W("lin_wv")[lo:hi, :])
            load(lin_raw[CV:CV + 1, :], row("lin_bs"))
            load(bias_row[:, B_NODE + C:B_NODE + C + 64], row("mdst_bs"))
            for t in range(G):
                load(bias_row[:, B_MLP1 + 64 * t:B_MLP1 + 64 * t + 64], row("rb1"))
                load(bias_row[:, B_MLP2 + 64 * t:B_MLP2 + 64 * t + 64], row("rb2"))
            for t in range(2):
                for at, lo, hi in W_ORDER:
                    load(bias_row[:, B_W + W_TILE * t + at:B_W + W_TILE * t + at + hi - lo], row("roff")[:, lo:hi])
            load(bias_row[:, B_PROJ:B_PROJ + 64], row("proj_bs"))
            load(bias_row[:, B_F1:B_F1 + 192], row("f1_bs"))
            load(bias_row[:, B_F2:B_F2 + 64], row("f2_bs"))
            load(w_f1_s[:, :], W("f1_ws"))
            load(w_f2_s[:, :], W("f2_ws"))
            load(w_f2_v[0:64, 0, 0:32], W("f2_wv"))
            load(w_f2_v[64:96, 0, 32:64], W("f2_wv")[0:32, :])
            load(w_f2_v[0:32, 1, 32:64], W("f2_wv")[32:64, :])
            load(w_f2_v[32:96, 1, 64:96], W("f2_wv"))
            assert loads[0] == LOADS, loads[0]
            sp.wait_ge(S["weight_step"], WEIGHT_STEPS)
            for k in range(3):
                sp.dma_start(bias3[k:k + 1, :], bias_parts[0:1, k, :]).then_inc(S["bias_moved"], 16)
            sp.wait_ge(S["bias_moved"], 48)
            barrier(sp, "prologue_over")

            sp.dma_start(x_in[0], x_v[0]).then_inc(S["x_loaded_0"], 16)

            def node_step(h, q, more):
                if more:
                    alone(sp, "x_norm_ready", done(h, q, 1, 1, 0))
                    sp.dma_start(x_in[1 - q], x_v[h * 2 + (q + 1)]).then_inc(S[f"x_loaded_{1 - q}"], 16)
                alone(sp, "table_ready", done(h, q, 0, NT, NT - 1))
                sp.dma_start(src_v[h * 2 + q], table[q][:, :, 0:C]).then_inc(S[f"stored_{q}"], 16)
                sp.dma_start(dst_v[h * 2 + q], table[q][:, :, C:2 * C]).then_inc(S[f"stored_{q}"], 16)

            node_groups(sp, node_step)
            for q in (0, 1):
                sp.wait_ge(S[f"stored_{q}"], 32 * (NODE_GROUPS // 2))
            barrier(sp, "node_pass_over")

            sp.dma_start(es_in[0], es_v[0]).then_inc(S["es_loaded_0"], 16)

            def step(h, q, live):
                if live(-1):
                    alone(sp, "es_turned", done(h, q, 1, 1, 0))
                    sp.dma_start(es_in[1 - q], es_v[h * 2 + (q + 1)]).then_inc(S[f"es_loaded_{1 - q}"], 16)
                if live(4):
                    alone(sp, "rows_ready", done(h, q, 4, G // 2, G // 2 - 1))
                    alone(sp, "max_kept", done(h, q, 4, 2, 1))
                    sp.dma_start(runs_v[h * 2 + (q - 4)], run_rows[q]).then_inc(S[f"rows_stored_{q}"], 16)
                if live(1):
                    alone(sp, "run_ne_ready", done(h, q, 3, 1, 0))
                    alone(sp, "eq_ready", done(h, q, 3, G // 2, G // 2 - 1))
                    sp.dma_start(dst_row[1 - q], dst_row_v[h * 2 + (q - 1)].broadcast_to([P, G * P])
                                 .rearrange("p (t e) -> p t e", t=G)).then_inc(S[f"meta_loaded_{1 - q}"], 16)
                    sp.dma_start(dst_th[1 - q], dst_th_v[h * 2 + (q - 1)].broadcast_to([G, H, P])).then_inc(
                        S[f"meta_loaded_{1 - q}"], 16)

            steps(sp, step)
            for q in (0, 1):
                sp.wait_ge(S[f"rows_stored_{q}"], 16 * (GROUPS // 2))
            barrier(sp, "edge_pass_over")

            sp.dma_start(last, last_v[P - 1]).then_inc(S["last_loaded"], 16)
            sp.wait_ge(S["carry_rows_ready"], CARRY_ROWS)
            sp.dma_start(carry[1:TILES + 1, :].rearrange("(a k) c -> a k c", k=K), carry_rows).then_inc(
                S["carry_stored"], 16)
            sp.dma_start(carry[0:1, :], sentinel).then_inc(S["carry_stored"], 16)
            sp.wait_ge(S["carry_stored"], 32)
            barrier(sp, "carry_over")

            def load_nodes(h, q, ahead):
                g = h * 2 + (q + ahead)
                r = (q + ahead) % 2
                sp.dma_start(x_in[r], x_v[g]).then_inc(S[f"nodes_loaded_{r}"], 16)
                sp.dma_start(a0[r].unsqueeze(2), a0_v[g], allow_slow_non_contiguous=True).then_inc(
                    S[f"nodes_loaded_{r}"], 16)

            load_nodes(0, 0, 0)

            def last_pass(h, q, more):
                if more:
                    alone(sp, "y_ready", done(h, q, 1, 1, 0))
                    load_nodes(h, q, 1)
                alone(sp, "y_ready", done(h, q, 0, 1, 0))
                sp.dma_start(out_v[h * 2 + q], y_out[q]).then_inc(S[f"out_stored_{q}"], 16)

            node_groups(sp, last_pass)
            for q in (0, 1):
                sp.wait_ge(S[f"out_stored_{q}"], 16 * (NODE_GROUPS // 2))

        @block.gpsimd
        def _(pool):
            nc.gpsimd.memset(ident[:, :], 0.0).then_inc(S["consts_made"], 1)
            nc.gpsimd.memset(minus_half[:, :], -0.5).then_inc(S["consts_made"], 1)
            nc.gpsimd.iota(node_i, pattern=[[P, NODE_TILES]], base=0, channel_multiplier=1).then_inc(
                S["consts_made"], 1)
            pool.wait_ge(S["consts_made"], 3)
            nc.gpsimd.affine_select(out=ident[:, :], in_=ident[:, :], compare_op=ALU.not_equal, fill=1.0, base=0,
                                    pattern=[[-1, 128]], channel_multiplier=1).then_inc(S["consts_made"], 1)
            def fetch_dst(h, q, more):
                alone(pool, "search_ready", done(h, q, 0, 1, 0))
                for t in range(NT):
                    nc.gpsimd.indirect_dma_start(
                        out=search_dst[q][:, t], out_offset=None, in_=dst_tiles,
                        in_offset=bass.IndirectOffsetOnAxis(ap=search_tile_i[q][:, t:t + 1], axis=0),
                    ).then_inc(S[f"search_loaded_{q}"], 16)

            node_groups(pool, fetch_dst)
            for q in (0, 1):
                pool.wait_ge(S[f"search_loaded_{q}"], 16 * NT * (NODE_GROUPS // 2))
            barrier(pool, "prologue_over")

            def rstd(name, count, n, ready):
                alone(pool, name, count)
                nc.gpsimd.tensor_tensor(
                    x_rstd.rearrange("p a b -> p (a b)")[:, 0:n], x_var.rearrange("p a b -> p (a b)")[:, 0:n],
                    minus_half[:, 0:n], ALU.pow).then_inc(S[ready], 1)

            node_groups(pool, lambda h, q, more: rstd("x_var_ready", done(h, q, 0, 1, 0), 2 * NT, "x_rstd_ready"))
            barrier(pool, "node_pass_over")

            def step(h, q, live):
                if not live(0):
                    return
                alone(pool, "idx_ready", done(h, q, 0, 1, 0))
                alone(pool, "sum_ready", done(h, q, 2, G // 2, G // 2 - 1))
                for j in range(G):
                    for at, table_, got in ((0, src_table, got_s), (G, dst_table, got_d)):
                        nc.gpsimd.indirect_dma_start(
                            out=got[q][:, j], out_offset=None, in_=table_,
                            in_offset=bass.IndirectOffsetOnAxis(ap=idx[q][:, at + j:at + j + 1], axis=0),
                        ).then_inc(S[f"gathered_{q}"], 16)
                    if j in (1, 5):
                        alone(pool, "mlp_var_ready", done(h, q, 0, 2, j // 4))
                        nc.gpsimd.tensor_tensor(mlp_rstd, mlp_var, minus_half[:, 0:G], ALU.pow).then_inc(
                            S["mlp_rstd_ready"], 1)

            steps(pool, step)
            for q in (0, 1):
                pool.wait_ge(S[f"gathered_{q}"], 16 * 2 * G * (GROUPS // 2))
            barrier(pool, "edge_pass_over")
            barrier(pool, "carry_over")

            def fetch(h, q, ahead):
                r = (q + ahead) % 2
                alone(pool, "place_ready", done(h, q + ahead, 0, 3, 2))
                for t in range(NT):
                    for k, rows in enumerate((runs, carry)):
                        nc.gpsimd.indirect_dma_start(
                            out=pieces[r][:, k, t], out_offset=None, in_=rows,
                            in_offset=bass.IndirectOffsetOnAxis(ap=place[r][:, k, t:t + 1], axis=0),
                        ).then_inc(S[f"pieces_loaded_{r}"], 16)

            fetch(0, 0, 0)

            def last_pass(h, q, more):
                if more:
                    fetch(h, q, 1)
                rstd("y_var_ready", done(h, q, 0, 2, 0), 2 * NT, "y_rstd_ready")
                rstd("y_var_ready", done(h, q, 0, 2, 1), NT, "y_rstd_ready")

            node_groups(pool, last_pass)
            for q in (0, 1):
                pool.wait_ge(S[f"pieces_loaded_{q}"], PIECES * (NODE_GROUPS // 2))

        @block.scalar
        def _(act):
            act.wait_ge(S["vec_step"], 3)
            nc.scalar.activation(vec_root, vec_n2, ACT.Sqrt).then_inc(S["vec_root"], 1)
            barrier(act, "prologue_over")

            def affine(u, w, count):
                wait(act, "node_turned" if w is ln1 else "tile_turned", count)
                nc.scalar.activation(tile_s[0:C0, u], PT[u][0:C0, 0:P], ACT.Identity, bias=w[0:C0, 1:2],
                                     scale=w[0:C0, 0:1]).then_inc(S["affine_ready" if w is ln1 else "tile_copied"], 1)
                nc.scalar.activation(tile_v[0:CV, u, 0], PT[u][0:CV, P:2 * P], ACT.Copy,
                                     scale=w[0:CV, 2:3]).then_inc(S["affine_ready" if w is ln1 else "tile_copied"], 1)

            def node_step(h, q, more):
                for t in range(NT + 1):
                    if t < NT:
                        wait(act, "node_projected", done(h, q, 0, NT, t, back=2))
                        affine((q * NT + t) % 2, ln1, done(h, q, 0, NT, t))
                    if t == 1:
                        wait(act, f"stored_{q}", turn(h, q, 2, 32))
                    if t > 0:
                        wait(act, "node_projected", done(h, q, 0, NT, t - 1))
                        nc.scalar.copy(table[q][:, t - 1], PL[(q * NT + t - 1) % 2][0:P, 0:2 * C]).then_inc(
                            S["table_ready"], 1)

            node_groups(act, node_step)
            barrier(act, "node_pass_over")

            def step(h, q, live):
                for j in range(G):
                    if live(0) and j == 0:
                        wait(act, "mlp_out", done(h, q, 1, 2, 0))
                        wait(act, "es_turned", done(h, q, 0, 1, 0))
                        nc.scalar.copy(es_t, PM[:, 0:4 * P].rearrange("p (a e) -> p a e", a=4)).then_inc(
                            S["es_copied"], 1)
                    if live(0) and j in (1, 4):
                        wait(act, "mlp_ss_ready", done(h, q, 0, 2, j // 4, back=1))
                        wait(act, "mlp_out", done(h, q, 0, 2, j // 4))
                        nc.scalar.activation(mlp_sq, PM[0:P, :].rearrange("p (t c) -> p t c", t=G),
                                             ACT.Square).then_inc(S["mlp_squared"], 1)
                    if live(0) and j == 3:
                        k = j // 6
                        wait(act, "mlp_h_ready", done(h, q, 0, 2, k, back=1))
                        wait(act, "mlp_turned", done(h, q, 0, 2, k))
                        turned = PM[:, 0:4 * P].rearrange("p (a e) -> p a e", a=4)
                        nc.scalar.activation(mlp_tanh, turned, ACT.Tanh, bias=mlp_affine[:, 5 + 2 * k:6 + 2 * k],
                                             scale=mlp_affine[:, 4 + 2 * k:5 + 2 * k]).then_inc(S["mlp_act_ready"], 1)
                        nc.scalar.activation(mlp_y, turned, ACT.Identity, bias=mlp_affine[:, 1 + 2 * k:2 + 2 * k],
                                             scale=mlp_affine[:, 2 * k:1 + 2 * k]).then_inc(S["mlp_act_ready"], 1)
                    lag, k = behind(j, LAG_SUM)
                    if live(lag) and k % 2 == 1:
                        r = (q - lag) % 2
                        if k == 1:
                            wait(act, f"rows_stored_{r}", turn(h, q, lag + 2))
                        wait(act, "sums_ready", done(h, q, lag, G, k))
                        nc.scalar.copy(run_rows[r][:, k - 1:k + 1, 0:SUMS],
                                       PO[0:P, 0:2 * SUMS].rearrange("p (t c) -> p t c", t=2)).then_inc(
                            S["rows_ready"], 1)
                    lag, k = behind(j, LAG_T)
                    if live(lag):
                        wait(act, "lin_ready", done(h, q, lag, G, k, back=2))
                        wait(act, "prods_turned", done(h, q, lag, G, k))
                        nc.scalar.copy(prod_t[k % 2], PT[k % 2][:, 0:4 * P].rearrange("p (a e) -> p a e", a=4)
                                       ).then_inc(S["prods_copied"], 1)
                    if live(0) and j == 6:
                        k = j // 6
                        wait(act, "mlp_h_ready", done(h, q, 0, 2, k, back=1))
                        wait(act, "mlp_turned", done(h, q, 0, 2, k))
                        turned = PM[:, 0:4 * P].rearrange("p (a e) -> p a e", a=4)
                        nc.scalar.activation(mlp_tanh, turned, ACT.Tanh, bias=mlp_affine[:, 5 + 2 * k:6 + 2 * k],
                                             scale=mlp_affine[:, 4 + 2 * k:5 + 2 * k]).then_inc(S["mlp_act_ready"], 1)
                        nc.scalar.activation(mlp_y, turned, ACT.Identity, bias=mlp_affine[:, 1 + 2 * k:2 + 2 * k],
                                             scale=mlp_affine[:, 2 * k:1 + 2 * k]).then_inc(S["mlp_act_ready"], 1)
                    lag, k = behind(j, LAG_LIN)
                    if live(lag):
                        wait(act, "att_u_ready", done(h, q, lag, G // 2, k // 2, back=2))
                        wait(act, "lin_ready", done(h, q, lag, G, k))
                        nc.scalar.activation(att_tanh[k // 2 % 2][:, k % 2], PL[k % 2][0:P, 0:64], ACT.Tanh, scale=0.5).then_inc(
                            S["att_tanh_ready"], 1)
                        wait(act, "pay_ready", done(h, q, lag + 2, G, 2 * (k // 2) + 1))
                        nc.scalar.copy(msg[(q - lag) % 2][:, k], PL[k % 2][0:P, 64:LIN]).then_inc(S["msg_ready"], 1)
                    if live(2) and j == 6:
                        wait(act, "pay_ready", done(h, q, 4, G, G - 1))
                        wait(act, "logit_d_ready", done(h, q, 2, 1, 0))
                        nc.scalar.activation(prob[q], logit_d, ACT.Exp).then_inc(S["prob_ready"], 1)

            steps(act, step)
            barrier(act, "edge_pass_over")

            act.wait_ge(S["carry_exp_in"], 2)
            nc.scalar.activation(keep, step_m, ACT.Exp).then_inc(S["carry_exp"], 1)
            nc.scalar.activation(take, chan_d, ACT.Exp).then_inc(S["carry_exp"], 1)
            barrier(act, "carry_over")

            def last_pass(h, q, more):
                wait(act, "merge_in", done(h, q, 0, 1, 0))
                nc.scalar.activation(piece_e, piece_d, ACT.Exp).then_inc(S["merge_exp"], 1)
                for t in range(NT):
                    u = (q * NT + t) % 2
                    wait(act, "tile_turned", done(h, q, 0, 3 * NT, t))
                    wait(act, "projected", done(h, q, 0, NT, t, back=2) if t >= 2 else 0)
                    nc.scalar.copy(tile_s[0:C0, u], PT[u][0:C0, 0:P]).then_inc(S["tile_copied"], 1)
                    nc.scalar.copy(tile_v[0:CV, u, 0], PT[u][0:CV, P:2 * P]).then_inc(S["tile_copied"], 1)
                for t in range(NT):
                    u = (q * NT + t) % 2
                    wait(act, "f1_ready", done(h, q, 0, NT, t, back=2) if t >= 2 else 0)
                    affine(u, ln2, done(h, q, 0, 3 * NT, NT + t))
                    wait(act, "ff_scaled", done(h, q, 0, NT, t))
                    wait(act, "ff_ready", done(h, q, 0, 2 * NT, 2 * t + 1, back=4))
                    nc.scalar.activation(ff_t[:, u], ff_g[:, u, 0:192], ACT.Tanh, scale=0.5).then_inc(S["ff_tanh"], 1)
                for t in range(NT):
                    u = (q * NT + t) % 2
                    wait(act, "tile_turned", done(h, q, 0, 3 * NT, 2 * NT + t))
                    wait(act, "f2_ready", done(h, q, 0, NT, t, back=2) if t >= 2 else 0)
                    nc.scalar.copy(tile_s[:, u], PT[u][:, 0:P]).then_inc(S["tile_copied"], 1)
                    nc.scalar.copy(tile_v[0:CV, u], PT[u][0:CV, P:3 * P].rearrange("p (a e) -> p a e", a=2)).then_inc(
                        S["tile_copied"], 1)

            node_groups(act, last_pass)

        @block.tensor
        def _(pe):
            def mm(o, lhs_t, rhs, start=False, stop=False):
                return nc.tensor.matmul(o, lhs_t, rhs, start=start, stop=stop)

            def turn_tile(o, i, n):
                return nc.tensor.transpose(o, i, ident[0:n, 0:n])

            def bias(o, at, n, stop=False):
                return mm(o, ones3[:, 0:P], bias3[:, at:at + n], start=True, stop=stop)

            pe.wait_ge(S["consts_made"], 4)
            pe.wait_ge(S["nat_cast"], 2)
            for c in range(6):
                for b in range(4):
                    k = (c % 2) * 4 + b
                    nat = nat_f[:, c // 2, k] if c < 4 else spread(nat_f[:, 1, k, 0:1], 2, P)[:, 0, :]
                    turned = turn_tile(ps[c][0:P, 100 * b:100 * b + 100], nat, 100)
                turned.then_inc(S["cols_turned"], 1)
            pe.wait_ge(S["nat_loaded"], 48)
            for c in range(6):
                bank = ps[(6 + c) % 8]
                if c >= 2:
                    pe.wait_ge(S["cols_kept"], (1, 2, 5, 6)[c - 2])
                for b in range(4):
                    turned = turn_tile(bank[0:P, 100 * b:100 * b + 100], nat_v[:, (c % 2) * 4 + b, :, c // 2], 100)
                turned.then_inc(S["cols_turned"], 1)
            pe.wait_ge(S["bias_moved"], 48)
            pe.wait_ge(S["weight_step"], WEIGHT_STEPS)
            barrier(pe, "prologue_over")

            def node_step(h, q, more):
                for t in range(NT + 1):
                    if t < NT:
                        u = (q * NT + t) % 2
                        if t == 0:
                            wait(pe, "x_norm_ready", done(h, q, 0, 1, 0))
                        turn_tile(PT[u][0:CV, P:2 * P], x_norm[q][:, t, C0:C], P)
                        turn_tile(PT[u][0:C0, 0:P], x_norm[q][:, t, 0:C0], P).then_inc(S["node_turned"], 1)
                    if t > 0:
                        u = (q * NT + t - 1) % 2
                        wait(pe, "affine_ready", done(h, q, 0, 2 * NT, 2 * t - 1))
                        wait(pe, "table_ready", done(h, q, 0, NT, t - 1, back=2))
                        o = PL[u][0:P, :]
                        bias(o[:, 0:2 * C], B_NODE, 2 * C)
                        mm(o[:, 0:C0], tile_s[0:C0, u], w_node_s[:, 0:64])
                        mm(o[:, C:C + C0], tile_s[0:C0, u], w_node_s[:, 64:128])
                        mm(o[:, C0:C], tile_v[0:CV, u, 0], w_node_v[:, 0:CV])
                        mm(o[:, C + C0:2 * C], tile_v[0:CV, u, 0], w_node_v[:, CV:2 * CV], stop=True).then_inc(
                            S["node_projected"], 1)

            node_groups(pe, node_step)
            barrier(pe, "node_pass_over")

            def mlp(h, q, k, j):
                src = es_t if k == 0 else h1_t
                if k == 0:
                    wait(pe, "es_copied", done(h, q, 0, 1, 0))
                else:
                    wait(pe, "mlp_h_ready", done(h, q, 0, 2, 0))
                wait(pe, "mlp_n_ready", done(h, q, 0, 2, k, back=1))
                bias(PM[0:P, :], (B_MLP1, B_MLP2)[k], 64 * G)
                for a in range(G // 2):
                    last_mm = mm(PM[0:P, 128 * a:128 * a + 128], src[:, a], w_mlp[:, k], stop=a == G // 2 - 1)
                last_mm.then_inc(S["mlp_out"], 1)

            def step(h, q, live):
                for j in range(G):
                    if live(0) and j == 0:
                        wait(pe, "mlp_act_ready", done(h, q, 1, 4, 3))
                        wait(pe, f"es_loaded_{q}", turn(h, q, 0))
                        for a in range(4):
                            turned = turn_tile(PM[:, P * a:P * a + P],
                                               es_in[q][:, 2 * a:2 * a + 2].rearrange("p t c -> p (t c)"), P)
                        turned.then_inc(S["es_turned"], 1)
                    if live(0) and j == 1:
                        mlp(h, q, 0, j)
                    if live(0) and j == 3:
                        k = 0
                        wait(pe, "mlp_n_ready", done(h, q, 0, 2, k))
                        if k == 0:
                            wait(pe, "es_copied", done(h, q, 0, 1, 0))
                        else:
                            wait(pe, "mlp_act_ready", done(h, q, 0, 4, 1))
                        for a in range(4):
                            turned = turn_tile(PM[:, P * a:P * a + P],
                                               mlp_n[:, 2 * a:2 * a + 2].rearrange("p t c -> p (t c)"), P)
                        turned.then_inc(S["mlp_turned"], 1)
                    if live(1) and j % 2 == 0:
                        r = 1 - q
                        wait(pe, "prods_ready", done(h, q, 1, 2 * G, 2 * j - 1))
                        wait(pe, "mlp_h_ready", done(h, q, 1, 2, 1))
                        bias(PW[0:P, 0:2 * W_TILE], B_W, 2 * W_TILE)
                        last_mm = mm(PW[0:P, 0:2 * W_TILE], h2_t[r][:, j // 2], w3[:, :], stop=True)
                        last_mm.then_inc(S["w_ready"], 1)
                    if live(2) and j == 4:
                        wait(pe, "logits_ready", done(h, q, 2, G // 2, G // 2 - 1))
                        wait(pe, "logit_d_ready", done(h, q, 3, 1, 0))
                        alone(pe, "max_kept", done(h, q, 3, 2, 1))
                        turn_tile(run_t, logit[q].rearrange("p t h -> p (t h)"), P).then_inc(S["logits_turned"], 1)
                    if live(0) and j == 4:
                        mlp(h, q, 1, j)
                    lag, k = behind(j, LAG_SUM)
                    if live(lag):
                        u = k % 2
                        r = k // 2 % 2
                        wait(pe, "eq_ready", done(h, q, lag, G // 2, k // 2))
                        wait(pe, "pay_ready", done(h, q, lag, G, 2 * (k // 2) + 1))
                        if u == 0:
                            wait(pe, "rows_ready", done(h, q, lag, G // 2, k // 2 - 1))
                        o = PO[0:P, SUMS * u:SUMS * (u + 1)]
                        mm(o, eq[r][:, u], pay[r][:, u, 0:SUMS], start=True)
                        mm(o[:, SUMS - CV:SUMS], eq[r][:, u], pay[r][:, u, SUMS:PAY], stop=True).then_inc(
                            S["sums_ready"], 1)
                    lag, k = behind(j, LAG_T)
                    if live(lag):
                        wait(pe, "prods_ready", done(h, q, lag, 2 * G, 4 * (k // 2) + 3))
                        wait(pe, "prods_copied", done(h, q, lag, G, k, back=2))
                        for a in range(4):
                            turned = turn_tile(PT[k % 2][:, P * a:P * a + P],
                                               prod[(k // 2) % 2][:, k % 2, 128 * a:128 * a + 128], P)
                        turned.then_inc(S["prods_turned"], 1)
                    if live(0) and j == 6:
                        k = 1
                        wait(pe, "mlp_n_ready", done(h, q, 0, 2, k))
                        if k == 0:
                            wait(pe, "es_copied", done(h, q, 0, 1, 0))
                        else:
                            wait(pe, "mlp_act_ready", done(h, q, 0, 4, 1))
                        for a in range(4):
                            turned = turn_tile(PM[:, P * a:P * a + P],
                                               mlp_n[:, 2 * a:2 * a + 2].rearrange("p t c -> p (t c)"), P)
                        turned.then_inc(S["mlp_turned"], 1)
                    lag, k = behind(j, LAG_LIN)
                    if live(lag):
                        u = k % 2
                        wait(pe, "prods_copied", done(h, q, lag, G, k))
                        wait(pe, "msg_ready", done(h, q, lag, G, k, back=2))
                        o = PL[u][0:P, :]
                        mm(o[:, 0:LIN_S], prod_t[u][:, 0], w_lin[:, :], start=True)
                        mm(o[:, LIN_S:LIN], prod_t[u][:, 1], w_rest[:, 0])
                        mm(o[:, LIN_S:LIN], prod_t[u][:, 2], w_rest[:, 1])
                        mm(o[:, LIN_S:LIN], prod_t[u][:, 3], w_rest[:, 2], stop=True).then_inc(S["lin_ready"], 1)
                    if live(2) and j == 5:
                        alone(pe, "max_ready", done(h, q, 2, 1, 0))
                        turn_tile(run_b, run_max, G * H).then_inc(S["max_turned"], 1)

            steps(pe, step)
            barrier(pe, "edge_pass_over")

            pe.wait_ge(S["last_loaded"], 16)
            pe.wait_ge(S["last_spread"], 1)
            for b in range(K // 4):
                for k in range(4):
                    cols = slice(100 * k, 100 * k + 100)
                    rows = last[:, 4 * b + k]
                    turn_tile(ps[b][0:HALF, cols], rows[:, 0:HALF], 100)
                    turn_tile(ps[2 + b][0:SUMS - HALF, cols], rows[:, HALF:SUMS], 100)
                    turn_tile(ps[4 + b][0:HALF, cols], last_max[:, 4 * b + k], 100)
                    turned = turn_tile(ps[6 + b][0:HALF, cols], spread(rows[:, R_DST:R_DST + 1], 2, HALF)[:, 0, :], 100)
                turned.then_inc(S["last_turned"], 1)
            pe.wait_ge(S["carry_done"], 1)
            for k in range(K):
                o = ps[k]
                col = scan_x.rearrange("p x (a k) -> p x k a", k=K)[:, :, k]
                turn_tile(o[0:100, 0:HALF], col[:, 0], HALF)
                turn_tile(o[0:100, HALF:SUMS], col[0:SUMS - HALF, 1], SUMS - HALF)
                turn_tile(o[0:100, R_MAX:R_MAX + H], scan_m[0:H].rearrange("p (a k) -> p k a", k=K)[:, k], H).then_inc(S["carry_turned"], 1)
            barrier(pe, "carry_over")

            def last_pass(h, q, more):
                def rounds(turn_in, product):
                    for t in range(NT + 1):
                        if t < NT:
                            turn_in(t, (q * NT + t) % 2)
                        if t > 0:
                            product(t - 1, (q * NT + t - 1) % 2)

                def turn_agg(t, u):
                    if t == 0:
                        wait(pe, "agg_ready", done(h, q, 0, 1, 0))
                    wait(pe, "tile_copied", done(h, q, 0, 6 * NT, 2 * t - 1, back=2))
                    turn_tile(PT[u][0:CV, P:2 * P], agg[:, t, H + C0:SUMS], P)
                    turn_tile(PT[u][0:C0, 0:P], agg[:, t, H:H + C0], P).then_inc(S["tile_turned"], 1)

                def project(t, u):
                    wait(pe, "tile_copied", done(h, q, 0, 6 * NT, 2 * t + 1))
                    wait(pe, "x1_ready", done(h, q, 0, 2 * NT, 2 * t - 3) if t >= 2 else 0)
                    o = PL[u][0:P, :]
                    bias(o[:, 0:C], B_PROJ, C)
                    mm(o[:, 0:C0], tile_s[0:C0, u], w_proj_s[:, :])
                    mm(o[:, C0:C], tile_v[0:CV, u, 0], w_proj_v[:, :], stop=True).then_inc(S["projected"], 1)

                def turn_norm(t, u):
                    if t == 0:
                        wait(pe, "x1_ready", done(h, q, 0, 2 * NT, 2 * NT - 1))
                        wait(pe, "x2_norm_ready", done(h, q, 0, 1, 0))
                    wait(pe, "tile_copied", done(h, q, 0, 6 * NT, 2 * NT + 2 * t - 1, back=2))
                    turn_tile(PT[u][0:CV, P:2 * P], x_norm[0][:, t, C0:C], P)
                    turn_tile(PT[u][0:C0, 0:P], x_norm[0][:, t, 0:C0], P).then_inc(S["tile_turned"], 1)

                def f1(t, u):
                    wait(pe, "tile_copied", done(h, q, 0, 6 * NT, 2 * NT + 2 * t + 1))
                    wait(pe, "ff_scaled", done(h, q, 0, NT, t, back=2))
                    o = PL[u][0:P, :]
                    bias(o[:, 0:192], B_F1, 192)
                    mm(o[:, 0:192], tile_s[0:C0, u], w_f1_s[:, :], stop=True)
                    mm(o[:, 192:384], tile_v[0:CV, u, 0], w_f1_v[:, :], start=True, stop=True).then_inc(
                        S["f1_ready"], 1)

                def turn_ff(t, u):
                    wait(pe, "ff_ready", done(h, q, 0, 2 * NT, 2 * t + 1))
                    wait(pe, "tile_copied", done(h, q, 0, 6 * NT, 4 * NT + 2 * t - 1, back=2))
                    turn_tile(PT[u][:, 0:P], ff_s[:, t], P)
                    turn_tile(PT[u][0:CV, P:2 * P], ff_v[:, t, 0:CV], P)
                    turn_tile(PT[u][0:CV, 2 * P:3 * P], ff_v[:, t, CV:2 * CV], P).then_inc(S["tile_turned"], 1)

                def f2(t, u):
                    wait(pe, "tile_copied", done(h, q, 0, 6 * NT, 4 * NT + 2 * t + 1))
                    wait(pe, "x2_ready", done(h, q, 0, 2 * NT, 2 * t - 3) if t >= 2 else 0)
                    o = (PW, PO)[u][0:P, 0:C]
                    bias(o, B_F2, C)
                    mm(o[:, 0:C0], tile_s[:, u], w_f2_s[:, :])
                    mm(o[:, C0:C], tile_v[0:CV, u, 0], w_f2_v[:, 0])
                    mm(o[:, C0:C], tile_v[0:CV, u, 1], w_f2_v[:, 1], stop=True).then_inc(S["f2_ready"], 1)

                rounds(turn_agg, project)
                for t in range(NT + 2):
                    if t < NT:
                        turn_norm(t, (q * NT + t) % 2)
                    if 0 < t <= NT:
                        f1(t - 1, (q * NT + t - 1) % 2)
                rounds(turn_ff, f2)

            node_groups(pe, last_pass)

        @block.vector
        def _(dve):
            v = nc.vector

            def chain(name):
                count = [0]

                def link(ins):
                    count[0] += 1
                    ins.then_inc(S[name], 1)
                    dve.wait_ge(S[name], count[0])
                return link

            for tile_ in ZERO_TILES:
                v.memset(tile_, 0.0).then_inc(S["zeroed"], 1)
            v.memset(ones3[:, :], 1.0).then_inc(S["zeroed"], 1)
            dve.wait_ge(S["nat_loaded"], 48)
            v.tensor_copy(nat_f[:, 1], nat_i[:, 1]).then_inc(S["nat_cast"], 1)
            v.tensor_copy(nat_f[:, 0], nat_i[:, 0]).then_inc(S["nat_cast"], 1)

            def cols(bank):
                return bank[0:P, 0:400].rearrange("p (k a) -> p a k", k=4)

            for c in range(4):
                dve.wait_ge(S["cols_turned"], c + 1)
                at = c * 4
                last_ins = v.tensor_copy(idx_all[:, :, at:at + 4], cols(ps[c]))
                last_ins.then_inc(S["cols_kept"], 1)
            for c in (2, 3):
                v.tensor_copy(dst_all[:, :, 4 * (c - 2):4 * (c - 2) + 4], cols(ps[c])).then_inc(S["cols_kept"], 1)
            for c in (4, 5):
                dve.wait_ge(S["cols_turned"], c + 1)
                v.tensor_copy(first_dst[:, 400 * (c - 4):400 * (c - 4) + 400], ps[c][0:P, 0:400]).then_inc(
                    S["cols_kept"], 1)
            for c in range(6):
                dve.wait_ge(S["cols_turned"], 6 + c + 1)
                k = (c % 2) * 4
                v.tensor_copy(vec_all[:, :, k:k + 4, c // 2], cols(ps[(6 + c) % 8])).then_inc(S["cols_kept"], 1)

            dve.wait_ge(S["cols_kept"], 14)
            flat = vec_all.rearrange("p g t c -> p (g t) c")
            v.tensor_tensor(vec_sq, flat, flat, ALU.mult).then_inc(S["vec_step"], 1)
            dve.wait_ge(S["vec_step"], 1)
            v.tensor_reduce(vec_n2, vec_sq, AX.X, ALU.add).then_inc(S["vec_step"], 1)
            dve.wait_ge(S["vec_step"], 2)
            v.tensor_scalar(vec_n2, vec_n2, 1e-12, None, ALU.add).then_inc(S["vec_step"], 1)
            dve.wait_ge(S["consts_made"], 4)
            v.tensor_copy(node_all[:, :], node_i).then_inc(S["vec_step"], 1)
            dve.wait_ge(S["vec_step"], 4)
            dve.wait_ge(S["vec_root"], 1)
            unit = chain("vec_unit")
            unit(v.reciprocal(vec_inv, vec_root))
            unit(v.tensor_tensor(vec_root, vec_inv, vec_inv, ALU.mult))
            unit(v.tensor_tensor(vec_root, vec_root, vec_n2, ALU.mult))
            unit(v.tensor_scalar(vec_root, vec_root, -0.5, 1.5, ALU.mult, ALU.add))
            unit(v.tensor_tensor(vec_inv, vec_inv, vec_root, ALU.mult))
            rh = rhat_all[:, :, :, :].rearrange("p g t c -> p (g t) c")
            v.tensor_tensor(rh[:, :, 0:3], flat, spread(vec_inv, 2, 3), ALU.mult).then_inc(S["vec_step"], 1)
            dve.wait_ge(S["vec_step"], 5)
            v.tensor_copy(rh[:, :, 3:4], rh[:, :, 0:1]).then_inc(S["vec_step"], 1)
            v.tensor_scalar(rh[:, :, 4:5], rh[:, :, 2:3], -1.0, None, ALU.mult).then_inc(S["vec_step"], 1)
            v.tensor_scalar(rh[:, :, 5:7], rh[:, :, 0:2], -1.0, None, ALU.mult).then_inc(S["vec_step"], 1)
            dve.wait_ge(S["vec_step"], 8)

            def find_place(h, q, ahead):
                r = (q + ahead) % 2
                links = [0]

                def link(ins):
                    links[0] += 1
                    ins.then_inc(S["place_step"], 1)
                    wait(dve, "place_step", h * (2 * PLACE_STEPS) + ((q + ahead) * PLACE_STEPS + links[0]))

                wait(dve, f"search_loaded_{r}", turn(h, q, -ahead, 16 * NT))
                link(v.tensor_tensor(search_le, search_dst[r], spread(search_node[r], 2, P), ALU.is_le))
                link(v.tensor_reduce(search_in, search_le, AX.X, ALU.add))
                link(v.scalar_tensor_tensor(search_row, search_tile[r], float(P), search_in, ALU.mult, ALU.add))
                link(v.tensor_scalar(place_all[:, 0, bass.ds(h * (2 * NT) + (q + ahead) * NT, NT)], search_row, -1.0,
                                     0.0, ALU.add, ALU.max))
                assert links[0] == PLACE_STEPS, links[0]

            def search(h, q, more):
                links = [0]
                group = bass.ds(h * (2 * NT) + q * NT, NT)

                def link(ins):
                    links[0] += 1
                    ins.then_inc(S["count_step"], 1)
                    wait(dve, "count_step", h * (2 * COUNT_STEPS) + (q * COUNT_STEPS + links[0]))

                link(v.tensor_copy(search_node[q], node_all[:, group]))
                for t in range(NT):
                    link(v.tensor_scalar(search_junk, first_dst, search_node[q][:, t:t + 1], None, ALU.is_le, ALU.add,
                                         accum_out=search_cnt[:, t:t + 1]))
                link(v.tensor_scalar(search_tile[q], search_cnt, -1.0, 0.0, ALU.add, ALU.max))
                link(v.tensor_copy(place_all[:, 1, group], search_tile[q]))
                v.tensor_copy(search_tile_i[q], search_tile[q]).then_inc(S["search_ready"], 1)
                assert links[0] == COUNT_STEPS, links[0]
                if not isinstance(h, int) or 2 * h + q > 0:
                    find_place(h, q, -1)

            node_groups(dve, search)
            find_place(NODE_GROUPS // 2 - 1, 1, 0)

            dve.wait_ge(S["weights_loaded"], 16 * LOADS)
            link = chain("weight_step")
            link(v.tensor_reduce(mlp_mean, w_mlp[:, :, :], AX.X, ALU.add))
            link(v.tensor_scalar(mlp_mean, mlp_mean, 1.0 / 64, None, ALU.mult))
            for rows in (slice(0, 64), slice(64, 128)):
                link(v.tensor_tensor(w_mlp[rows, :, rows], w_mlp[rows, :, rows], spread(mlp_mean[rows], 2, 64),
                                     ALU.subtract))
            link(v.tensor_scalar(w_mlp[:, 1], w_mlp[:, 1], 0.5, None, ALU.mult))
            link(v.tensor_scalar(w3[:, :], w3_raw, 0.5, None, ALU.mult))
            link(v.tensor_scalar(w_f2_s[:, :], w_f2_s[:, :], 0.5, None, ALU.mult))
            link(v.tensor_scalar(w_f2_v[:, :, :], w_f2_v[:, :, :], 0.5, None, ALU.mult))
            link(v.tensor_scalar(mlp_affine[:, 4:8], mlp_affine[:, 0:4], 0.5, None, ALU.mult))
            mlp_bias = bias_row[:, B_MLP1:B_W].rearrange("p (l t c) -> p l t c", l=2, t=G)
            link(v.tensor_reduce(bias_mean, mlp_bias, AX.X, ALU.add))
            link(v.tensor_scalar(bias_mean, bias_mean, 1.0 / 64, None, ALU.mult))
            for l in (0, 1):
                link(v.tensor_tensor(mlp_bias[:, l], mlp_bias[:, l], spread(bias_mean[:, l], 2, 64), ALU.subtract))
            link(v.tensor_copy(w_lin[0:CV + 1, 0:64], lin_raw[:, 0:64]))
            link(v.scalar_tensor_tensor(w_lin[0:CV + 1, 64:128], lin_raw[:, 0:64], 0.4, adot, ALU.mult, ALU.mult))
            link(v.memset(w_lin[ONE:ONE + 1, 128:128 + H], 1.0))
            link(v.tensor_copy(w_lin[0:CV + 1, 128 + H:LIN_S].rearrange("p (k h) -> p k h", k=8),
                               lin_raw[:, 64:128].rearrange("p (h k) -> p k h", h=H)))
            for at, lo, hi, col, factor in REST_BLOCKS:
                rows = slice(at % 128, at % 128 + hi - lo)
                link(v.tensor_scalar(w_rest[rows, at // 128, col:col + C1].rearrange("p (k h) -> p k h", k=4),
                                     raw_rest[rows, at // 128].rearrange("p (h k) -> p k h", h=H),
                                     factor, None, ALU.mult))
            link(v.tensor_copy(bias_parts[:, 0], bias_row))
            link(v.tensor_tensor(bias_rest, bias_row, bias_parts[:, 0], ALU.subtract))
            link(v.tensor_copy(bias_parts[:, 1], bias_rest))
            link(v.tensor_tensor(bias_row, bias_rest, bias_parts[:, 1], ALU.subtract))
            link(v.tensor_copy(bias_parts[:, 2], bias_row))
            barrier(dve, "prologue_over")

            def by_component(ap):
                return ap.rearrange("p t (u d) -> p t d u", d=3)

            def normed(link, x, o, var_ready, count, rstd_ready, last_link):
                link(v.tensor_reduce(x_sum, x[:, :, 0:C0], AX.X, ALU.add))
                link(v.tensor_scalar(x_mean, x_sum, 1.0 / C0, None, ALU.mult))
                link(v.tensor_tensor(x_cen[:, :, 0:C0], x[:, :, 0:C0], spread(x_mean, 2, C0), ALU.subtract))
                link(v.tensor_tensor(x_sq[:, :, 0:C0], x_cen[:, :, 0:C0], x_cen[:, :, 0:C0], ALU.mult))
                link(v.tensor_tensor(x_sq[:, :, C0:C], x[:, :, C0:C], x[:, :, C0:C], ALU.mult))
                link(v.tensor_reduce(x_ss[:, 0], x_sq[:, :, 0:C0], AX.X, ALU.add))
                link(v.tensor_reduce(x_ss[:, 1], x_sq[:, :, C0:C], AX.X, ALU.add))
                link(v.tensor_scalar(x_var[:, 0], x_ss[:, 0], 1.0 / C0, EPS, ALU.mult, ALU.add))
                v.tensor_scalar(x_var[:, 1], x_ss[:, 1], 1.0 / CV, EPS, ALU.mult, ALU.add).then_inc(S[var_ready], 1)
                wait(dve, rstd_ready, count)
                link(v.tensor_tensor(o[:, :, 0:C0], x_cen[:, :, 0:C0], spread(x_rstd[:, 0], 2, C0), ALU.mult))
                last_link(v.tensor_tensor(o[:, :, C0:C].rearrange("p t (d u) -> p t d u", d=3),
                                          by_component(x[:, :, C0:C]),
                                          spread(spread(x_rstd[:, 1], 2, 3), 3, C1), ALU.mult))

            def node_step(h, q, more):
                links = [0]

                def link(ins):
                    links[0] += 1
                    ins.then_inc(S["norm_step"], 1)
                    dve.wait_ge(S["norm_step"], h * (2 * NORM_STEPS) + (q * NORM_STEPS + links[0]))

                wait(dve, f"x_loaded_{q}", turn(h, q, 0))
                wait(dve, "node_turned", done(h, q, 2, NT, NT - 1))
                normed(link, x_in[q], x_norm[q], "x_var_ready", done(h, q, 0, 1, 0), "x_rstd_ready",
                       lambda ins: ins.then_inc(S["x_norm_ready"], 1))
                assert links[0] == NORM_STEPS, links[0]

            node_groups(dve, node_step)
            barrier(dve, "node_pass_over")

            v.memset(run_mask, -BIG).then_inc(S["edge_consts"], 1)
            for q in (0, 1):
                v.memset(prod[q], 0.0).then_inc(S["edge_consts"], 1)
            for q in (0, 1):
                v.memset(run_rows[q], 0.0).then_inc(S["edge_consts"], 1)

            dve.wait_ge(S["edge_consts"], 5)
            for q in (0, 1):
                v.memset(prod[q][:, :, ONE:ONE + 1], 1.0).then_inc(S["edge_consts"], 1)
            dve.wait_ge(S["edge_consts"], 7)
            v.tensor_copy(idx[0], idx_all[:, 0, :]).then_inc(S["idx_ready"], 1)

            def step(h, q, live):
                for j in range(G):
                    p = j // 2
                    if j == 0 and live(1):
                        r = 1 - q
                        wait(dve, "prob_r_ready", done(h, q, 3, 1, 0))
                        wait(dve, "dots_in", done(h, q, 3, G // 2, G // 2 - 1))
                        wait(dve, "prods_ready", done(h, q, 3, 2 * G, 2 * G - 1))
                        v.tensor_copy(rhat[r], rhat_all[:, one(h * 2 + (q - 1))].rearrange(
                            "p x t c -> p (x t) c")).then_inc(S["rhat_ready"], 1)
                    ea = live(1)
                    r = 1 - q
                    pair = slice(2 * p, 2 * p + 2)
                    mv = feat[:, :, C0:C]
                    if ea and j % 2 == 0:
                        if p == 0:
                            wait(dve, f"gathered_{r}", turn(h, q, 1, 16 * 2 * G))
                        wait(dve, "prods_ready", done(h, q, 1, 2 * G, 4 * p - 1))
                        wait(dve, "dots_in", done(h, q, 1, G // 2, p - 1))
                        v.tensor_tensor(feat[:, :, 0:C], got_s[r][:, pair], got_d[r][:, pair], ALU.add).then_inc(
                            S["sum_ready"], 1)
                    plag, pk = behind(j, LAG_PAY)
                    pr, pu = (q - plag) % 2, pk // 2 % 2
                    paying = live(plag) and pk % 2 == 0
                    pays = slice(pk, pk + 2)
                    if paying:
                        if pk == 0:
                            wait(dve, f"meta_loaded_{pr}", turn(h, q, plag, 32))
                            wait(dve, "cols_ready", done(h, q, plag, 1, 0))
                        wait(dve, "sums_ready", done(h, q, plag, G, pk + 1, back=4))
                        v.tensor_tensor(eq[pu], dst_row[pr][:, pays], spread(dst_col[pr][:, pays], 2, P),
                                        ALU.is_equal).then_inc(S["eq_ready"], 1)
                    if ea and j % 2 == 0:
                        if p == 0:
                            wait(dve, "rhat_ready", done(h, q, 1, 1, 0))
                        wait(dve, "sum_ready", done(h, q, 1, G // 2, p))
                        wait(dve, "dots_ready", done(h, q, 1, G // 2, p - 1))
                        v.tensor_tensor(dot_in.rearrange("p t (d u) -> p t d u", d=3),
                                        mv.rearrange("p t (d u) -> p t d u", d=3),
                                        spread(rhat[r][:, pair, 0:3], 3, C1), ALU.mult).then_inc(S["dots_in"], 1)
                    if paying:
                        if pk == 0:
                            wait(dve, "prob_r_ready", done(h, q, plag, 1, 0))
                            wait(dve, "prob_ready", done(h, q, plag, 1, 0))
                        wait(dve, "msg_ready", done(h, q, plag, G, pk + 1))
                        v.tensor_tensor(pay[pu][:, :, 0:SUMS].rearrange("p t (k h) -> p t k h", h=H),
                                        msg[pr][:, pays, 64:64 + SUMS].rearrange("p t (k h) -> p t k h", h=H),
                                        spread(prob[pr][:, pays], 2, SUMS // H), ALU.mult).then_inc(S["pay_ready"], 1)
                    if ea and j % 2 == 0:
                        wait(dve, "dots_in", done(h, q, 1, G // 2, p))
                        v.tensor_reduce(feat[:, :, C:C + C1], dot_in.rearrange("p t (d u) -> p t u d", d=3), AX.X,
                                        ALU.add).then_inc(S["dots_ready"], 1)
                    if paying:
                        a = msg[pr][:, pays, 64 + SUMS:MSG].rearrange("p t (k h) -> p t k h", h=H)
                        v.tensor_tensor(pay[pu][:, :, SUMS:PAY].rearrange("p t (d k h) -> p t d k h", d=3, h=H),
                                        spread(a, 2, 3), spread(prob_r[pr][:, pays], 3, C1 // H),
                                        ALU.mult).then_inc(S["pay_ready"], 1)
                    if live(2) and j == 5:
                        wait(dve, "max_turned", done(h, q, 3, 1, 0))
                        wait(dve, "fwd_ready", done(h, q, 2, 1, 0))
                        v.tensor_tensor_scan(run_max[:, ::-1], run_mask[:, 1:P + 1][:, ::-1], run_fwd[:, ::-1], 0.0,
                                             ALU.add, ALU.max).then_inc(S["max_ready"], 1)
                    if ea and j % 2 == 1:
                        w = PW[0:P, 0:2 * W_TILE].rearrange("p (t c) -> p t c", t=2)
                        o = prod[p % 2]
                        by_d = mv.rearrange("p t (d u) -> p t d u", d=3)
                        wait(dve, "dots_ready", done(h, q, 1, G // 2, p))
                        wait(dve, "prods_turned", done(h, q, 1, G, 2 * p + 1, back=4))
                        wait(dve, "w_ready", done(h, q, 1, G // 2, p))
                        v.tensor_tensor(prod_u.rearrange("p t (d u) -> p t d u", d=3),
                                        spread(w[:, :, 192:192 + C1], 2, 3), by_d, ALU.mult).then_inc(
                            S["cross_in"], 1)
                        v.tensor_tensor(
                            o[:, :, 0:2 * REST].rearrange("p t (a c) -> p t a c", a=2)[:, :, :, 0:C0],
                            w[:, :, 0:192].rearrange("p t (a c) -> p t a c", a=2)[:, :, :, 0:C0],
                            spread(feat[:, :, 0:C0], 2, 2), ALU.mult).then_inc(S["prods_ready"], 1)
                        v.tensor_tensor(o[:, :, C0:ONE], w[:, :, 64:96], feat[:, :, C:C + C1], ALU.mult).then_inc(
                            S["prods_ready"], 1)
                        v.tensor_tensor(o[:, :, REST + C0:REST + C].rearrange("p t (d u) -> p t d u", d=3),
                                        spread(w[:, :, 160:160 + C1], 2, 3), by_d, ALU.mult).then_inc(
                            S["prods_ready"], 1)
                    lag, k = behind(j, LAG_ATT)
                    if live(lag) and k % 2 == 1:
                        wait(dve, "logits_ready", done(h, q, lag, G // 2, k // 2, back=1))
                        wait(dve, "att_tanh_ready", done(h, q, lag, G, k))
                        wait(dve, "msg_ready", done(h, q, lag, G, k))
                        v.scalar_tensor_tensor(att_u, att_tanh[k // 2 % 2], 1.5,
                                               msg[(q - lag) % 2][:, k - 1:k + 1, 0:64],
                                               ALU.add, ALU.mult).then_inc(S["att_u_ready"], 1)
                    if ea and j % 2 == 1:
                        wait(dve, "cross_in", done(h, q, 1, G // 2, p))
                        v.tensor_tensor(
                            o[:, :, REST + C:REST + C + 2 * CV].rearrange("p t (x d u) -> p t x d u", x=2, d=3),
                            spread(prod_u.rearrange("p t (d u) -> p t d u", d=3), 2, 2),
                            spread(rhat[r][:, pair, 1:7].rearrange("p t (x d) -> p t x d", x=2), 4, C1),
                            ALU.mult).then_inc(S["prods_ready"], 1)
                    lag, k = behind(j, LAG_ATT)
                    if live(lag) and k % 2 == 1:
                        wait(dve, "att_u_ready", done(h, q, lag, G // 2, k // 2))
                        if k == 1:
                            wait(dve, "logit_d_ready", done(h, q, lag + 2, 1, 0))
                            wait(dve, "logits_turned", done(h, q, lag + 2, 1, 0))
                        v.tensor_reduce(logit[(q - lag) % 2][:, k - 1:k + 1],
                                        att_u.rearrange("p t (h k) -> p t h k", h=H),
                                        AX.X, ALU.add).then_inc(S["logits_ready"], 1)
                    if j == 1 and live(-1):
                        wait(dve, f"gathered_{1 - q}", turn(h, q, 1, 16 * 2 * G))
                        v.tensor_copy(idx[1 - q], idx_all[:, one(h * 2 + (q + 1))].rearrange("p x t -> p (x t)")).then_inc(
                            S["idx_ready"], 1)
                    if live(0) and j in (1, 4):
                        k = j // 4
                        wait(dve, "mlp_var_ready", done(h, q, 0, 2, k, back=1))
                        wait(dve, "mlp_squared", done(h, q, 0, 2, k))
                        v.tensor_reduce(mlp_ss, mlp_sq, AX.X, ALU.add).then_inc(S["mlp_ss_ready"], 1)
                        wait(dve, "mlp_rstd_ready", done(h, q, 0, 2, k, back=1))
                        wait(dve, "mlp_ss_ready", done(h, q, 0, 2, k))
                        v.tensor_scalar(mlp_var, mlp_ss, 1.0 / 64, EPS, ALU.mult, ALU.add).then_inc(
                            S["mlp_var_ready"], 1)
                    if live(0) and j in (2, 5):
                        k = j // 5
                        wait(dve, "mlp_turned", done(h, q, 0, 2, k, back=1))
                        wait(dve, "mlp_rstd_ready", done(h, q, 0, 2, k))
                        v.tensor_tensor(mlp_n, PM[0:P, :].rearrange("p (t c) -> p t c", t=G), spread(mlp_rstd, 2, 64),
                                        ALU.mult).then_inc(S["mlp_n_ready"], 1)
                    if live(2) and j == 3:
                        wait(dve, "eq_ready", done(h, q, 4, G // 2, G // 2 - 1))
                        v.tensor_copy(dst_col[q], dst_all[:, one(h * 2 + (q - 2))].rearrange("p x t -> p (x t)")
                                      ).then_inc(S["cols_ready"], 1)
                        wait(dve, "mask_ready", done(h, q, 3, 1, 0))
                        wait(dve, f"meta_loaded_{q}", turn(h, q, 2, 32))
                        v.tensor_tensor(run_ne[:, 0:P - 1], dst_th[q][:, 1:P], dst_th[q][:, 0:P - 1],
                                        ALU.not_equal).then_inc(S["run_ne_ready"], 1)
                        wait(dve, "run_ne_ready", done(h, q, 2, 1, 0))
                        wait(dve, "max_ready", done(h, q, 3, 1, 0))
                        v.tensor_scalar(run_mask[:, 1:P], run_ne[:, 0:P - 1], -BIG, None, ALU.mult).then_inc(
                            S["mask_ready"], 1)
                    if live(0) and j in (3, 7):
                        k = j // 7
                        wait(dve, "mlp_act_ready", done(h, q, 0, 4, 2 * k + 1))
                        if k == 0:
                            wait(dve, "mlp_out", done(h, q, 1, 2, 1))
                        else:
                            wait(dve, "w_ready", done(h, q, 2, G // 2, G // 2 - 1))
                        v.scalar_tensor_tensor((h1_t, h2_t[q])[k], mlp_tanh, 1.0, mlp_y, ALU.add, ALU.mult).then_inc(
                            S["mlp_h_ready"], 1)
                    if live(2) and j == 4:
                        wait(dve, "mask_ready", done(h, q, 2, 1, 0))
                        wait(dve, "max_ready", done(h, q, 3, 1, 0))
                        wait(dve, "logits_turned", done(h, q, 2, 1, 0))
                        v.tensor_tensor_scan(run_fwd, run_mask[:, 0:P], run_t, 0.0, ALU.add, ALU.max).then_inc(
                            S["fwd_ready"], 1)
                    if live(2) and j == 6:
                        wait(dve, "prob_ready", done(h, q, 3, 1, 0))
                        wait(dve, "max_turned", done(h, q, 2, 1, 0))
                        back = run_b.rearrange("p (t h) -> p t h", t=G)
                        v.tensor_tensor(logit_d, logit[q], back, ALU.subtract).then_inc(S["logit_d_ready"], 1)
                        wait(dve, f"rows_stored_{q}", turn(h, q, 4))
                        v.tensor_copy(run_rows[q][:, :, R_MAX:R_MAX + H], back).then_inc(S["max_kept"], 1)
                        wait(dve, "cols_ready", done(h, q, 2, 1, 0))
                        v.tensor_copy(run_rows[q][:, :, R_DST:R_DST + 1], dst_col[q].unsqueeze(2)).then_inc(
                            S["max_kept"], 1)
                    if live(2) and j == 7:
                        wait(dve, "pay_ready", done(h, q, 4, G, G - 1))
                        wait(dve, "prob_ready", done(h, q, 2, 1, 0))
                        v.tensor_tensor(prob_r[q], spread(prob[q], 2, 3), spread(rhat[q][:, :, 0:3], 3, H), ALU.mult).then_inc(
                            S["prob_r_ready"], 1)

            steps(dve, step)
            barrier(dve, "edge_pass_over")

            link = chain("carry_step")

            def by_tile(ap):
                return ap.rearrange("p (a k) -> p a k", k=K)

            dve.wait_ge(S["last_loaded"], 16)
            v.tensor_copy(last_max.rearrange("p t (k h) -> p t k h", h=H),
                          spread(last[:, :, R_MAX:R_MAX + H], 2, HALF // H)).then_inc(S["last_spread"], 1)
            for b in range(2):
                dve.wait_ge(S["last_turned"], b + 1)
                for o, bank, n in ((chan[:, 0], ps[b], HALF), (chan[:, 1], ps[2 + b], SUMS - HALF),
                                   (chan_m, ps[4 + b], HALF), (chan_d, ps[6 + b], HALF)):
                    link(v.tensor_copy(by_tile(o[0:n])[:, :, 4 * b:4 * b + 4],
                                       bank[0:n, 0:400].rearrange("p (k a) -> p a k", k=4)))
            link(v.memset(same[:, 0:1], 0.0))
            link(v.memset(step_m[:, 0:1], 0.0))
            link(v.tensor_tensor(same[:, 1:], chan_d[:, 1:], chan_d[:, 0:TILES - 1], ALU.is_equal))
            link(v.tensor_scalar(restart, same, BIG, -BIG, ALU.mult, ALU.add))
            link(v.tensor_tensor_scan(scan_m, restart, chan_m, 0.0, ALU.add, ALU.max))
            link(v.tensor_tensor(step_m[:, 1:], scan_m[:, 0:TILES - 1], scan_m[:, 1:], ALU.subtract))
            link(v.tensor_scalar(step_m, step_m, 0.0, None, ALU.min))
            v.tensor_copy(chan_x[:, 0], chan[:, 0]).then_inc(S["carry_exp_in"], 1)
            v.tensor_tensor(chan_d, chan_m, scan_m, ALU.subtract).then_inc(S["carry_exp_in"], 1)
            dve.wait_ge(S["carry_exp"], 2)
            link(v.tensor_tensor(keep, keep, same, ALU.mult))
            link(v.tensor_tensor(chan_x[:, 0], chan[:, 0], take, ALU.mult))
            n = SUMS - HALF
            link(v.tensor_tensor(chan_x[0:n, 1], chan[0:n, 1], take[0:n], ALU.mult))
            link(v.tensor_tensor_scan(scan_x[:, 0], keep, chan_x[:, 0], 0.0, ALU.mult, ALU.add))
            link(v.memset(sentinel, 0.0))
            link(v.memset(sentinel[:, R_DST:R_DST + 1], -1.0))
            v.tensor_tensor_scan(scan_x[0:n, 1], keep[0:n], chan_x[0:n, 1], 0.0, ALU.mult, ALU.add).then_inc(
                S["carry_done"], 1)
            v.memset(carry_rows, 0.0).then_inc(S["carry_rows_ready"], 1)
            dve.wait_ge(S["carry_rows_ready"], 1)
            v.tensor_copy(carry_rows[:, :, R_DST:R_DST + 1], last[:, :, R_DST:R_DST + 1]).then_inc(
                S["carry_rows_ready"], 1)
            for k in range(K):
                dve.wait_ge(S["carry_turned"], k + 1)
                v.tensor_copy(carry_rows[:, k, 0:R_DST], ps[k][0:100, 0:R_DST]).then_inc(S["carry_rows_ready"], 1)
            barrier(dve, "carry_over")

            def places(h, q, ahead):
                r = (q + ahead) % 2
                g = h * (2 * NT) + (q + ahead) * NT
                for k in (0, 1):
                    v.tensor_copy(place[r][:, k], place_all[:, k, bass.ds(g, NT)]).then_inc(S["place_ready"], 1)
                v.tensor_copy(node_no[r], node_all[:, bass.ds(g, NT)]).then_inc(S["place_ready"], 1)

            places(0, 0, 0)

            def last_pass(h, q, more):
                links = [0]

                def link(ins):
                    links[0] += 1
                    ins.then_inc(S["last_step"], 1)
                    dve.wait_ge(S["last_step"], h * (2 * LAST_STEPS) + (q * LAST_STEPS + links[0]))

                if more:
                    places(h, q, 1)
                wait(dve, "place_ready", done(h, q, 0, 3, 2))
                wait(dve, f"pieces_loaded_{q}", turn(h, q, 0, PIECES))
                wait(dve, f"nodes_loaded_{q}", turn(h, q, 0, 32))
                two = pieces[q]
                link(v.tensor_tensor(found, two[:, :, :, R_DST], spread(node_no[q], 1, 2), ALU.is_equal))
                link(v.tensor_scalar(absent, found, BIG, -BIG, ALU.mult, ALU.add))
                link(v.tensor_tensor(piece_max, two[:, :, :, R_MAX:R_MAX + H], spread(absent, 3, H), ALU.add))
                link(v.tensor_tensor(both_max, piece_max[:, 0], piece_max[:, 1], ALU.max))
                v.tensor_tensor(piece_d, piece_max, spread(both_max, 1, 2), ALU.subtract).then_inc(S["merge_in"], 1)
                wait(dve, "merge_exp", done(h, q, 0, 1, 0))
                link(v.tensor_tensor(piece_f, piece_e, spread(found, 3, H), ALU.mult))
                for k, o in enumerate((agg_a, agg_b)):
                    link(v.tensor_tensor(o.rearrange("p t (k h) -> p t k h", h=H),
                                         two[:, k, :, 0:SUMS].rearrange("p t (k h) -> p t k h", h=H),
                                         spread(piece_f[:, k], 2, SUMS // H), ALU.mult))
                link(v.tensor_tensor(agg_a, agg_a, agg_b, ALU.add))
                link(v.tensor_scalar(den, agg_a[:, :, 0:H], 1e-12, None, ALU.add))
                link(v.reciprocal(rden, den))
                v.tensor_tensor(agg[:, :, H:SUMS].rearrange("p t (k h) -> p t k h", h=H),
                                agg_a[:, :, H:SUMS].rearrange("p t (k h) -> p t k h", h=H),
                                spread(rden, 2, C // H), ALU.mult).then_inc(S["agg_ready"], 1)
                x = x_in[q]
                for t in range(NT):
                    u = (q * NT + t) % 2
                    wait(dve, "projected", done(h, q, 0, NT, t))
                    v.tensor_tensor(x1[:, t, 0:C0], x[:, t, 0:C0], PL[u][0:P, 0:C0], ALU.add).then_inc(
                        S["x1_ready"], 1)
                    v.tensor_tensor(x1[:, t, C0:C].rearrange("p (u d) -> p d u", d=3),
                                    x[:, t, C0:C].rearrange("p (u d) -> p d u", d=3),
                                    PL[u][0:P, C0:C].rearrange("p (d u) -> p d u", d=3), ALU.add).then_inc(
                        S["x1_ready"], 1)
                wait(dve, "x1_ready", done(h, q, 0, 2 * NT, 2 * NT - 1))
                normed(link, x1, x_norm[0], "y_var_ready", done(h, q, 0, 2, 0), "y_rstd_ready",
                       lambda ins: ins.then_inc(S["x2_norm_ready"], 1))
                link(v.tensor_tensor(y_sum, x, x1, ALU.add))
                for t in range(NT):
                    u = (q * NT + t) % 2
                    wait(dve, "f1_ready", done(h, q, 0, NT, t))
                    v.tensor_scalar(ff_g[:, u], PL[u][0:P, 0:384], a0[q][:, t:t + 1], None, ALU.mult).then_inc(
                        S["ff_scaled"], 1)
                    wait(dve, "ff_scaled", done(h, q, 0, NT, t))
                    wait(dve, "ff_tanh", done(h, q, 0, NT, t))
                    v.scalar_tensor_tensor(ff_s[:, t], ff_t[:, u, 0:M0], 1.0, ff_g[:, u, 0:M0], ALU.add,
                                           ALU.mult).then_inc(S["ff_ready"], 1)
                    v.scalar_tensor_tensor(ff_v[:, t].rearrange("p (d m) -> p d m", d=3),
                                           spread(ff_t[:, u, M0:192], 1, 3), 1.0,
                                           ff_g[:, u, 192:384].rearrange("p (d m) -> p d m", d=3), ALU.add,
                                           ALU.mult).then_inc(S["ff_ready"], 1)
                for t in range(NT):
                    u = (q * NT + t) % 2
                    o = (PW, PO)[u][0:P, 0:C]
                    wait(dve, "f2_ready", done(h, q, 0, NT, t))
                    v.scalar_tensor_tensor(y_sum[:, t, 0:C0], o[:, 0:C0], a0[q][:, t:t + 1], y_sum[:, t, 0:C0],
                                           ALU.mult, ALU.add).then_inc(S["x2_ready"], 1)
                    yv = y_sum[:, t, C0:C].rearrange("p (u d) -> p d u", d=3)
                    v.scalar_tensor_tensor(yv, o[:, C0:C].rearrange("p (d u) -> p d u", d=3), a0[q][:, t:t + 1], yv,
                                           ALU.mult, ALU.add).then_inc(S["x2_ready"], 1)
                wait(dve, "x2_ready", done(h, q, 0, 2 * NT, 2 * NT - 1))
                link(v.tensor_reduce(x_sum, y_sum, AX.X, ALU.add))
                link(v.tensor_scalar(x_mean, x_sum, 1.0 / C, None, ALU.mult))
                link(v.tensor_tensor(x_cen, y_sum, spread(x_mean, 2, C), ALU.subtract))
                link(v.tensor_tensor(x_sq, x_cen, x_cen, ALU.mult))
                link(v.tensor_reduce(x_ss[:, 0], x_sq, AX.X, ALU.add))
                v.tensor_scalar(x_var[:, 0], x_ss[:, 0], 1.0 / C, EPS, ALU.mult, ALU.add).then_inc(
                    S["y_var_ready"], 1)
                wait(dve, f"out_stored_{q}", turn(h, q, 2))
                wait(dve, "y_rstd_ready", done(h, q, 0, 2, 1))
                v.tensor_tensor(y_out[q], x_cen, spread(x_rstd[:, 0], 2, C), ALU.mult).then_inc(S["y_ready"], 1)
                assert links[0] == LAST_STEPS, links[0]

            node_groups(dve, last_pass)


def kernel(**inputs):
    import numpy as _np
    import concourse.bacc as _bacc
    from concourse import mybir as _mybir
    from concourse.bass_utils import run_bass_kernel_spmd as _run

    nc = _bacc.Bacc("TRN2", target_bir_lowering=False, num_devices=1)
    arrays, handles = {}, {}
    for name in inputs:
        a = _np.ascontiguousarray(inputs[name])
        arrays[f"in_{name}"] = a
        handles[name] = nc.dram_tensor(f"in_{name}", a.shape, _mybir.dt.from_np(a.dtype), kind="ExternalInput").ap()
    out = nc.dram_tensor("out", (N, C), F32, kind="ExternalOutput").ap()
    build(nc, handles, out)
    r = _run(nc, [arrays], core_ids=[0])
    return r.results[0]["out"]
```

```python
import concourse.bass as bass
from concourse import mybir
from contextlib import ExitStack

F32 = mybir.dt.float32
BF16 = mybir.dt.bfloat16
I32 = mybir.dt.int32
ALU = mybir.AluOpType
ACT = mybir.ActivationFunctionType
AX = mybir.AxisListType

N, E = 6250, 100000
C0, C1 = 64, 32
CV = 3 * C1
C = C0 + CV
H = 8
M0, M1 = 128, 64
P = 125
G = 8
TILES = E // P
GROUPS = TILES // G
NT = 5
NODE_TILES = N // P
NODE_GROUPS = NODE_TILES // NT
ROW = 180
SUMS = H + C
R_MAX, R_DST = SUMS, SUMS + H
BIG = 1e30
EPS = 1e-5
SQ3 = 3.0 ** 0.5
SQ2 = 2.0 ** 0.5

B_NODE, B_MLP1, B_MLP2, B_W, B_PROJ, B_F1, B_F2, B_END = 0, 320, 832, 1344, 1792, 1952, 2144, 2304
W_TILE = 224
PROD = 4 * 128
ONE, REST = C0 + C1, 128
LIN = 328
LIN_S = 200
MSG = LIN - 64
PAY = SUMS + CV

RDIR = 7
LAG_T, LAG_LIN, LAG_ATT, LAG_PAY, LAG_SUM = 2, 3, 4, 16, 17
W_ORDER = ((0, 0, 64), (64, 160, 192), (96, 64, 128), (160, 128, 160), (192, 192, 224))
PIECES = 16 * 2 * NT
LOADS, WEIGHT_STEPS, COUNT_STEPS, PLACE_STEPS, NORM_STEPS = 112, 32, 7, 4, 9
REST_BLOCKS = ((0, 0, C0, CV, SQ3),) + tuple(
    (C0 + C1 * b, lo, lo + C1, C1 * d, factor)
    for b, (lo, d, factor) in enumerate(
        [(C0, d, 1.0) for d in range(3)]
        + [(C0 + C1, (d + 2) % 3, SQ3 / SQ2) for d in range(3)]
        + [(C0 + C1, (d + 1) % 3, SQ3 / SQ2) for d in range(3)]))
CARRY_ROWS = 2 + TILES // 100
EARLY = ((0, 0), (0, 1), (NODE_GROUPS // 2 - 1, 0), (NODE_GROUPS // 2 - 1, 1))
MERGE_STEPS, FINAL_STEPS = 10, 5
LAST_PEEL, LAST_LOOP_END, LAST_PASS = 4, NODE_GROUPS - 2, NODE_GROUPS + 3
PEEL, LOOP_END, STEPS = 6, GROUPS - 2, GROUPS + 4


def spread(ap, axis, n):
    ap = ap.unsqueeze(axis)
    shape = list(ap.shape)
    shape[axis] = n
    return ap.broadcast_to(shape)


def build(nc, inp, out):
    ctx = ExitStack()
    with ctx:
        def sb(name, shape, dt=F32):
            return ctx.enter_context(nc.sbuf_tensor(name, shape, dt))

        def sem(name):
            return ctx.enter_context(nc.semaphore(name))

        src_table = nc.dram_tensor("src_table", (N, C), F32).ap()
        dst_table = nc.dram_tensor("dst_table", (N, C), F32).ap()
        runs = nc.dram_tensor("runs", (E, ROW), F32).ap()
        carry = nc.dram_tensor("carry", (TILES + 1, ROW), F32).ap()

        ident = sb("ident", [128, 128])
        ones3 = sb("ones3", [3, 128], BF16)
        bias3 = sb("bias3", [3, B_END], BF16)
        ln1 = sb("ln1", [CV, 3])
        ln2 = sb("ln2", [CV, 3])
        mlp_affine = sb("mlp_affine", [128, 8])
        w_node_s = sb("w_node_s", [C0, 128])
        w_node_v = sb("w_node_v", [CV, 192])
        w_mlp = sb("w_mlp", [128, 2, 128])
        w3 = sb("w3", [128, 2 * W_TILE])
        w_lin = sb("w_lin", [128, LIN_S])
        w_rest = sb("w_rest", [128, 3, 128])
        w_proj_s = sb("w_proj_s", [C0, C0])
        w_proj_v = sb("w_proj_v", [CV, CV])
        w_f1_s = sb("w_f1_s", [C0, 192])
        w_f1_v = sb("w_f1_v", [CV, 192])
        w_f2_s = sb("w_f2_s", [M0, C0])
        w_f2_v = sb("w_f2_v", [CV, 2, CV])
        minus_half = sb("minus_half", [P, 16])

        idx_all = sb("idx_all", [P, GROUPS, 2 * G], I32)
        dst_all = sb("dst_all", [P, GROUPS, G])
        rhat_all = sb("rhat_all", [P, GROUPS, G, RDIR])
        node_all = sb("node_all", [P, NODE_TILES])
        place_all = sb("place_all", [P, 2, NODE_TILES], I32)

        AREA = 34000
        area = sb("area", [128, AREA])
        top = [0]

        def part(parts, *dims, dt=F32, reset=None):
            if reset is not None:
                top[0] = reset
            n = 1
            for d in dims:
                n *= d
            words = n if dt != BF16 else (n + 1) // 2
            ap = area[0:parts, top[0]:top[0] + words]
            top[0] += words
            assert top[0] <= AREA, top[0]
            if dt != F32:
                ap = ap.bitcast(dt)
            names = "abcd"[:len(dims)]
            if len(dims) > 1:
                ap = ap.rearrange(f"p ({' '.join(names)}) -> p {' '.join(names)}",
                                  **{m: d for m, d in zip(names[1:], dims[1:])})
            return ap

        first_dst = part(P, TILES, reset=0)
        search_junk = part(P, TILES)
        search_node = [part(P, NT) for q in (0, 1)]
        search_cnt = part(P, NT)
        count_node = part(P, NT)
        search_tile_i = [part(P, NT, dt=I32) for q in (0, 1)]
        search_dst = [part(P, NT, P, dt=I32) for q in (0, 1)]
        search_le = part(P, NT, P)
        search_in = part(P, NT)
        search_row = part(P, NT)
        SEARCH_END = top[0]
        K = TILES // 100
        nat_i = part(100, 2, K, P, dt=I32)
        nat_f = part(100, 2, K, P)
        nat_v = part(100, K, P, 3)
        vec_all = part(P, GROUPS, G, 3)
        vec_sq = part(P, TILES, 3)
        vec_n2 = part(P, TILES)
        vec_inv = part(P, TILES)
        vec_root = part(P, TILES)
        node_i = part(P, NODE_TILES, dt=I32)
        bias_row = part(1, B_END)
        bias_rest = part(1, B_END)
        bias_parts = part(1, 3, B_END, dt=BF16)
        bias_mean = part(1, 2, G)
        mlp_mean = part(128, 2)
        w3_raw = part(128, 2 * W_TILE)
        lin_raw = part(CV + 1, 128)
        adot = part(CV + 1, 64)
        raw_rest = part(128, 3, C1)
        x_in = [part(P, NT, C, reset=None if q else SEARCH_END) for q in (0, 1)]
        x_sq = part(P, NT, C)
        x_norm = [part(P, NT, C) for q in (0, 1)]
        x_sum = part(P, NT)
        x_mean = part(P, NT)
        x_cen = part(P, NT, C)
        x_ss = part(P, 2, NT)
        x_var = part(P, 2, NT)
        x_rstd = part(P, 2, NT)
        table = [part(P, NT, 2 * C) for q in (0, 1)]
        tile_s = part(128, 2, P)
        tile_v = part(CV, 2, 2, P)
        a0 = [part(P, NT) for q in (0, 1)]
        node_no = [part(P, NT) for q in (0, 1)]
        place = [part(P, 2, NT, dt=I32) for q in (0, 1)]
        pieces = [part(P, 2, NT, ROW) for q in (0, 1)]
        found = part(P, 2, NT)
        absent = part(P, 2, NT)
        piece_max = part(P, 2, NT, H)
        both_max = part(P, NT, H)
        piece_d = part(P, 2, NT, H)
        piece_e = part(P, 2, NT, H)
        piece_f = part(P, 2, NT, H)
        agg_a = part(P, NT, SUMS)
        agg_b = part(P, NT, SUMS)
        agg = [part(P, NT, SUMS) for q in (0, 1)]
        den = part(P, NT, H)
        rden = part(P, NT, H)
        x1 = part(P, NT, C)
        ff_g = part(P, 2, 384)
        ff_t = part(P, 2, 192)
        ff_s = part(P, NT, M0)
        ff_v = part(P, NT, 192)
        y_sum = [part(P, NT, C) for q in (0, 1)]
        y_cen = part(P, NT, C)
        y_var = part(P, NT)
        y_rstd = part(P, NT)
        y_out = part(P, NT, C)
        agg_s = part(C0, 2, P)
        agg_v = part(CV, 2, P)
        ff_st = part(128, 2, P)
        ff_vt = part(CV, 2, 2, P)
        es_in = [part(P, G, 64, reset=None if q else 0) for q in (0, 1)]
        got_s = [part(P, G, C) for q in (0, 1)]
        got_d = [part(P, G, C) for q in (0, 1)]
        dst_row = [part(P, G, P, dt=I32) for q in (0, 1)]
        dst_th = [part(G * H, P, dt=I32) for q in (0, 1)]
        idx = [part(P, 2 * G, dt=I32) for q in (0, 1)]
        dst_col = [part(P, G) for q in (0, 1)]
        rhat = [part(P, G, RDIR) for q in (0, 1)]
        es_t = part(128, 4, P)
        mlp_sq = part(P, G, 64)
        mlp_ss = part(P, G)
        mlp_var = part(P, G)
        mlp_rstd = part(P, G)
        mlp_n = part(P, G, 64)
        mlp_tanh = part(128, 4, P)
        mlp_y = part(128, 4, P)
        h1_t = part(128, 4, P)
        h2_t = [part(128, 4, P) for q in (0, 1)]
        feat = part(P, 2, C + C1)
        dot_in = part(P, 2, CV)
        prod_u = part(P, 2, CV)
        prod = [part(P, 2, PROD) for q in (0, 1)]
        prod_t = [part(128, 4, P) for q in (0, 1)]
        att_tanh = [part(P, 2, 64) for q in (0, 1)]
        att_u = part(P, 2, 64)
        msg = [part(P, G, MSG) for q in (0, 1)]
        logit = [part(P, G, H) for q in (0, 1)]
        run_ne = part(G * H, P)
        run_mask = part(G * H, P + 1)
        run_fwd = part(G * H, P)
        run_max = part(G * H, P)
        logit_d = part(P, G, H)
        prob = [part(P, G, H) for q in (0, 1)]
        prob_r = [part(P, G, 3, H) for q in (0, 1)]
        eq = [part(P, 2, P) for q in (0, 1)]
        pay = [part(P, 2, PAY) for q in (0, 1)]
        run_rows = [part(P, G, ROW) for q in (0, 1)]
        HALF = 88
        last = part(100, K, ROW, reset=0)
        last_max = part(100, K, HALF)
        chan = part(HALF, 2, TILES)
        chan_m = part(HALF, TILES)
        chan_d = part(HALF, TILES)
        same = part(HALF, TILES)
        restart = part(HALF, TILES)
        scan_m = part(HALF, TILES)
        step_m = part(HALF, TILES)
        keep = part(HALF, TILES)
        take = part(HALF, TILES)
        chan_x = part(HALF, 2, TILES)
        scan_x = part(HALF, 2, TILES)
        carry_rows = part(100, K, ROW)
        sentinel = part(1, ROW)

        ps = [ctx.enter_context(nc.psum_tensor(f"ps{i}", [128, 512], F32)) for i in range(8)]
        PM = ps[0]
        PR, PW, PT, PL, PO = ps[1], ps[2], (ps[3], ps[4]), (ps[5], ps[6]), ps[7]
        run_t = PR[0:G * H, 0:P]
        run_b = PR[0:P, 128:128 + G * H]

        x_v = inp["x"].rearrange("(g t p) c -> g p t c", t=NT, p=P)
        a0_v = inp["node_vec1"].rearrange("(g t p) c -> g p t c", t=NT, p=P)
        out_v = out.rearrange("(g t p) c -> g p t c", t=NT, p=P)
        src_v = src_table.rearrange("(g t p) c -> g p t c", t=NT, p=P)
        dst_v = dst_table.rearrange("(g t p) c -> g p t c", t=NT, p=P)
        es_v = inp["edge_attr_64"].rearrange("(g t p) c -> g p t c", t=G, p=P)
        dst_row_v = inp["dst"].rearrange("(g x e) -> g x e", x=1, e=G * P)
        dst_th_v = inp["dst"].rearrange("(g t x e) -> g t x e", t=G, x=1, e=P)
        dst_tiles = inp["dst"].rearrange("(t e) -> t e", e=P)
        runs_v = runs.rearrange("(g t p) c -> g p t c", t=G, p=P)
        last_v = runs.rearrange("(a k p) c -> p a k c", k=K, p=P)

        def W(name):
            return inp["L0_gnn_" + name]

        S = {}
        for name in (
            "zeroed", "weights_loaded", "weight_step", "bias_moved", "consts_made", "nat_loaded", "nat_cast",
            "cols_turned", "cols_kept", "vec_step", "vec_root", "vec_unit", "count_step", "place_step", "search_ready",
            "search_loaded_0", "search_loaded_1",
            "x_loaded_0", "x_loaded_1", "norm_step", "x_var_ready", "x_rstd_ready", "x_norm_ready", "node_turned",
            "affine_ready", "node_projected", "table_ready", "stored_0", "stored_1",
            "es_loaded_0", "es_loaded_1", "meta_loaded_0", "meta_loaded_1", "gathered_0", "gathered_1",
            "idx_ready", "rhat_ready", "es_turned", "es_copied", "mlp_out", "mlp_squared", "mlp_ss_ready",
            "mlp_var_ready", "mlp_rstd_ready", "mlp_n_ready", "mlp_turned", "mlp_act_ready", "mlp_h_ready",
            "edge_consts", "sum_ready", "dots_in", "dots_ready", "w_ready", "cross_in", "prods_ready", "prods_turned",
            "prods_copied", "lin_ready", "att_tanh_ready", "msg_ready", "att_u_ready", "logits_ready",
            "cols_ready", "run_ne_ready", "mask_ready", "logits_turned", "fwd_ready", "max_ready", "max_turned",
            "max_kept", "logit_d_ready", "prob_ready", "prob_r_ready", "eq_ready", "pay_ready", "sums_ready",
            "rows_ready", "rows_stored_0", "rows_stored_1",
            "last_loaded", "last_spread", "last_turned", "last_copied", "carry_step", "carry_exp_in", "carry_exp", "carry_done",
            "carry_turned", "carry_rows_ready", "carry_stored",
            "place_ready", "pieces_loaded_0", "pieces_loaded_1", "nodes_loaded_0", "nodes_loaded_1", "attrs_loaded_0",
            "attrs_loaded_1", "merge_step", "merge_in", "merge_exp", "agg_ready", "agg_turned", "agg_copied",
            "projected", "x1_ready", "x1_step", "x1_var_ready", "x1_rstd_ready", "x1_norm_ready", "norm_turned",
            "norm_scaled", "y_base_ready", "f1_ready", "ff_scaled", "ff_tanh", "ff_ready", "ff_turned",
            "ff_copied", "f2_ready", "x2_ready", "final_step", "y_var_ready", "y_rstd_ready", "y_ready",
            "out_stored", "waits_passed",
            "prologue_over", "node_pass_over", "edge_pass_over", "carry_over",
        ):
            S[name] = sem(name)

        def done(h, q, lag, n, k, back=0):
            return h * (2 * n) + ((q - lag) * n + k + 1 - back)

        def turn(h, q, lag, n=16):
            return h * n + ((q - lag) // 2 + 1) * n

        def wait(eng, name, count):
            if isinstance(count, int) and count <= 0:
                return
            eng.wait_ge(S[name], count)

        def alone(eng, name, count):
            wait(eng, name, count)
            if not isinstance(count, int):
                eng.sem_inc(S["waits_passed"])

        def steps(eng, body):
            for s in range(PEEL):
                body(s // 2, s % 2, lambda lag, s=s: 0 <= s - lag < GROUPS)
            with eng.Fori(PEEL // 2, LOOP_END // 2) as h:
                for q in (0, 1):
                    body(h, q, lambda lag: True)
            for s in range(LOOP_END, STEPS):
                body(s // 2, s % 2, lambda lag, s=s: 0 <= s - lag < GROUPS)

        def node_groups(eng, body):
            for q in (0, 1):
                body(0, q, True)
            with eng.Fori(1, NODE_GROUPS // 2 - 1) as h:
                for q in (0, 1):
                    body(h, q, True)
            for q in (0, 1):
                body(NODE_GROUPS // 2 - 1, q, q == 0)

        def last_steps(eng, body):
            for s in range(LAST_PEEL):
                body(s // 2, s % 2, lambda lag, s=s: 0 <= s - lag < NODE_GROUPS)
            with eng.Fori(LAST_PEEL // 2, LAST_LOOP_END // 2) as h:
                for q in (0, 1):
                    body(h, q, lambda lag: True)
            for s in range(LAST_LOOP_END, LAST_PASS):
                body(s // 2, s % 2, lambda lag, s=s: 0 <= s - lag < NODE_GROUPS)

        def behind(j, lag):
            return 1 - (j - lag) // G, (j - lag) % G

        def barrier(eng, name):
            eng.drain().then_inc(S[name], 1)
            eng.wait_ge(S[name], 5)

        def one(g):
            return bass.ds(g, 1)

        loads = [0]
        ZERO_TILES = (w_mlp[:, :, :], w3_raw, w_node_v[:, :], w_lin[:, :], w_rest[:, :, :], w_proj_v[:, :], w_f1_v[:, :], w_f2_v[:, :, :], bias_row)
        ZEROED = len(ZERO_TILES) + 1

        block = ctx.enter_context(nc.Block())

        @block.sync
        def _(sp):
            def load(dst, src):
                sp.dma_start(dst, src, allow_slow_non_contiguous=True).then_inc(S["weights_loaded"], 16)
                loads[0] += 1

            def row(name):
                return W(name).unsqueeze(0)

            sp.dma_start(nat_i[:, 0], inp["src"].rearrange("(a k e) -> a k e", k=K, e=P)).then_inc(S["nat_loaded"], 16)
            sp.dma_start(nat_i[:, 1], inp["dst"].rearrange("(a k e) -> a k e", k=K, e=P)).then_inc(S["nat_loaded"], 16)
            sp.dma_start(nat_v, inp["edge_attr_3"].rearrange("(a k e) c -> a k e c", k=K, e=P)).then_inc(
                S["nat_loaded"], 16)
            sp.wait_ge(S["zeroed"], ZEROED)
            for w, b, v, dst in (("ln1_w0", "ln1_b0", "ln1_w1", ln1), ("ln2_w0", "ln2_b0", "ln2_w1", ln2)):
                load(dst[0:C0, 0:1], W(w).unsqueeze(1))
                load(dst[0:C0, 1:2], W(b).unsqueeze(1))
                for d in range(3):
                    load(dst[C1 * d:C1 * (d + 1), 2:3], W(v).unsqueeze(1))
            load(w_node_s[:, 0:64], W("msrc_ws"))
            load(w_node_s[:, 64:128], W("mdst_ws"))
            for d in range(3):
                rows = slice(C1 * d, C1 * (d + 1))
                load(w_node_v[rows, C1 * d:C1 * (d + 1)], W("msrc_wv"))
                load(w_node_v[rows, CV + C1 * d:CV + C1 * (d + 1)], W("mdst_wv"))
                load(w_f1_v[rows, M1 * d:M1 * (d + 1)], W("f1_wv"))
                for k in range(4):
                    load(w_proj_v[C1 * d + 8 * k:C1 * d + 8 * k + 8, C1 * d:C1 * (d + 1)],
                         W("proj_wv").rearrange("(h k) n -> k h n", k=4)[k])
            for k in range(8):
                load(w_proj_s[8 * k:8 * k + 8, :], W("proj_ws").rearrange("(h k) n -> k h n", k=8)[k])
            for half in (0, 1):
                rows = slice(64 * half, 64 * half + 64)
                load(w_mlp[rows, 0, rows], W("rw1"))
                load(w_mlp[rows, 1, rows], W("rw2"))
                for c, v in enumerate(("rg1", "rbe1", "rg2", "rbe2")):
                    load(mlp_affine[rows, c:c + 1], W(v).unsqueeze(1))
                for at, lo, hi in W_ORDER:
                    load(w3_raw[rows, W_TILE * half + at:W_TILE * half + at + hi - lo], W("rw3")[:, lo:hi])
            load(lin_raw[0:CV], W("lin_ws"))
            load(adot, W("alpha_dot").rearrange("(x h) k -> x (h k)", x=1).broadcast_to([CV + 1, 64]))
            for at, lo, hi, _, _ in REST_BLOCKS:
                load(raw_rest[at % 128:at % 128 + hi - lo, at // 128], W("lin_wv")[lo:hi, :])
            load(lin_raw[CV:CV + 1, :], row("lin_bs"))
            load(bias_row[:, B_NODE + C:B_NODE + C + 64], row("mdst_bs"))
            for t in range(G):
                load(bias_row[:, B_MLP1 + 64 * t:B_MLP1 + 64 * t + 64], row("rb1"))
                load(bias_row[:, B_MLP2 + 64 * t:B_MLP2 + 64 * t + 64], row("rb2"))
            for t in range(2):
                for at, lo, hi in W_ORDER:
                    load(bias_row[:, B_W + W_TILE * t + at:B_W + W_TILE * t + at + hi - lo], row("roff")[:, lo:hi])
            load(bias_row[:, B_PROJ:B_PROJ + 64], row("proj_bs"))
            load(bias_row[:, B_F1:B_F1 + 192], row("f1_bs"))
            load(bias_row[:, B_F2:B_F2 + 64], row("f2_bs"))
            load(w_f1_s[:, :], W("f1_ws"))
            load(w_f2_s[:, :], W("f2_ws"))
            load(w_f2_v[0:64, 0, 0:32], W("f2_wv"))
            load(w_f2_v[64:96, 0, 32:64], W("f2_wv")[0:32, :])
            load(w_f2_v[0:32, 1, 32:64], W("f2_wv")[32:64, :])
            load(w_f2_v[32:96, 1, 64:96], W("f2_wv"))
            assert loads[0] == LOADS, loads[0]
            sp.wait_ge(S["weight_step"], WEIGHT_STEPS)
            for k in range(3):
                sp.dma_start(bias3[k:k + 1, :], bias_parts[0:1, k, :]).then_inc(S["bias_moved"], 16)
            sp.wait_ge(S["bias_moved"], 48)
            barrier(sp, "prologue_over")

            sp.dma_start(x_in[0], x_v[0]).then_inc(S["x_loaded_0"], 16)

            def node_step(h, q, more):
                if more:
                    alone(sp, "x_norm_ready", done(h, q, 1, 1, 0))
                    sp.dma_start(x_in[1 - q], x_v[h * 2 + (q + 1)]).then_inc(S[f"x_loaded_{1 - q}"], 16)
                alone(sp, "table_ready", done(h, q, 0, NT, NT - 1))
                sp.dma_start(src_v[h * 2 + q], table[q][:, :, 0:C]).then_inc(S[f"stored_{q}"], 16)
                sp.dma_start(dst_v[h * 2 + q], table[q][:, :, C:2 * C]).then_inc(S[f"stored_{q}"], 16)

            node_groups(sp, node_step)
            for q in (0, 1):
                sp.wait_ge(S[f"stored_{q}"], 32 * (NODE_GROUPS // 2))
            barrier(sp, "node_pass_over")

            sp.dma_start(es_in[0], es_v[0]).then_inc(S["es_loaded_0"], 16)

            def step(h, q, live):
                if live(-1):
                    alone(sp, "es_turned", done(h, q, 1, 1, 0))
                    sp.dma_start(es_in[1 - q], es_v[h * 2 + (q + 1)]).then_inc(S[f"es_loaded_{1 - q}"], 16)
                if live(4):
                    alone(sp, "rows_ready", done(h, q, 4, G // 2, G // 2 - 1))
                    alone(sp, "max_kept", done(h, q, 4, 2, 1))
                    sp.dma_start(runs_v[h * 2 + (q - 4)], run_rows[q]).then_inc(S[f"rows_stored_{q}"], 16)
                if live(1):
                    alone(sp, "run_ne_ready", done(h, q, 3, 1, 0))
                    alone(sp, "eq_ready", done(h, q, 3, G // 2, G // 2 - 1))
                    sp.dma_start(dst_row[1 - q], dst_row_v[h * 2 + (q - 1)].broadcast_to([P, G * P])
                                 .rearrange("p (t e) -> p t e", t=G)).then_inc(S[f"meta_loaded_{1 - q}"], 16)
                    sp.dma_start(dst_th[1 - q], dst_th_v[h * 2 + (q - 1)].broadcast_to([G, H, P])).then_inc(
                        S[f"meta_loaded_{1 - q}"], 16)

            steps(sp, step)
            for q in (0, 1):
                sp.wait_ge(S[f"rows_stored_{q}"], 16 * (GROUPS // 2))
            barrier(sp, "edge_pass_over")

            sp.dma_start(last, last_v[P - 1]).then_inc(S["last_loaded"], 16)
            sp.wait_ge(S["carry_rows_ready"], CARRY_ROWS)
            sp.dma_start(carry[1:TILES + 1, :].rearrange("(a k) c -> a k c", k=K), carry_rows).then_inc(
                S["carry_stored"], 16)
            sp.dma_start(carry[0:1, :], sentinel).then_inc(S["carry_stored"], 16)
            sp.wait_ge(S["carry_stored"], 32)
            barrier(sp, "carry_over")

            sp.dma_start(x_in[0], x_v[0]).then_inc(S["nodes_loaded_0"], 16)

            def last_step(h, q, live):
                if live(1):
                    alone(sp, "ff_scaled", done(h, q, 3, NT, NT - 1))
                    alone(sp, "x2_ready", done(h, q, 3, 2 * NT, 2 * NT - 1))
                    sp.dma_start(a0[1 - q].unsqueeze(2), a0_v[h * 2 + (q - 1)], allow_slow_non_contiguous=True
                                 ).then_inc(S[f"attrs_loaded_{1 - q}"], 16)
                if live(3):
                    alone(sp, "y_ready", done(h, q, 3, 1, 0))
                    sp.dma_start(out_v[h * 2 + (q - 3)], y_out).then_inc(S["out_stored"], 16)
                if live(-1):
                    alone(sp, "y_base_ready", done(h, q, 1, 1, 0))
                    sp.dma_start(x_in[1 - q], x_v[h * 2 + (q + 1)]).then_inc(S[f"nodes_loaded_{1 - q}"], 16)

            last_steps(sp, last_step)
            sp.wait_ge(S["out_stored"], 16 * NODE_GROUPS)

        @block.gpsimd
        def _(pool):
            nc.gpsimd.memset(ident[:, :], 0.0).then_inc(S["consts_made"], 1)
            nc.gpsimd.memset(minus_half[:, :], -0.5).then_inc(S["consts_made"], 1)
            nc.gpsimd.iota(node_i, pattern=[[P, NODE_TILES]], base=0, channel_multiplier=1).then_inc(
                S["consts_made"], 1)
            pool.wait_ge(S["consts_made"], 3)
            nc.gpsimd.affine_select(out=ident[:, :], in_=ident[:, :], compare_op=ALU.not_equal, fill=1.0, base=0,
                                    pattern=[[-1, 128]], channel_multiplier=1).then_inc(S["consts_made"], 1)
            barrier(pool, "prologue_over")

            def fetch_dst(h, q):
                alone(pool, "search_ready", done(h, q, 0, 2, 1))
                for t in range(NT):
                    nc.gpsimd.indirect_dma_start(
                        out=search_dst[q][:, t], out_offset=None, in_=dst_tiles,
                        in_offset=bass.IndirectOffsetOnAxis(ap=search_tile_i[q][:, t:t + 1], axis=0),
                    ).then_inc(S[f"search_loaded_{q}"], 16)


            def rstd(name, count, var, root, ready):
                alone(pool, name, count)
                nc.gpsimd.tensor_tensor(root, var, minus_half[:, 0:var.shape[1]], ALU.pow).then_inc(S[ready], 1)

            two_vars, two_roots = (ap.rearrange("p a b -> p (a b)") for ap in (x_var, x_rstd))

            def node_step(h, q, more):
                rstd("x_var_ready", done(h, q, 0, 1, 0), two_vars, two_roots, "x_rstd_ready")
                fetch_dst(h, q)

            node_groups(pool, node_step)
            for q in (0, 1):
                pool.wait_ge(S[f"search_loaded_{q}"], 16 * NT * (NODE_GROUPS // 2))
            barrier(pool, "node_pass_over")

            def step(h, q, live):
                if not live(0):
                    return
                alone(pool, "idx_ready", done(h, q, 0, 1, 0))
                alone(pool, "sum_ready", done(h, q, 2, G // 2, G // 2 - 1))
                for j in range(G):
                    for at, table_, got in ((0, src_table, got_s), (G, dst_table, got_d)):
                        nc.gpsimd.indirect_dma_start(
                            out=got[q][:, j], out_offset=None, in_=table_,
                            in_offset=bass.IndirectOffsetOnAxis(ap=idx[q][:, at + j:at + j + 1], axis=0),
                        ).then_inc(S[f"gathered_{q}"], 16)
                    if j in (3, 6):
                        alone(pool, "mlp_var_ready", done(h, q, 0, 2, j // 4))
                        nc.gpsimd.tensor_tensor(mlp_rstd, mlp_var, minus_half[:, 0:G], ALU.pow).then_inc(
                            S["mlp_rstd_ready"], 1)

            steps(pool, step)
            for q in (0, 1):
                pool.wait_ge(S[f"gathered_{q}"], 16 * 2 * G * (GROUPS // 2))
            barrier(pool, "edge_pass_over")
            barrier(pool, "carry_over")

            def fetch(h, q, ahead):
                r = (q + ahead) % 2
                alone(pool, "place_ready", done(h, q + ahead, 0, 3, 2))
                for t in range(NT):
                    for k, rows in enumerate((runs, carry)):
                        nc.gpsimd.indirect_dma_start(
                            out=pieces[r][:, k, t], out_offset=None, in_=rows,
                            in_offset=bass.IndirectOffsetOnAxis(ap=place[r][:, k, t:t + 1], axis=0),
                        ).then_inc(S[f"pieces_loaded_{r}"], 16)

            fetch(0, 0, 0)

            def last_step(h, q, live):
                if live(-1):
                    fetch(h, q, 1)
                if live(3):
                    rstd("y_var_ready", done(h, q, 3, 1, 0), y_var, y_rstd, "y_rstd_ready")
                if live(1):
                    rstd("x1_var_ready", done(h, q, 1, 1, 0), two_vars, two_roots, "x1_rstd_ready")

            last_steps(pool, last_step)
            for q in (0, 1):
                pool.wait_ge(S[f"pieces_loaded_{q}"], PIECES * (NODE_GROUPS // 2))

        @block.scalar
        def _(act):
            act.wait_ge(S["vec_step"], 3)
            nc.scalar.activation(vec_root, vec_n2, ACT.Sqrt).then_inc(S["vec_root"], 1)
            barrier(act, "prologue_over")

            def affine(bank, u, w, turned, count, scaled):
                wait(act, turned, count)
                nc.scalar.activation(tile_s[0:C0, u], bank[0:C0, 0:P], ACT.Identity, bias=w[0:C0, 1:2],
                                     scale=w[0:C0, 0:1]).then_inc(S[scaled], 1)
                nc.scalar.activation(tile_v[0:CV, u, 0], bank[0:CV, P:2 * P], ACT.Copy,
                                     scale=w[0:CV, 2:3]).then_inc(S[scaled], 1)

            def node_step(h, q, more):
                for t in range(NT + 1):
                    if t < NT:
                        wait(act, "node_projected", done(h, q, 0, NT, t, back=2))
                        u = (q * NT + t) % 2
                        affine(PT[u], u, ln1, "node_turned", done(h, q, 0, NT, t), "affine_ready")
                    if t == 1:
                        wait(act, f"stored_{q}", turn(h, q, 2, 32))
                    if t > 0:
                        wait(act, "node_projected", done(h, q, 0, NT, t - 1))
                        nc.scalar.copy(table[q][:, t - 1], PL[(q * NT + t - 1) % 2][0:P, 0:2 * C]).then_inc(
                            S["table_ready"], 1)

            node_groups(act, node_step)
            barrier(act, "node_pass_over")

            def step(h, q, live):
                for j in range(G):
                    if live(0) and j == 0:
                        wait(act, "mlp_out", done(h, q, 1, 2, 0))
                        wait(act, "es_turned", done(h, q, 0, 1, 0))
                        nc.scalar.copy(es_t, PM[:, 0:4 * P].rearrange("p (a e) -> p a e", a=4)).then_inc(
                            S["es_copied"], 1)
                    if live(0) and j in (1, 4):
                        wait(act, "mlp_ss_ready", done(h, q, 0, 2, j // 4, back=1))
                        wait(act, "mlp_out", done(h, q, 0, 2, j // 4))
                        nc.scalar.activation(mlp_sq, PM[0:P, :].rearrange("p (t c) -> p t c", t=G),
                                             ACT.Square).then_inc(S["mlp_squared"], 1)
                    if live(0) and j == 3:
                        k = j // 6
                        wait(act, "mlp_h_ready", done(h, q, 0, 2, k, back=1))
                        wait(act, "mlp_turned", done(h, q, 0, 2, k))
                        turned = PM[:, 0:4 * P].rearrange("p (a e) -> p a e", a=4)
                        nc.scalar.activation(mlp_tanh, turned, ACT.Tanh, bias=mlp_affine[:, 5 + 2 * k:6 + 2 * k],
                                             scale=mlp_affine[:, 4 + 2 * k:5 + 2 * k]).then_inc(S["mlp_act_ready"], 1)
                        nc.scalar.activation(mlp_y, turned, ACT.Identity, bias=mlp_affine[:, 1 + 2 * k:2 + 2 * k],
                                             scale=mlp_affine[:, 2 * k:1 + 2 * k]).then_inc(S["mlp_act_ready"], 1)
                    lag, k = behind(j, LAG_SUM)
                    if live(lag) and k % 2 == 1:
                        r = (q - lag) % 2
                        if k == 1:
                            wait(act, f"rows_stored_{r}", turn(h, q, lag + 2))
                        wait(act, "sums_ready", done(h, q, lag, G, k))
                        nc.scalar.copy(run_rows[r][:, k - 1:k + 1, 0:SUMS],
                                       PO[0:P, 0:2 * SUMS].rearrange("p (t c) -> p t c", t=2)).then_inc(
                            S["rows_ready"], 1)
                    lag, k = behind(j, LAG_T)
                    if live(lag):
                        wait(act, "lin_ready", done(h, q, lag, G, k, back=2))
                        wait(act, "prods_turned", done(h, q, lag, G, k))
                        nc.scalar.copy(prod_t[k % 2], PT[k % 2][:, 0:4 * P].rearrange("p (a e) -> p a e", a=4)
                                       ).then_inc(S["prods_copied"], 1)
                    if live(0) and j == 6:
                        k = j // 6
                        wait(act, "mlp_h_ready", done(h, q, 0, 2, k, back=1))
                        wait(act, "mlp_turned", done(h, q, 0, 2, k))
                        turned = PM[:, 0:4 * P].rearrange("p (a e) -> p a e", a=4)
                        nc.scalar.activation(mlp_tanh, turned, ACT.Tanh, bias=mlp_affine[:, 5 + 2 * k:6 + 2 * k],
                                             scale=mlp_affine[:, 4 + 2 * k:5 + 2 * k]).then_inc(S["mlp_act_ready"], 1)
                        nc.scalar.activation(mlp_y, turned, ACT.Identity, bias=mlp_affine[:, 1 + 2 * k:2 + 2 * k],
                                             scale=mlp_affine[:, 2 * k:1 + 2 * k]).then_inc(S["mlp_act_ready"], 1)
                    lag, k = behind(j, LAG_LIN)
                    if live(lag):
                        wait(act, "att_u_ready", done(h, q, lag, G // 2, k // 2, back=2))
                        wait(act, "lin_ready", done(h, q, lag, G, k))
                        nc.scalar.activation(att_tanh[k // 2 % 2][:, k % 2], PL[k % 2][0:P, 0:64], ACT.Tanh, scale=0.5).then_inc(
                            S["att_tanh_ready"], 1)
                        wait(act, "pay_ready", done(h, q, lag + 2, G, 2 * (k // 2) + 1))
                        nc.scalar.copy(msg[(q - lag) % 2][:, k], PL[k % 2][0:P, 64:LIN]).then_inc(S["msg_ready"], 1)
                    if live(2) and j == 6:
                        wait(act, "pay_ready", done(h, q, 4, G, G - 1))
                        wait(act, "logit_d_ready", done(h, q, 2, 1, 0))
                        nc.scalar.activation(prob[q], logit_d, ACT.Exp).then_inc(S["prob_ready"], 1)

            steps(act, step)
            barrier(act, "edge_pass_over")

            act.wait_ge(S["carry_exp_in"], 2)
            nc.scalar.activation(keep, step_m, ACT.Exp).then_inc(S["carry_exp"], 1)
            nc.scalar.activation(take, chan_d, ACT.Exp).then_inc(S["carry_exp"], 1)
            barrier(act, "carry_over")

            def last_step(h, q, live):
                if live(0):
                    wait(act, "merge_in", done(h, q, 0, 1, 0))
                    nc.scalar.activation(piece_e, piece_d, ACT.Exp).then_inc(S["merge_exp"], 1)
                if live(3):
                    for t in range(NT):
                        bank, u = PT[(q + t) % 2], ((q - 3) * NT + t) % 2
                        wait(act, "f2_ready", done(h, q, 3, NT, t, back=2))
                        wait(act, "ff_turned", done(h, q, 3, NT, t))
                        nc.scalar.copy(ff_st[:, u], bank[:, 0:P]).then_inc(S["ff_copied"], 1)
                        nc.scalar.copy(ff_vt[:, u], bank[0:CV, P:3 * P].rearrange("p (a e) -> p a e", a=2)).then_inc(
                            S["ff_copied"], 1)
                if live(1):
                    for t in range(NT):
                        bank, u = PT[(q + NT + t) % 2], ((q - 1) * NT + t) % 2
                        wait(act, "projected", done(h, q, 1, NT, t, back=2))
                        wait(act, "agg_turned", done(h, q, 1, NT, t))
                        nc.scalar.copy(agg_s[:, u], bank[0:C0, 0:P]).then_inc(S["agg_copied"], 1)
                        nc.scalar.copy(agg_v[:, u], bank[0:CV, P:2 * P]).then_inc(S["agg_copied"], 1)
                if live(2):
                    for t in range(NT + 1):
                        if t < NT:
                            u = (q * NT + t) % 2
                            wait(act, "f1_ready", done(h, q, 2, NT, t, back=2))
                            affine(PT[(q + t) % 2], u, ln2, "norm_turned", done(h, q, 2, NT, t), "norm_scaled")
                        if t > 0:
                            u = (q * NT + t - 1) % 2
                            if t == 1:
                                wait(act, f"attrs_loaded_{q}", turn(h, q, 2))
                            wait(act, "ff_ready", done(h, q, 2, 2 * NT, 2 * (t - 1) + 1, back=4))
                            wait(act, "f1_ready", done(h, q, 2, NT, t - 1))
                            nc.scalar.activation(ff_g[:, u], PL[u][0:P, 0:384], ACT.Copy,
                                                 scale=a0[q][:, t - 1:t]).then_inc(S["ff_scaled"], 1)
                            wait(act, "ff_scaled", done(h, q, 2, NT, t - 1))
                            nc.scalar.activation(ff_t[:, u], ff_g[:, u, 0:192], ACT.Tanh, scale=0.5).then_inc(
                                S["ff_tanh"], 1)

            last_steps(act, last_step)

        @block.tensor
        def _(pe):
            def mm(o, lhs_t, rhs, start=False, stop=False):
                return nc.tensor.matmul(o, lhs_t, rhs, start=start, stop=stop)

            def turn_tile(o, i, n):
                return nc.tensor.transpose(o, i, ident[0:n, 0:n])

            def bias(o, at, n, stop=False):
                return mm(o, ones3[:, 0:P], bias3[:, at:at + n], start=True, stop=stop)

            pe.wait_ge(S["consts_made"], 4)
            pe.wait_ge(S["nat_cast"], 2)
            for c in range(6):
                for b in range(4):
                    k = (c % 2) * 4 + b
                    nat = nat_f[:, c // 2, k] if c < 4 else spread(nat_f[:, 1, k, 0:1], 2, P)[:, 0, :]
                    turned = turn_tile(ps[c][0:P, 100 * b:100 * b + 100], nat, 100)
                turned.then_inc(S["cols_turned"], 1)
            pe.wait_ge(S["nat_loaded"], 48)
            for c in range(6):
                bank = ps[(6 + c) % 8]
                if c >= 2:
                    pe.wait_ge(S["cols_kept"], (1, 2, 5, 6)[c - 2])
                for b in range(4):
                    turned = turn_tile(bank[0:P, 100 * b:100 * b + 100], nat_v[:, (c % 2) * 4 + b, :, c // 2], 100)
                turned.then_inc(S["cols_turned"], 1)
            pe.wait_ge(S["bias_moved"], 48)
            pe.wait_ge(S["weight_step"], WEIGHT_STEPS)
            barrier(pe, "prologue_over")

            def node_step(h, q, more):
                for t in range(NT + 1):
                    if t < NT:
                        u = (q * NT + t) % 2
                        if t == 0:
                            wait(pe, "x_norm_ready", done(h, q, 0, 1, 0))
                        turn_tile(PT[u][0:CV, P:2 * P], x_norm[q][:, t, C0:C], P)
                        turn_tile(PT[u][0:C0, 0:P], x_norm[q][:, t, 0:C0], P).then_inc(S["node_turned"], 1)
                    if t > 0:
                        u = (q * NT + t - 1) % 2
                        wait(pe, "affine_ready", done(h, q, 0, 2 * NT, 2 * t - 1))
                        wait(pe, "table_ready", done(h, q, 0, NT, t - 1, back=2))
                        o = PL[u][0:P, :]
                        bias(o[:, 0:2 * C], B_NODE, 2 * C)
                        both = o[:, 0:2 * C].rearrange("p (a c) -> p a c", a=2)
                        mm(both[:, :, 0:C0], tile_s[0:C0, u], w_node_s[:, :].rearrange("p (a c) -> p a c", a=2))
                        mm(both[:, :, C0:C], tile_v[0:CV, u, 0], w_node_v[:, :].rearrange("p (a c) -> p a c", a=2),
                           stop=True).then_inc(S["node_projected"], 1)

            node_groups(pe, node_step)
            barrier(pe, "node_pass_over")

            def mlp(h, q, k, j):
                src = es_t if k == 0 else h1_t
                if k == 0:
                    wait(pe, "es_copied", done(h, q, 0, 1, 0))
                else:
                    wait(pe, "mlp_h_ready", done(h, q, 0, 2, 0))
                wait(pe, "mlp_n_ready", done(h, q, 0, 2, k, back=1))
                bias(PM[0:P, :], (B_MLP1, B_MLP2)[k], 64 * G)
                for a in range(G // 2):
                    last_mm = mm(PM[0:P, 128 * a:128 * a + 128], src[:, a], w_mlp[:, k], stop=a == G // 2 - 1)
                last_mm.then_inc(S["mlp_out"], 1)

            def step(h, q, live):
                for j in range(G):
                    if live(0) and j == 0:
                        wait(pe, "mlp_act_ready", done(h, q, 1, 4, 3))
                        wait(pe, f"es_loaded_{q}", turn(h, q, 0))
                        for a in range(4):
                            turned = turn_tile(PM[:, P * a:P * a + P],
                                               es_in[q][:, 2 * a:2 * a + 2].rearrange("p t c -> p (t c)"), P)
                        turned.then_inc(S["es_turned"], 1)
                    if live(0) and j == 1:
                        mlp(h, q, 0, j)
                    if live(0) and j == 3:
                        k = 0
                        wait(pe, "mlp_n_ready", done(h, q, 0, 2, k))
                        if k == 0:
                            wait(pe, "es_copied", done(h, q, 0, 1, 0))
                        else:
                            wait(pe, "mlp_act_ready", done(h, q, 0, 4, 1))
                        for a in range(4):
                            turned = turn_tile(PM[:, P * a:P * a + P],
                                               mlp_n[:, 2 * a:2 * a + 2].rearrange("p t c -> p (t c)"), P)
                        turned.then_inc(S["mlp_turned"], 1)
                    if live(1) and j % 2 == 0:
                        r = 1 - q
                        wait(pe, "prods_ready", done(h, q, 1, 2 * G, 2 * j - 1))
                        wait(pe, "mlp_h_ready", done(h, q, 1, 2, 1))
                        bias(PW[0:P, 0:2 * W_TILE], B_W, 2 * W_TILE)
                        last_mm = mm(PW[0:P, 0:2 * W_TILE], h2_t[r][:, j // 2], w3[:, :], stop=True)
                        last_mm.then_inc(S["w_ready"], 1)
                    if live(2) and j == 4:
                        wait(pe, "logits_ready", done(h, q, 2, G // 2, G // 2 - 1))
                        wait(pe, "logit_d_ready", done(h, q, 3, 1, 0))
                        alone(pe, "max_kept", done(h, q, 3, 2, 1))
                        turn_tile(run_t, logit[q].rearrange("p t h -> p (t h)"), P).then_inc(S["logits_turned"], 1)
                    if live(0) and j == 4:
                        mlp(h, q, 1, j)
                    lag, k = behind(j, LAG_SUM)
                    if live(lag):
                        u = k % 2
                        r = k // 2 % 2
                        wait(pe, "eq_ready", done(h, q, lag, G // 2, k // 2))
                        wait(pe, "pay_ready", done(h, q, lag, G, 2 * (k // 2) + 1))
                        if u == 0:
                            wait(pe, "rows_ready", done(h, q, lag, G // 2, k // 2 - 1))
                        o = PO[0:P, SUMS * u:SUMS * (u + 1)]
                        mm(o, eq[r][:, u], pay[r][:, u, 0:SUMS], start=True)
                        mm(o[:, SUMS - CV:SUMS], eq[r][:, u], pay[r][:, u, SUMS:PAY], stop=True).then_inc(
                            S["sums_ready"], 1)
                    lag, k = behind(j, LAG_T)
                    if live(lag):
                        wait(pe, "prods_ready", done(h, q, lag, 2 * G, 4 * (k // 2) + 3))
                        wait(pe, "prods_copied", done(h, q, lag, G, k, back=2))
                        for a in range(4):
                            turned = turn_tile(PT[k % 2][:, P * a:P * a + P],
                                               prod[(k // 2) % 2][:, k % 2, 128 * a:128 * a + 128], P)
                        turned.then_inc(S["prods_turned"], 1)
                    if live(0) and j == 6:
                        k = 1
                        wait(pe, "mlp_n_ready", done(h, q, 0, 2, k))
                        if k == 0:
                            wait(pe, "es_copied", done(h, q, 0, 1, 0))
                        else:
                            wait(pe, "mlp_act_ready", done(h, q, 0, 4, 1))
                        for a in range(4):
                            turned = turn_tile(PM[:, P * a:P * a + P],
                                               mlp_n[:, 2 * a:2 * a + 2].rearrange("p t c -> p (t c)"), P)
                        turned.then_inc(S["mlp_turned"], 1)
                    lag, k = behind(j, LAG_LIN)
                    if live(lag):
                        u = k % 2
                        wait(pe, "prods_copied", done(h, q, lag, G, k))
                        wait(pe, "msg_ready", done(h, q, lag, G, k, back=2))
                        o = PL[u][0:P, :]
                        mm(o[:, 0:LIN_S], prod_t[u][:, 0], w_lin[:, :], start=True)
                        mm(o[:, LIN_S:LIN], prod_t[u][:, 1], w_rest[:, 0])
                        mm(o[:, LIN_S:LIN], prod_t[u][:, 2], w_rest[:, 1])
                        mm(o[:, LIN_S:LIN], prod_t[u][:, 3], w_rest[:, 2], stop=True).then_inc(S["lin_ready"], 1)
                    if live(2) and j == 5:
                        alone(pe, "max_ready", done(h, q, 2, 1, 0))
                        turn_tile(run_b, run_max, G * H).then_inc(S["max_turned"], 1)

            steps(pe, step)
            barrier(pe, "edge_pass_over")

            pe.wait_ge(S["last_loaded"], 16)
            pe.wait_ge(S["last_spread"], 1)
            for b in range(K // 4):
                for k in range(4):
                    cols = slice(100 * k, 100 * k + 100)
                    rows = last[:, 4 * b + k]
                    turn_tile(ps[b][0:HALF, cols], rows[:, 0:HALF], 100)
                    turn_tile(ps[2 + b][0:SUMS - HALF, cols], rows[:, HALF:SUMS], 100)
                    turn_tile(ps[4 + b][0:HALF, cols], last_max[:, 4 * b + k], 100)
                    turned = turn_tile(ps[6 + b][0:HALF, cols], spread(rows[:, R_DST:R_DST + 1], 2, HALF)[:, 0, :], 100)
                turned.then_inc(S["last_turned"], 1)
            pe.wait_ge(S["carry_done"], 1)
            for k in range(K):
                o = ps[k]
                col = scan_x.rearrange("p x (a k) -> p x k a", k=K)[:, :, k]
                turn_tile(o[0:100, 0:HALF], col[:, 0], HALF)
                turn_tile(o[0:100, HALF:SUMS], col[0:SUMS - HALF, 1], SUMS - HALF)
                turn_tile(o[0:100, R_MAX:R_MAX + H], scan_m[0:H].rearrange("p (a k) -> p k a", k=K)[:, k], H).then_inc(S["carry_turned"], 1)
            barrier(pe, "carry_over")

            def last_step(h, q, live):
                def rounds(lag, turn_in, product):
                    for t in range(NT + 1):
                        if t < NT:
                            turn_in(t)
                        if t > 0:
                            product(t - 1, ((q - lag) * NT + t - 1) % 2)

                def turn_ff(t):
                    bank = PT[(q + t) % 2]
                    wait(pe, "ff_ready", done(h, q, 3, 2 * NT, 2 * t + 1))
                    turn_tile(bank[:, 0:P], ff_s[:, t], P)
                    turn_tile(bank[0:CV, P:2 * P], ff_v[:, t, 0:CV], P)
                    turn_tile(bank[0:CV, 2 * P:3 * P], ff_v[:, t, CV:2 * CV], P).then_inc(S["ff_turned"], 1)

                def f2(t, u):
                    wait(pe, "ff_copied", done(h, q, 3, 2 * NT, 2 * t + 1))
                    wait(pe, "x2_ready", done(h, q, 3, 2 * NT, 2 * t + 1, back=4))
                    o = (PW, PO)[u][0:P, 0:C]
                    bias(o, B_F2, C)
                    mm(o[:, 0:C0], ff_st[:, u], w_f2_s[:, :])
                    mm(o[:, C0:C], ff_vt[:, u, 0], w_f2_v[:, 0])
                    mm(o[:, C0:C], ff_vt[:, u, 1], w_f2_v[:, 1], stop=True).then_inc(S["f2_ready"], 1)

                def turn_agg(t):
                    bank = PT[(q + NT + t) % 2]
                    if t == 0:
                        wait(pe, "agg_ready", done(h, q, 1, 1, 0))
                    turn_tile(bank[0:CV, P:2 * P], agg[1 - q][:, t, H + C0:SUMS], P)
                    turn_tile(bank[0:C0, 0:P], agg[1 - q][:, t, H:H + C0], P).then_inc(S["agg_turned"], 1)

                def project(t, u):
                    wait(pe, "agg_copied", done(h, q, 1, 2 * NT, 2 * t + 1))
                    wait(pe, "x1_ready", done(h, q, 1, 2 * NT, 2 * t + 1, back=4))
                    o = (PM, PR)[u][0:P, :]
                    bias(o[:, 0:C], B_PROJ, C)
                    mm(o[:, 0:C0], agg_s[:, u], w_proj_s[:, :])
                    mm(o[:, C0:C], agg_v[:, u], w_proj_v[:, :], stop=True).then_inc(S["projected"], 1)

                def turn_norm(t):
                    bank = PT[(q + t) % 2]
                    if t == 0:
                        wait(pe, "x1_norm_ready", done(h, q, 2, 1, 0))
                        wait(pe, "x1_step", done(h, q, 2, NORM_STEPS, NORM_STEPS - 1))
                    turn_tile(bank[0:CV, P:2 * P], x_norm[q][:, t, C0:C], P)
                    turn_tile(bank[0:C0, 0:P], x_norm[q][:, t, 0:C0], P).then_inc(S["norm_turned"], 1)

                def f1(t, u):
                    wait(pe, "norm_scaled", done(h, q, 2, 2 * NT, 2 * t + 1))
                    wait(pe, "ff_scaled", done(h, q, 2, NT, t, back=2))
                    o = PL[u][0:P, :]
                    bias(o[:, 0:192], B_F1, 192)
                    mm(o[:, 0:192], tile_s[0:C0, u], w_f1_s[:, :], stop=True)
                    mm(o[:, 192:384], tile_v[0:CV, u, 0], w_f1_v[:, :], start=True, stop=True).then_inc(
                        S["f1_ready"], 1)

                if live(3):
                    rounds(3, turn_ff, f2)
                if live(1):
                    rounds(1, turn_agg, project)
                if live(2):
                    rounds(2, turn_norm, f1)

            last_steps(pe, last_step)

        @block.vector
        def _(dve):
            v = nc.vector

            def chain(name):
                count = [0]

                def link(ins):
                    count[0] += 1
                    ins.then_inc(S[name], 1)
                    dve.wait_ge(S[name], count[0])
                return link

            for tile_ in ZERO_TILES:
                v.memset(tile_, 0.0).then_inc(S["zeroed"], 1)
            v.memset(ones3[:, :], 1.0).then_inc(S["zeroed"], 1)
            dve.wait_ge(S["nat_loaded"], 48)
            v.tensor_copy(nat_f[:, 1], nat_i[:, 1]).then_inc(S["nat_cast"], 1)
            v.tensor_copy(nat_f[:, 0], nat_i[:, 0]).then_inc(S["nat_cast"], 1)

            def cols(bank):
                return bank[0:P, 0:400].rearrange("p (k a) -> p a k", k=4)

            for c in range(4):
                dve.wait_ge(S["cols_turned"], c + 1)
                at = c * 4
                last_ins = v.tensor_copy(idx_all[:, :, at:at + 4], cols(ps[c]))
                last_ins.then_inc(S["cols_kept"], 1)
            for c in (2, 3):
                v.tensor_copy(dst_all[:, :, 4 * (c - 2):4 * (c - 2) + 4], cols(ps[c])).then_inc(S["cols_kept"], 1)
            for c in (4, 5):
                dve.wait_ge(S["cols_turned"], c + 1)
                v.tensor_copy(first_dst[:, 400 * (c - 4):400 * (c - 4) + 400], ps[c][0:P, 0:400]).then_inc(
                    S["cols_kept"], 1)
            for c in range(6):
                dve.wait_ge(S["cols_turned"], 6 + c + 1)
                k = (c % 2) * 4
                v.tensor_copy(vec_all[:, :, k:k + 4, c // 2], cols(ps[(6 + c) % 8])).then_inc(S["cols_kept"], 1)

            dve.wait_ge(S["cols_kept"], 14)
            flat = vec_all.rearrange("p g t c -> p (g t) c")
            v.tensor_tensor(vec_sq, flat, flat, ALU.mult).then_inc(S["vec_step"], 1)
            dve.wait_ge(S["vec_step"], 1)
            v.tensor_reduce(vec_n2, vec_sq, AX.X, ALU.add).then_inc(S["vec_step"], 1)
            dve.wait_ge(S["vec_step"], 2)
            v.tensor_scalar(vec_n2, vec_n2, 1e-12, None, ALU.add).then_inc(S["vec_step"], 1)
            dve.wait_ge(S["consts_made"], 4)
            v.tensor_copy(node_all[:, :], node_i).then_inc(S["vec_step"], 1)
            dve.wait_ge(S["vec_step"], 4)
            dve.wait_ge(S["vec_root"], 1)
            unit = chain("vec_unit")
            unit(v.reciprocal(vec_inv, vec_root))
            unit(v.tensor_tensor(vec_root, vec_inv, vec_inv, ALU.mult))
            unit(v.tensor_tensor(vec_root, vec_root, vec_n2, ALU.mult))
            unit(v.tensor_scalar(vec_root, vec_root, -0.5, 1.5, ALU.mult, ALU.add))
            unit(v.tensor_tensor(vec_inv, vec_inv, vec_root, ALU.mult))
            rh = rhat_all[:, :, :, :].rearrange("p g t c -> p (g t) c")
            v.tensor_tensor(rh[:, :, 0:3], flat, spread(vec_inv, 2, 3), ALU.mult).then_inc(S["vec_step"], 1)
            dve.wait_ge(S["vec_step"], 5)
            v.tensor_copy(rh[:, :, 3:4], rh[:, :, 0:1]).then_inc(S["vec_step"], 1)
            v.tensor_scalar(rh[:, :, 4:5], rh[:, :, 2:3], -1.0, None, ALU.mult).then_inc(S["vec_step"], 1)
            v.tensor_scalar(rh[:, :, 5:7], rh[:, :, 0:2], -1.0, None, ALU.mult).then_inc(S["vec_step"], 1)
            dve.wait_ge(S["vec_step"], 8)

            def count_tiles(h, q, before):
                links = [0]
                group = bass.ds(h * (2 * NT) + q * NT, NT)

                def link(ins):
                    links[0] += 1
                    ins.then_inc(S["count_step"], 1)
                    wait(dve, "count_step", h * (2 * COUNT_STEPS) + (before * COUNT_STEPS + links[0]))

                link(v.tensor_copy(count_node, node_all[:, group]))
                for t in range(NT):
                    link(v.tensor_scalar(search_junk, first_dst, count_node[:, t:t + 1], None, ALU.is_le, ALU.add,
                                         accum_out=search_cnt[:, t:t + 1]))
                v.tensor_scalar(place_all[:, 1, group], search_cnt, -1.0, 0.0, ALU.add, ALU.max).then_inc(
                    S["count_step"], 1)
                alone(dve, "count_step", h * (2 * COUNT_STEPS) + (before * COUNT_STEPS + COUNT_STEPS))
                assert links[0] == COUNT_STEPS - 1, links[0]

            dve.wait_ge(S["vec_step"], 4)
            for n, (h, q) in enumerate(EARLY):
                count_tiles(h, q, n - 2 * h)

            dve.wait_ge(S["weights_loaded"], 16 * LOADS)
            link = chain("weight_step")
            link(v.tensor_reduce(mlp_mean, w_mlp[:, :, :], AX.X, ALU.add))
            link(v.tensor_scalar(mlp_mean, mlp_mean, 1.0 / 64, None, ALU.mult))
            for rows in (slice(0, 64), slice(64, 128)):
                link(v.tensor_tensor(w_mlp[rows, :, rows], w_mlp[rows, :, rows], spread(mlp_mean[rows], 2, 64),
                                     ALU.subtract))
            link(v.tensor_scalar(w_mlp[:, 1], w_mlp[:, 1], 0.5, None, ALU.mult))
            link(v.tensor_scalar(w3[:, :], w3_raw, 0.5, None, ALU.mult))
            link(v.tensor_scalar(w_f2_s[:, :], w_f2_s[:, :], 0.5, None, ALU.mult))
            link(v.tensor_scalar(w_f2_v[:, :, :], w_f2_v[:, :, :], 0.5, None, ALU.mult))
            link(v.tensor_scalar(mlp_affine[:, 4:8], mlp_affine[:, 0:4], 0.5, None, ALU.mult))
            mlp_bias = bias_row[:, B_MLP1:B_W].rearrange("p (l t c) -> p l t c", l=2, t=G)
            link(v.tensor_reduce(bias_mean, mlp_bias, AX.X, ALU.add))
            link(v.tensor_scalar(bias_mean, bias_mean, 1.0 / 64, None, ALU.mult))
            for l in (0, 1):
                link(v.tensor_tensor(mlp_bias[:, l], mlp_bias[:, l], spread(bias_mean[:, l], 2, 64), ALU.subtract))
            link(v.tensor_copy(w_lin[0:CV + 1, 0:64], lin_raw[:, 0:64]))
            link(v.scalar_tensor_tensor(w_lin[0:CV + 1, 64:128], lin_raw[:, 0:64], 0.4, adot, ALU.mult, ALU.mult))
            link(v.memset(w_lin[ONE:ONE + 1, 128:128 + H], 1.0))
            link(v.tensor_copy(w_lin[0:CV + 1, 128 + H:LIN_S].rearrange("p (k h) -> p k h", k=8),
                               lin_raw[:, 64:128].rearrange("p (h k) -> p k h", h=H)))
            for at, lo, hi, col, factor in REST_BLOCKS:
                rows = slice(at % 128, at % 128 + hi - lo)
                link(v.tensor_scalar(w_rest[rows, at // 128, col:col + C1].rearrange("p (k h) -> p k h", k=4),
                                     raw_rest[rows, at // 128].rearrange("p (h k) -> p k h", h=H),
                                     factor, None, ALU.mult))
            link(v.tensor_copy(bias_parts[:, 0], bias_row))
            link(v.tensor_tensor(bias_rest, bias_row, bias_parts[:, 0], ALU.subtract))
            link(v.tensor_copy(bias_parts[:, 1], bias_rest))
            link(v.tensor_tensor(bias_row, bias_rest, bias_parts[:, 1], ALU.subtract))
            link(v.tensor_copy(bias_parts[:, 2], bias_row))
            barrier(dve, "prologue_over")

            def by_component(ap):
                return ap.rearrange("p t (u d) -> p t d u", d=3)

            def normed(link, x, o, var_ready, count, rstd_ready, last_link, meanwhile=lambda: None):
                link(v.tensor_reduce(x_sum, x[:, :, 0:C0], AX.X, ALU.add))
                link(v.tensor_scalar(x_mean, x_sum, 1.0 / C0, None, ALU.mult))
                link(v.tensor_tensor(x_cen[:, :, 0:C0], x[:, :, 0:C0], spread(x_mean, 2, C0), ALU.subtract))
                link(v.tensor_tensor(x_sq[:, :, 0:C0], x_cen[:, :, 0:C0], x_cen[:, :, 0:C0], ALU.mult))
                link(v.tensor_tensor(x_sq[:, :, C0:C], x[:, :, C0:C], x[:, :, C0:C], ALU.mult))
                link(v.tensor_reduce(x_ss[:, 0], x_sq[:, :, 0:C0], AX.X, ALU.add))
                link(v.tensor_reduce(x_ss[:, 1], x_sq[:, :, C0:C], AX.X, ALU.add))
                link(v.tensor_scalar(x_var[:, 0], x_ss[:, 0], 1.0 / C0, EPS, ALU.mult, ALU.add))
                v.tensor_scalar(x_var[:, 1], x_ss[:, 1], 1.0 / CV, EPS, ALU.mult, ALU.add).then_inc(S[var_ready], 1)
                meanwhile()
                wait(dve, rstd_ready, count)
                link(v.tensor_tensor(o[:, :, 0:C0], x_cen[:, :, 0:C0], spread(x_rstd[:, 0], 2, C0), ALU.mult))
                last_link(v.tensor_tensor(o[:, :, C0:C].rearrange("p t (d u) -> p t d u", d=3),
                                          by_component(x[:, :, C0:C]),
                                          spread(spread(x_rstd[:, 1], 2, 3), 3, C1), ALU.mult))

            def find_place(h, q, ahead):
                r = (q + ahead) % 2
                links = [0]
                group = bass.ds(h * (2 * NT) + (q + ahead) * NT, NT)

                def link(ins):
                    links[0] += 1
                    ins.then_inc(S["place_step"], 1)
                    wait(dve, "place_step", h * (2 * PLACE_STEPS) + ((q + ahead) * PLACE_STEPS + links[0]))

                wait(dve, f"search_loaded_{r}", turn(h, q, -ahead, 16 * NT))
                link(v.tensor_tensor(search_le, search_dst[r], spread(search_node[r], 2, P), ALU.is_le))
                link(v.tensor_reduce(search_in, search_le, AX.X, ALU.add))
                link(v.scalar_tensor_tensor(search_row, place_all[:, 1, group], float(P), search_in, ALU.mult,
                                            ALU.add))
                link(v.tensor_scalar(place_all[:, 0, group], search_row, -1.0, 0.0, ALU.add, ALU.max))
                assert links[0] == PLACE_STEPS, links[0]

            def search(h, q):
                group = bass.ds(h * (2 * NT) + q * NT, NT)
                if not isinstance(h, int):
                    count_tiles(h, q, q + len(EARLY) - 2)
                v.tensor_copy(search_node[q], node_all[:, group]).then_inc(S["search_ready"], 1)
                v.tensor_copy(search_tile_i[q], place_all[:, 1, group]).then_inc(S["search_ready"], 1)
                dve.wait_ge(S["search_ready"], done(h, q, 0, 2, 1))

            def node_step(h, q, more):
                links = [0]

                def link(ins):
                    links[0] += 1
                    ins.then_inc(S["norm_step"], 1)
                    dve.wait_ge(S["norm_step"], h * (2 * NORM_STEPS) + (q * NORM_STEPS + links[0]))

                wait(dve, f"x_loaded_{q}", turn(h, q, 0))
                wait(dve, "node_turned", done(h, q, 2, NT, NT - 1))
                normed(link, x_in[q], x_norm[q], "x_var_ready", done(h, q, 0, 1, 0), "x_rstd_ready",
                       lambda ins: ins.then_inc(S["x_norm_ready"], 1), lambda: search(h, q))
                assert links[0] == NORM_STEPS, links[0]
                if not isinstance(h, int) or 2 * h + q > 0:
                    find_place(h, q, -1)

            node_groups(dve, node_step)
            find_place(NODE_GROUPS // 2 - 1, 1, 0)
            barrier(dve, "node_pass_over")

            v.memset(run_mask, -BIG).then_inc(S["edge_consts"], 1)
            for q in (0, 1):
                v.memset(prod[q], 0.0).then_inc(S["edge_consts"], 1)
            for q in (0, 1):
                v.memset(run_rows[q], 0.0).then_inc(S["edge_consts"], 1)

            dve.wait_ge(S["edge_consts"], 5)
            for q in (0, 1):
                v.memset(prod[q][:, :, ONE:ONE + 1], 1.0).then_inc(S["edge_consts"], 1)
            dve.wait_ge(S["edge_consts"], 7)
            v.tensor_copy(idx[0], idx_all[:, 0, :]).then_inc(S["idx_ready"], 1)

            def step(h, q, live):
                for j in range(G):
                    p = j // 2
                    if j == 0 and live(1):
                        r = 1 - q
                        wait(dve, "prob_r_ready", done(h, q, 3, 1, 0))
                        wait(dve, "dots_in", done(h, q, 3, G // 2, G // 2 - 1))
                        wait(dve, "prods_ready", done(h, q, 3, 2 * G, 2 * G - 1))
                        v.tensor_copy(rhat[r], rhat_all[:, one(h * 2 + (q - 1))].rearrange(
                            "p x t c -> p (x t) c")).then_inc(S["rhat_ready"], 1)
                    ea = live(1)
                    r = 1 - q
                    pair = slice(2 * p, 2 * p + 2)
                    mv = feat[:, :, C0:C]
                    if ea and j % 2 == 0:
                        if p == 0:
                            wait(dve, f"gathered_{r}", turn(h, q, 1, 16 * 2 * G))
                        wait(dve, "prods_ready", done(h, q, 1, 2 * G, 4 * p - 1))
                        wait(dve, "dots_in", done(h, q, 1, G // 2, p - 1))
                        v.tensor_tensor(feat[:, :, 0:C], got_s[r][:, pair], got_d[r][:, pair], ALU.add).then_inc(
                            S["sum_ready"], 1)
                    plag, pk = behind(j, LAG_PAY)
                    pr, pu = (q - plag) % 2, pk // 2 % 2
                    paying = live(plag) and pk % 2 == 0
                    pays = slice(pk, pk + 2)
                    if paying:
                        if pk == 0:
                            wait(dve, f"meta_loaded_{pr}", turn(h, q, plag, 32))
                            wait(dve, "cols_ready", done(h, q, plag, 1, 0))
                        wait(dve, "sums_ready", done(h, q, plag, G, pk + 1, back=4))
                        v.tensor_tensor(eq[pu], dst_row[pr][:, pays], spread(dst_col[pr][:, pays], 2, P),
                                        ALU.is_equal).then_inc(S["eq_ready"], 1)
                    if ea and j % 2 == 0:
                        if p == 0:
                            wait(dve, "rhat_ready", done(h, q, 1, 1, 0))
                        wait(dve, "sum_ready", done(h, q, 1, G // 2, p))
                        wait(dve, "dots_ready", done(h, q, 1, G // 2, p - 1))
                        v.tensor_tensor(dot_in.rearrange("p t (d u) -> p t d u", d=3),
                                        mv.rearrange("p t (d u) -> p t d u", d=3),
                                        spread(rhat[r][:, pair, 0:3], 3, C1), ALU.mult).then_inc(S["dots_in"], 1)
                    if paying:
                        if pk == 0:
                            wait(dve, "prob_r_ready", done(h, q, plag, 1, 0))
                            wait(dve, "prob_ready", done(h, q, plag, 1, 0))
                        wait(dve, "msg_ready", done(h, q, plag, G, pk + 1))
                        v.tensor_tensor(pay[pu][:, :, 0:SUMS].rearrange("p t (k h) -> p t k h", h=H),
                                        msg[pr][:, pays, 64:64 + SUMS].rearrange("p t (k h) -> p t k h", h=H),
                                        spread(prob[pr][:, pays], 2, SUMS // H), ALU.mult).then_inc(S["pay_ready"], 1)
                    if ea and j % 2 == 0:
                        wait(dve, "dots_in", done(h, q, 1, G // 2, p))
                        v.tensor_reduce(feat[:, :, C:C + C1], dot_in.rearrange("p t (d u) -> p t u d", d=3), AX.X,
                                        ALU.add).then_inc(S["dots_ready"], 1)
                    if paying:
                        a = msg[pr][:, pays, 64 + SUMS:MSG].rearrange("p t (k h) -> p t k h", h=H)
                        v.tensor_tensor(pay[pu][:, :, SUMS:PAY].rearrange("p t (d k h) -> p t d k h", d=3, h=H),
                                        spread(a, 2, 3), spread(prob_r[pr][:, pays], 3, C1 // H),
                                        ALU.mult).then_inc(S["pay_ready"], 1)
                    if live(2) and j == 5:
                        wait(dve, "max_turned", done(h, q, 3, 1, 0))
                        wait(dve, "fwd_ready", done(h, q, 2, 1, 0))
                        v.tensor_tensor_scan(run_max[:, ::-1], run_mask[:, 1:P + 1][:, ::-1], run_fwd[:, ::-1], 0.0,
                                             ALU.add, ALU.max).then_inc(S["max_ready"], 1)
                    if ea and j % 2 == 1:
                        w = PW[0:P, 0:2 * W_TILE].rearrange("p (t c) -> p t c", t=2)
                        o = prod[p % 2]
                        by_d = mv.rearrange("p t (d u) -> p t d u", d=3)
                        wait(dve, "dots_ready", done(h, q, 1, G // 2, p))
                        wait(dve, "prods_turned", done(h, q, 1, G, 2 * p + 1, back=4))
                        wait(dve, "w_ready", done(h, q, 1, G // 2, p))
                        v.tensor_tensor(prod_u.rearrange("p t (d u) -> p t d u", d=3),
                                        spread(w[:, :, 192:192 + C1], 2, 3), by_d, ALU.mult).then_inc(
                            S["cross_in"], 1)
                        v.tensor_tensor(
                            o[:, :, 0:2 * REST].rearrange("p t (a c) -> p t a c", a=2)[:, :, :, 0:C0],
                            w[:, :, 0:192].rearrange("p t (a c) -> p t a c", a=2)[:, :, :, 0:C0],
                            spread(feat[:, :, 0:C0], 2, 2), ALU.mult).then_inc(S["prods_ready"], 1)
                        v.tensor_tensor(o[:, :, C0:ONE], w[:, :, 64:96], feat[:, :, C:C + C1], ALU.mult).then_inc(
                            S["prods_ready"], 1)
                        v.tensor_tensor(o[:, :, REST + C0:REST + C].rearrange("p t (d u) -> p t d u", d=3),
                                        spread(w[:, :, 160:160 + C1], 2, 3), by_d, ALU.mult).then_inc(
                            S["prods_ready"], 1)
                    if ea and j % 2 == 1:
                        wait(dve, "cross_in", done(h, q, 1, G // 2, p))
                        v.tensor_tensor(
                            o[:, :, REST + C:REST + C + 2 * CV].rearrange("p t (x d u) -> p t x d u", x=2, d=3),
                            spread(prod_u.rearrange("p t (d u) -> p t d u", d=3), 2, 2),
                            spread(rhat[r][:, pair, 1:7].rearrange("p t (x d) -> p t x d", x=2), 4, C1),
                            ALU.mult).then_inc(S["prods_ready"], 1)
                    lag, k = behind(j, LAG_ATT)
                    if live(lag) and k % 2 == 1:
                        wait(dve, "logits_ready", done(h, q, lag, G // 2, k // 2, back=1))
                        wait(dve, "att_tanh_ready", done(h, q, lag, G, k))
                        wait(dve, "msg_ready", done(h, q, lag, G, k))
                        v.scalar_tensor_tensor(att_u, att_tanh[k // 2 % 2], 1.5,
                                               msg[(q - lag) % 2][:, k - 1:k + 1, 0:64],
                                               ALU.add, ALU.mult).then_inc(S["att_u_ready"], 1)
                    if j == 1 and live(-1):
                        wait(dve, f"gathered_{1 - q}", turn(h, q, 1, 16 * 2 * G))
                        v.tensor_copy(idx[1 - q], idx_all[:, one(h * 2 + (q + 1))].rearrange("p x t -> p (x t)")).then_inc(
                            S["idx_ready"], 1)
                    if live(0) and j in (1, 4):
                        k = j // 4
                        wait(dve, "mlp_var_ready", done(h, q, 0, 2, k, back=1))
                        wait(dve, "mlp_squared", done(h, q, 0, 2, k))
                        v.tensor_reduce(mlp_ss, mlp_sq, AX.X, ALU.add).then_inc(S["mlp_ss_ready"], 1)
                        wait(dve, "mlp_rstd_ready", done(h, q, 0, 2, k, back=1))
                        wait(dve, "mlp_ss_ready", done(h, q, 0, 2, k))
                        v.tensor_scalar(mlp_var, mlp_ss, 1.0 / 64, EPS, ALU.mult, ALU.add).then_inc(
                            S["mlp_var_ready"], 1)
                    if live(0) and j in (2, 5):
                        k = j // 5
                        wait(dve, "mlp_turned", done(h, q, 0, 2, k, back=1))
                        wait(dve, "mlp_rstd_ready", done(h, q, 0, 2, k))
                        v.tensor_tensor(mlp_n, PM[0:P, :].rearrange("p (t c) -> p t c", t=G), spread(mlp_rstd, 2, 64),
                                        ALU.mult).then_inc(S["mlp_n_ready"], 1)
                    if live(2) and j == 3:
                        wait(dve, "eq_ready", done(h, q, 4, G // 2, G // 2 - 1))
                        v.tensor_copy(dst_col[q], dst_all[:, one(h * 2 + (q - 2))].rearrange("p x t -> p (x t)")
                                      ).then_inc(S["cols_ready"], 1)
                        wait(dve, "mask_ready", done(h, q, 3, 1, 0))
                        wait(dve, f"meta_loaded_{q}", turn(h, q, 2, 32))
                        v.tensor_tensor(run_ne[:, 0:P - 1], dst_th[q][:, 1:P], dst_th[q][:, 0:P - 1],
                                        ALU.not_equal).then_inc(S["run_ne_ready"], 1)
                        wait(dve, "run_ne_ready", done(h, q, 2, 1, 0))
                        wait(dve, "max_ready", done(h, q, 3, 1, 0))
                        v.tensor_scalar(run_mask[:, 1:P], run_ne[:, 0:P - 1], -BIG, None, ALU.mult).then_inc(
                            S["mask_ready"], 1)
                    if live(0) and j in (3, 7):
                        k = j // 7
                        wait(dve, "mlp_act_ready", done(h, q, 0, 4, 2 * k + 1))
                        if k == 0:
                            wait(dve, "mlp_out", done(h, q, 1, 2, 1))
                        else:
                            wait(dve, "w_ready", done(h, q, 2, G // 2, G // 2 - 1))
                        v.scalar_tensor_tensor((h1_t, h2_t[q])[k], mlp_tanh, 1.0, mlp_y, ALU.add, ALU.mult).then_inc(
                            S["mlp_h_ready"], 1)
                    lag, k = behind(j, LAG_ATT)
                    if live(lag) and k % 2 == 1:
                        wait(dve, "att_u_ready", done(h, q, lag, G // 2, k // 2))
                        if k == 1:
                            wait(dve, "logit_d_ready", done(h, q, lag + 2, 1, 0))
                            wait(dve, "logits_turned", done(h, q, lag + 2, 1, 0))
                        v.tensor_reduce(logit[(q - lag) % 2][:, k - 1:k + 1],
                                        att_u.rearrange("p t (h k) -> p t h k", h=H),
                                        AX.X, ALU.add).then_inc(S["logits_ready"], 1)
                    if live(2) and j == 4:
                        wait(dve, "mask_ready", done(h, q, 2, 1, 0))
                        wait(dve, "max_ready", done(h, q, 3, 1, 0))
                        wait(dve, "logits_turned", done(h, q, 2, 1, 0))
                        v.tensor_tensor_scan(run_fwd, run_mask[:, 0:P], run_t, 0.0, ALU.add, ALU.max).then_inc(
                            S["fwd_ready"], 1)
                    if live(2) and j == 6:
                        wait(dve, "prob_ready", done(h, q, 3, 1, 0))
                        wait(dve, "max_turned", done(h, q, 2, 1, 0))
                        back = run_b.rearrange("p (t h) -> p t h", t=G)
                        v.tensor_tensor(logit_d, logit[q], back, ALU.subtract).then_inc(S["logit_d_ready"], 1)
                        wait(dve, f"rows_stored_{q}", turn(h, q, 4))
                        v.tensor_copy(run_rows[q][:, :, R_MAX:R_MAX + H], back).then_inc(S["max_kept"], 1)
                        wait(dve, "cols_ready", done(h, q, 2, 1, 0))
                        v.tensor_copy(run_rows[q][:, :, R_DST:R_DST + 1], dst_col[q].unsqueeze(2)).then_inc(
                            S["max_kept"], 1)
                    if live(2) and j == 7:
                        wait(dve, "pay_ready", done(h, q, 4, G, G - 1))
                        wait(dve, "prob_ready", done(h, q, 2, 1, 0))
                        v.tensor_tensor(prob_r[q], spread(prob[q], 2, 3), spread(rhat[q][:, :, 0:3], 3, H), ALU.mult).then_inc(
                            S["prob_r_ready"], 1)

            steps(dve, step)
            barrier(dve, "edge_pass_over")

            link = chain("carry_step")

            def by_tile(ap):
                return ap.rearrange("p (a k) -> p a k", k=K)

            dve.wait_ge(S["last_loaded"], 16)
            v.tensor_copy(last_max.rearrange("p t (k h) -> p t k h", h=H),
                          spread(last[:, :, R_MAX:R_MAX + H], 2, HALF // H)).then_inc(S["last_spread"], 1)
            for b in range(2):
                dve.wait_ge(S["last_turned"], b + 1)
                for o, bank, n in ((chan[:, 0], ps[b], HALF), (chan[:, 1], ps[2 + b], SUMS - HALF),
                                   (chan_m, ps[4 + b], HALF), (chan_d, ps[6 + b], HALF)):
                    link(v.tensor_copy(by_tile(o[0:n])[:, :, 4 * b:4 * b + 4],
                                       bank[0:n, 0:400].rearrange("p (k a) -> p a k", k=4)))
            link(v.memset(same[:, 0:1], 0.0))
            link(v.memset(step_m[:, 0:1], 0.0))
            link(v.tensor_tensor(same[:, 1:], chan_d[:, 1:], chan_d[:, 0:TILES - 1], ALU.is_equal))
            link(v.tensor_scalar(restart, same, BIG, -BIG, ALU.mult, ALU.add))
            link(v.tensor_tensor_scan(scan_m, restart, chan_m, 0.0, ALU.add, ALU.max))
            link(v.tensor_tensor(step_m[:, 1:], scan_m[:, 0:TILES - 1], scan_m[:, 1:], ALU.subtract))
            link(v.tensor_scalar(step_m, step_m, 0.0, None, ALU.min))
            v.tensor_copy(chan_x[:, 0], chan[:, 0]).then_inc(S["carry_exp_in"], 1)
            v.tensor_tensor(chan_d, chan_m, scan_m, ALU.subtract).then_inc(S["carry_exp_in"], 1)
            dve.wait_ge(S["carry_exp"], 2)
            link(v.tensor_tensor(keep, keep, same, ALU.mult))
            link(v.tensor_tensor(chan_x[:, 0], chan[:, 0], take, ALU.mult))
            n = SUMS - HALF
            link(v.tensor_tensor(chan_x[0:n, 1], chan[0:n, 1], take[0:n], ALU.mult))
            link(v.tensor_tensor_scan(scan_x[:, 0], keep, chan_x[:, 0], 0.0, ALU.mult, ALU.add))
            link(v.memset(sentinel, 0.0))
            link(v.memset(sentinel[:, R_DST:R_DST + 1], -1.0))
            v.tensor_tensor_scan(scan_x[0:n, 1], keep[0:n], chan_x[0:n, 1], 0.0, ALU.mult, ALU.add).then_inc(
                S["carry_done"], 1)
            v.memset(carry_rows, 0.0).then_inc(S["carry_rows_ready"], 1)
            dve.wait_ge(S["carry_rows_ready"], 1)
            v.tensor_copy(carry_rows[:, :, R_DST:R_DST + 1], last[:, :, R_DST:R_DST + 1]).then_inc(
                S["carry_rows_ready"], 1)
            for k in range(K):
                dve.wait_ge(S["carry_turned"], k + 1)
                v.tensor_copy(carry_rows[:, k, 0:R_DST], ps[k][0:100, 0:R_DST]).then_inc(S["carry_rows_ready"], 1)
            barrier(dve, "carry_over")

            def places(h, q, ahead):
                r = (q + ahead) % 2
                g = h * (2 * NT) + (q + ahead) * NT
                for k in (0, 1):
                    v.tensor_copy(place[r][:, k], place_all[:, k, bass.ds(g, NT)]).then_inc(S["place_ready"], 1)
                v.tensor_copy(node_no[r], node_all[:, bass.ds(g, NT)]).then_inc(S["place_ready"], 1)

            places(0, 0, 0)

            def linker(name, n, h, q, lag):
                links = [0]

                def link(ins):
                    links[0] += 1
                    assert links[0] <= n, (name, links[0])
                    ins.then_inc(S[name], 1)
                    wait(dve, name, done(h, q, lag, n, links[0] - 1))
                return link

            def merge(h, q):
                link = linker("merge_step", MERGE_STEPS, h, q, 0)
                wait(dve, "place_ready", done(h, q, 0, 3, 2))
                wait(dve, f"pieces_loaded_{q}", turn(h, q, 0, PIECES))
                two = pieces[q]
                link(v.tensor_tensor(found, two[:, :, :, R_DST], spread(node_no[q], 1, 2), ALU.is_equal))
                link(v.tensor_scalar(absent, found, BIG, -BIG, ALU.mult, ALU.add))
                link(v.tensor_tensor(piece_max, two[:, :, :, R_MAX:R_MAX + H], spread(absent, 3, H), ALU.add))
                link(v.tensor_tensor(both_max, piece_max[:, 0], piece_max[:, 1], ALU.max))
                v.tensor_tensor(piece_d, piece_max, spread(both_max, 1, 2), ALU.subtract).then_inc(S["merge_in"], 1)
                wait(dve, "merge_exp", done(h, q, 0, 1, 0))
                link(v.tensor_tensor(piece_f, piece_e, spread(found, 3, H), ALU.mult))
                for k, o in enumerate((agg_a, agg_b)):
                    link(v.tensor_tensor(o.rearrange("p t (k h) -> p t k h", h=H),
                                         two[:, k, :, 0:SUMS].rearrange("p t (k h) -> p t k h", h=H),
                                         spread(piece_f[:, k], 2, SUMS // H), ALU.mult))
                link(v.tensor_tensor(agg_a, agg_a, agg_b, ALU.add))
                link(v.tensor_scalar(den, agg_a[:, :, 0:H], 1e-12, None, ALU.add))
                link(v.reciprocal(rden, den))
                wait(dve, "agg_turned", done(h, q, 2, NT, NT - 1))
                v.tensor_tensor(agg[q][:, :, H:SUMS].rearrange("p t (k h) -> p t k h", h=H),
                                agg_a[:, :, H:SUMS].rearrange("p t (k h) -> p t k h", h=H),
                                spread(rden, 2, C // H), ALU.mult).then_inc(S["agg_ready"], 1)

            def add_feed_forward(h, q):
                link = linker("final_step", FINAL_STEPS, h, q, 3)
                r = 1 - q
                y, a = y_sum[r], a0[r]
                wait(dve, f"attrs_loaded_{r}", turn(h, q, 3))
                wait(dve, "y_base_ready", done(h, q, 3, 1, 0))
                for t in range(NT):
                    o = (PW, PO)[((q - 3) * NT + t) % 2][0:P, 0:C]
                    wait(dve, "f2_ready", done(h, q, 3, NT, t))
                    v.scalar_tensor_tensor(y[:, t, 0:C0], o[:, 0:C0], a[:, t:t + 1], y[:, t, 0:C0],
                                           ALU.mult, ALU.add).then_inc(S["x2_ready"], 1)
                    yv = y[:, t, C0:C].rearrange("p (u d) -> p d u", d=3)
                    v.scalar_tensor_tensor(yv, o[:, C0:C].rearrange("p (d u) -> p d u", d=3), a[:, t:t + 1], yv,
                                           ALU.mult, ALU.add).then_inc(S["x2_ready"], 1)
                wait(dve, "x2_ready", done(h, q, 3, 2 * NT, 2 * NT - 1))
                wait(dve, "y_ready", done(h, q, 4, 1, 0))
                link(v.tensor_reduce(x_sum, y, AX.X, ALU.add))
                link(v.tensor_scalar(x_mean, x_sum, 1.0 / C, None, ALU.mult))
                link(v.tensor_tensor(y_cen, y, spread(x_mean, 2, C), ALU.subtract))
                link(v.tensor_tensor(x_sq, y_cen, y_cen, ALU.mult))
                link(v.tensor_reduce(x_ss[:, 0], x_sq, AX.X, ALU.add))
                v.tensor_scalar(y_var, x_ss[:, 0], 1.0 / C, EPS, ALU.mult, ALU.add).then_inc(S["y_var_ready"], 1)

            def last_step(h, q, live):
                if live(-1):
                    places(h, q, 1)
                if live(0):
                    merge(h, q)
                if live(3):
                    add_feed_forward(h, q)
                if live(1):
                    x = x_in[1 - q]
                    wait(dve, f"nodes_loaded_{1 - q}", turn(h, q, 1))
                    wait(dve, "y_base_ready", done(h, q, 2, 1, 0))
                    for t in range(NT):
                        o = (PM, PR)[((q - 1) * NT + t) % 2][0:P, :]
                        wait(dve, "projected", done(h, q, 1, NT, t))
                        v.tensor_tensor(x1[:, t, 0:C0], x[:, t, 0:C0], o[:, 0:C0], ALU.add).then_inc(
                            S["x1_ready"], 1)
                        v.tensor_tensor(x1[:, t, C0:C].rearrange("p (u d) -> p d u", d=3),
                                        x[:, t, C0:C].rearrange("p (u d) -> p d u", d=3),
                                        o[:, C0:C].rearrange("p (d u) -> p d u", d=3), ALU.add).then_inc(
                            S["x1_ready"], 1)
                if live(3):
                    wait(dve, "out_stored", 16 * done(h, q, 4, 1, 0))
                    wait(dve, "y_rstd_ready", done(h, q, 3, 1, 0))
                    v.tensor_tensor(y_out, y_cen, spread(y_rstd, 2, C), ALU.mult).then_inc(S["y_ready"], 1)
                if live(1):
                    wait(dve, "x1_ready", done(h, q, 1, 2 * NT, 2 * NT - 1))
                    wait(dve, "norm_turned", done(h, q, 3, NT, NT - 1))

                    def base():
                        v.tensor_tensor(y_sum[1 - q], x_in[1 - q], x1, ALU.add).then_inc(S["y_base_ready"], 1)

                    if live(3):
                        wait(dve, "y_var_ready", done(h, q, 3, 1, 0))
                    normed(linker("x1_step", NORM_STEPS, h, q, 1), x1, x_norm[1 - q], "x1_var_ready",
                           done(h, q, 1, 1, 0), "x1_rstd_ready",
                           lambda ins: ins.then_inc(S["x1_norm_ready"], 1), base)
                if live(2):
                    for t in range(NT):
                        u = (q * NT + t) % 2
                        wait(dve, "ff_turned", done(h, q, 3, NT, t))
                        wait(dve, "ff_scaled", done(h, q, 2, NT, t))
                        wait(dve, "ff_tanh", done(h, q, 2, NT, t))
                        v.scalar_tensor_tensor(ff_s[:, t], ff_t[:, u, 0:M0], 1.0, ff_g[:, u, 0:M0], ALU.add,
                                               ALU.mult).then_inc(S["ff_ready"], 1)
                        v.scalar_tensor_tensor(ff_v[:, t].rearrange("p (d m) -> p d m", d=3),
                                               spread(ff_t[:, u, M0:192], 1, 3), 1.0,
                                               ff_g[:, u, 192:384].rearrange("p (d m) -> p d m", d=3), ALU.add,
                                               ALU.mult).then_inc(S["ff_ready"], 1)

            last_steps(dve, last_step)


def kernel(**inputs):
    import numpy as _np
    import concourse.bacc as _bacc
    from concourse import mybir as _mybir
    from concourse.bass_utils import run_bass_kernel_spmd as _run

    nc = _bacc.Bacc("TRN2", target_bir_lowering=False, num_devices=1)
    arrays, handles = {}, {}
    for name in inputs:
        a = _np.ascontiguousarray(inputs[name])
        arrays[f"in_{name}"] = a
        handles[name] = nc.dram_tensor(f"in_{name}", a.shape, _mybir.dt.from_np(a.dtype), kind="ExternalInput").ap()
    out = nc.dram_tensor("out", (N, C), F32, kind="ExternalOutput").ap()
    build(nc, handles, out)
    r = _run(nc, [arrays], core_ids=[0])
    return r.results[0]["out"]
```
